# Optimizing a Trainium2 kernel written in Bass

```python
import numpy as np
import jax
import jax.numpy as jnp

def _softmax(x, axis=-1):
    return jax.nn.softmax(x, axis=axis)

def _gelu(x):
    return jax.nn.gelu(x, approximate=True)

def _silu(x):
    return jax.nn.silu(x)

def _sigmoid(x):
    return jax.nn.sigmoid(x)

def _layernorm(x, axis=-1, eps=1e-05):
    m = jnp.mean(x, axis=axis, keepdims=True)
    v = jnp.var(x, axis=axis, keepdims=True)
    return (x - m) / jnp.sqrt(v + eps)

def _scatter_add(tgt, idx, src, axis=0):
    return tgt.at[idx].add(src)

def _segment_sum(src, seg, n):
    return jax.ops.segment_sum(src, seg, n)
kernel_name = 'mk_decoder_preln_d2_seqx_r4_fe0246'

def setup_inputs(seed: int=0):
    np.random.seed(seed)
    _w = jnp.asarray

    def _rec_inputs():
        import jax
        import jax.numpy as jnp
        _rk = jax.random.key(seed)
        x = -0.0002928 + 1 * jax.random.normal(jax.random.fold_in(_rk, 1), (16, 128, 256), jnp.float32)
        _lenS = 128 - jax.random.randint(jax.random.fold_in(_rk, 7), (16,), 0, max(1, 128 // 4) + 1, jnp.int32)
        _lenS2 = 128 - jax.random.randint(jax.random.fold_in(_rk, 8), (16,), 0, max(1, 128 // 4) + 1, jnp.int32)
        _ctx_1024P = jax.random.normal(jax.random.fold_in(_rk, 11), (16, 16, 256), jnp.float32)
        _ctx_1024c = jax.random.dirichlet(jax.random.fold_in(_rk, 511), 0.3 * jnp.ones((16,), jnp.float32), (16, 128))
        _ctx_1024t = jnp.einsum('bsk,bkd->bsd', _ctx_1024c, _ctx_1024P)
        _ctx_1024t = _ctx_1024t * jax.lax.rsqrt(jnp.mean(jnp.square(_ctx_1024t)) + 1e-12) * 0.953939
        ctx_1024 = -1.39393e-06 + 0.999914 * (_ctx_1024t + 0.3 * jax.random.normal(jax.random.fold_in(_rk, 611), (16, 128, 256), jnp.float32))
        return (x, ctx_1024)
    x, ctx_1024 = _rec_inputs()

    def _L0_attn_setup():
        import jax, jax.numpy as jnp
        import numpy as np
        D_MODEL = 256
        D_STATE = 64
        D_CONV = 4
        EXPAND = 2
        N_HEADS = 16
        HEAD_DIM = 64
        ATTN_EVERY = 6
        N_LAYERS = 6
        D_INNER = D_MODEL * EXPAND
        N_SSM = sum((1 for i in range(N_LAYERS) if i % ATTN_EVERY != ATTN_EVERY - 1))
        CHUNK = 128

        def layer_norm(x, g, b, eps=1e-05):
            mu = jnp.mean(x, axis=-1, keepdims=True)
            var = jnp.mean((x - mu) ** 2, axis=-1, keepdims=True)
            return (x - mu) * jax.lax.rsqrt(var + eps) * g + b

        def ssm_layer(x, Wi, cw, cb, Wo, g, b):
            Bsz, T, _ = x.shape
            proj = x @ Wi
            xs = proj[..., :D_INNER]
            Bm = proj[..., D_INNER:D_INNER + D_STATE]
            Cm = proj[..., D_INNER + D_STATE:]
            xc = jax.lax.conv_general_dilated(xs.transpose(0, 2, 1), cw[:, None, :], (1,), [(D_CONV - 1, 0)], feature_group_count=D_INNER, dimension_numbers=('NCH', 'OIH', 'NCH'))
            xc = jax.nn.silu(xc + cb[None, :, None]).transpose(0, 2, 1)
            A = -jnp.exp(jnp.full((D_INNER,), np.float32(np.log(0.5)), x.dtype))
            nC = T // CHUNK
            u = xc.transpose(1, 0, 2).reshape(nC, CHUNK, Bsz, D_INNER)
            bm = Bm.transpose(1, 0, 2).reshape(nC, CHUNK, Bsz, D_STATE)
            cm = Cm.transpose(1, 0, 2).reshape(nC, CHUNK, Bsz, D_STATE)

            def step(h, inp):
                u_t, b_t, c_t = inp
                h = A[None, :, None] * h + u_t[:, :, None] * b_t[:, None, :]
                y = jnp.einsum('bds,bs->bd', h, c_t)
                return (h, y)

            @jax.checkpoint
            def chunk_fn(h, ch):
                return jax.lax.scan(step, h, ch)
            h0 = jnp.zeros((Bsz, D_INNER, D_STATE), x.dtype)
            _, y = jax.lax.scan(chunk_fn, h0, (u, bm, cm))
            y = y.reshape(T, Bsz, D_INNER).transpose(1, 0, 2)
            return layer_norm(y @ Wo + x, g, b)

        def attn_layer(x, wq, wk, wv, wo, g, b):
            Bsz, T, _ = x.shape
            sh = (Bsz, T, N_HEADS, HEAD_DIM)
            q = (x @ wq).reshape(sh)
            k = (x @ wk).reshape(sh)
            v = (x @ wv).reshape(sh)
            scores = jnp.einsum('bqhd,bkhd->bhqk', q, k) * HEAD_DIM ** (-0.5)
            mask = jnp.tril(jnp.ones((T, T), bool))
            scores = jnp.where(mask[None, None], scores, -jnp.inf)
            w = jax.nn.softmax(scores, axis=-1)
            o = jnp.einsum('bhqk,bkhd->bqhd', w, v).reshape(Bsz, T, N_HEADS * HEAD_DIM)
            return layer_norm(o @ wo + x, g, b)
        key = jax.random.key(seed)
        ks = jax.random.split(key, 8)
        s = jnp.float32(0.02)
        d_attn = N_HEADS * HEAD_DIM
        return {'x': jax.random.normal(ks[0], (2, 512, D_MODEL), jnp.float32), 'in_proj_w': jax.random.normal(ks[1], (N_SSM, D_MODEL, D_INNER + 2 * D_STATE), jnp.float32) * s, 'conv_w': jax.random.normal(ks[2], (N_SSM, D_INNER, D_CONV), jnp.float32) * s, 'conv_b': jnp.zeros((N_SSM, D_INNER), jnp.float32), 'out_proj_w': jax.random.normal(ks[3], (N_SSM, D_INNER, D_MODEL), jnp.float32) * s, 'ssm_ln_g': jnp.ones((N_SSM, D_MODEL), jnp.float32), 'ssm_ln_b': jnp.zeros((N_SSM, D_MODEL), jnp.float32), 'wq': jax.random.normal(ks[4], (D_MODEL, d_attn), jnp.float32) * s, 'wk': jax.random.normal(ks[5], (D_MODEL, d_attn), jnp.float32) * s, 'wv': jax.random.normal(ks[6], (D_MODEL, d_attn), jnp.float32) * s, 'wo': jax.random.normal(ks[7], (d_attn, D_MODEL), jnp.float32) * s, 'attn_ln_g': jnp.ones((D_MODEL,), jnp.float32), 'attn_ln_b': jnp.zeros((D_MODEL,), jnp.float32)}
    _L0_attn_all = _L0_attn_setup()
    _L0_attn_in = {k: v for k, v in _L0_attn_all.items() if k in ('in_proj_w', 'conv_w', 'conv_b', 'out_proj_w', 'ssm_ln_g', 'ssm_ln_b', 'wq', 'wk', 'wv', 'wo', 'attn_ln_g', 'attn_ln_b')}
    del _L0_attn_all

    def _L0_xattn_setup():
        import jax, jax.numpy as jnp
        import numpy as np
        D_MODEL = 256
        NUM_HEADS = 16
        D_K = D_MODEL // NUM_HEADS
        key = jax.random.key(seed)
        ks = jax.random.split(key, 12)
        B, S = (1, 1024)
        s = 1.0 / np.sqrt(D_MODEL)
        inp = {'query': jax.random.normal(ks[0], (B, S, D_MODEL), jnp.float32), 'key': jax.random.normal(ks[1], (B, S, D_MODEL), jnp.float32), 'value': jax.random.normal(ks[2], (B, S, D_MODEL), jnp.float32), 'W_q': jax.random.normal(ks[3], (D_MODEL, D_MODEL), jnp.float32) * s, 'b_q': jnp.zeros((D_MODEL,), jnp.float32), 'W_k': jax.random.normal(ks[4], (D_MODEL, D_MODEL), jnp.float32) * s, 'b_k': jnp.zeros((D_MODEL,), jnp.float32), 'W_v': jax.random.normal(ks[5], (D_MODEL, D_MODEL), jnp.float32) * s, 'b_v': jnp.zeros((D_MODEL,), jnp.float32), 'W_o': jax.random.normal(ks[6], (D_MODEL, D_MODEL), jnp.float32) * s, 'b_o': jnp.zeros((D_MODEL,), jnp.float32)}
        return inp
    _L0_xattn_all = _L0_xattn_setup()
    _L0_xattn_in = {k: v for k, v in _L0_xattn_all.items() if k in ('W_q', 'b_q', 'W_k', 'b_k', 'W_v', 'b_v', 'W_o', 'b_o')}
    del _L0_xattn_all

    def _L0_ffn_setup():
        import jax, jax.numpy as jnp
        import numpy as np
        TOP_K = 2
        key = jax.random.key(seed)
        k1, k2, k3, k4, k5 = jax.random.split(key, 5)
        B, S, D, F, E = (2, 256, 256, 512, 8)
        return {'x': jax.random.normal(k1, (B, S, D), dtype=jnp.float32), 'router_kernel_DE': jax.random.normal(k2, (D, E), dtype=jnp.float32) * 0.02, 'kernel_gating_EDF': jax.random.normal(k3, (E, D, F), dtype=jnp.float32) * 0.02, 'kernel_up_EDF': jax.random.normal(k4, (E, D, F), dtype=jnp.float32) * 0.02, 'kernel_down_EFD': jax.random.normal(k5, (E, F, D), dtype=jnp.float32) * 0.02}
    _L0_ffn_all = _L0_ffn_setup()
    _L0_ffn_in = {k: v for k, v in _L0_ffn_all.items() if k in ('router_kernel_DE', 'kernel_gating_EDF', 'kernel_up_EDF', 'kernel_down_EFD')}
    del _L0_ffn_all

    def _L1_attn_setup():
        import jax, jax.numpy as jnp
        import numpy as np
        B, T, D = (4, 512, 256)
        key = jax.random.key(seed)
        kx, kq, kk, kv = jax.random.split(key, 4)
        scale = 1.0 / np.sqrt(D)
        return {'x': jax.random.normal(kx, (B, T, D), dtype=jnp.float32), 'Wq': jax.random.normal(kq, (D, D), dtype=jnp.float32) * scale, 'Wk': jax.random.normal(kk, (D, D), dtype=jnp.float32) * scale, 'Wv': jax.random.normal(kv, (D, D), dtype=jnp.float32) * scale}
    _L1_attn_all = _L1_attn_setup()
    _L1_attn_in = {k: v for k, v in _L1_attn_all.items() if k in ('Wq', 'Wk', 'Wv')}
    del _L1_attn_all

    def _L1_xattn_setup():
        import jax, jax.numpy as jnp
        import numpy as np
        B, S, D = (8, 512, 256)
        EPS = 1e-05

        def _layernorm(x, w, b):
            mu = jnp.mean(x, axis=-1, keepdims=True)
            var = jnp.mean(jnp.square(x - mu), axis=-1, keepdims=True)
            return (x - mu) * jax.lax.rsqrt(var + EPS) * w + b
        key = jax.random.key(seed)
        ks = jax.random.split(key, 4)
        inp = {'query': jax.random.normal(ks[0], (B, S, D), jnp.float32), 'key': jax.random.normal(ks[1], (B, S, D), jnp.float32), 'value': jax.random.normal(ks[2], (B, S, D), jnp.float32), 'inv_scale_factor': jnp.full((1, 1), float(np.sqrt(D)), jnp.float32), 'dropout_p': 0}
        pk = jax.random.split(ks[3], 8)
        for i in range(1, 5):
            inp[f'ln{i}_w'] = 1.0 + 0.02 * jax.random.normal(pk[2 * (i - 1)], (D,), jnp.float32)
            inp[f'ln{i}_b'] = 0.02 * jax.random.normal(pk[2 * (i - 1) + 1], (D,), jnp.float32)
        return inp
    _L1_xattn_all = _L1_xattn_setup()
    _L1_xattn_in = {k: v for k, v in _L1_xattn_all.items() if k in ('inv_scale_factor', 'ln1_w', 'ln1_b', 'ln2_w', 'ln2_b', 'ln3_w', 'ln3_b', 'ln4_w', 'ln4_b')}
    del _L1_xattn_all

    def _L1_ffn_setup():
        import jax, jax.numpy as jnp
        import numpy as np
        INT8_MAX = 127.0

        def _absmax_scale(x, axes):
            amax = jnp.max(jnp.abs(x), axis=axes, keepdims=True)
            return jnp.maximum(amax, 1e-12) / INT8_MAX
        key = jax.random.key(seed)
        k1, k2 = jax.random.split(key)
        lhs = jax.random.normal(k1, (4, 2048, 256), dtype=jnp.float32)
        rhs = jax.random.normal(k2, (256, 256), dtype=jnp.float32)
        return {'lhs': lhs, 'rhs': rhs}
    _L1_ffn_all = _L1_ffn_setup()
    _L1_ffn_in = {k: v for k, v in _L1_ffn_all.items() if k in ('rhs',)}
    del _L1_ffn_all
    return {'x': x, 'ctx_1024': ctx_1024, 'L0_attn_in_proj_w': _L0_attn_in['in_proj_w'], 'L0_attn_conv_w': _L0_attn_in['conv_w'], 'L0_attn_conv_b': _L0_attn_in['conv_b'], 'L0_attn_out_proj_w': _L0_attn_in['out_proj_w'], 'L0_attn_ssm_ln_g': _L0_attn_in['ssm_ln_g'], 'L0_attn_ssm_ln_b': _L0_attn_in['ssm_ln_b'], 'L0_attn_wq': _L0_attn_in['wq'], 'L0_attn_wk': _L0_attn_in['wk'], 'L0_attn_wv': _L0_attn_in['wv'], 'L0_attn_wo': _L0_attn_in['wo'], 'L0_attn_attn_ln_g': _L0_attn_in['attn_ln_g'], 'L0_attn_attn_ln_b': _L0_attn_in['attn_ln_b'], 'L0_xattn_W_q': _L0_xattn_in['W_q'], 'L0_xattn_b_q': _L0_xattn_in['b_q'], 'L0_xattn_W_k': _L0_xattn_in['W_k'], 'L0_xattn_b_k': _L0_xattn_in['b_k'], 'L0_xattn_W_v': _L0_xattn_in['W_v'], 'L0_xattn_b_v': _L0_xattn_in['b_v'], 'L0_xattn_W_o': _L0_xattn_in['W_o'], 'L0_xattn_b_o': _L0_xattn_in['b_o'], 'L0_ffn_router_kernel_DE': _L0_ffn_in['router_kernel_DE'], 'L0_ffn_kernel_gating_EDF': _L0_ffn_in['kernel_gating_EDF'], 'L0_ffn_kernel_up_EDF': _L0_ffn_in['kernel_up_EDF'], 'L0_ffn_kernel_down_EFD': _L0_ffn_in['kernel_down_EFD'], 'L1_attn_Wq': _L1_attn_in['Wq'], 'L1_attn_Wk': _L1_attn_in['Wk'], 'L1_attn_Wv': _L1_attn_in['Wv'], 'L1_xattn_inv_scale_factor': _L1_xattn_in['inv_scale_factor'], 'L1_xattn_ln1_w': _L1_xattn_in['ln1_w'], 'L1_xattn_ln1_b': _L1_xattn_in['ln1_b'], 'L1_xattn_ln2_w': _L1_xattn_in['ln2_w'], 'L1_xattn_ln2_b': _L1_xattn_in['ln2_b'], 'L1_xattn_ln3_w': _L1_xattn_in['ln3_w'], 'L1_xattn_ln3_b': _L1_xattn_in['ln3_b'], 'L1_xattn_ln4_w': _L1_xattn_in['ln4_w'], 'L1_xattn_ln4_b': _L1_xattn_in['ln4_b'], 'L1_ffn_rhs': _L1_ffn_in['rhs']}

def reference(x, ctx_1024, L0_attn_in_proj_w, L0_attn_conv_w, L0_attn_conv_b, L0_attn_out_proj_w, L0_attn_ssm_ln_g, L0_attn_ssm_ln_b, L0_attn_wq, L0_attn_wk, L0_attn_wv, L0_attn_wo, L0_attn_attn_ln_g, L0_attn_attn_ln_b, L0_xattn_W_q, L0_xattn_b_q, L0_xattn_W_k, L0_xattn_b_k, L0_xattn_W_v, L0_xattn_b_v, L0_xattn_W_o, L0_xattn_b_o, L0_ffn_router_kernel_DE, L0_ffn_kernel_gating_EDF, L0_ffn_kernel_up_EDF, L0_ffn_kernel_down_EFD, L1_attn_Wq, L1_attn_Wk, L1_attn_Wv, L1_xattn_inv_scale_factor, L1_xattn_ln1_w, L1_xattn_ln1_b, L1_xattn_ln2_w, L1_xattn_ln2_b, L1_xattn_ln3_w, L1_xattn_ln3_b, L1_xattn_ln4_w, L1_xattn_ln4_b, L1_ffn_rhs):
    import jax
    import jax.numpy as jnp

    def _L0_attn_ref(x, in_proj_w, conv_w, conv_b, out_proj_w, ssm_ln_g, ssm_ln_b, wq, wk, wv, wo, attn_ln_g, attn_ln_b):
        import jax, jax.numpy as jnp
        import numpy as np
        D_MODEL = 256
        D_STATE = 64
        D_CONV = 4
        EXPAND = 2
        N_HEADS = 16
        HEAD_DIM = 64
        ATTN_EVERY = 6
        N_LAYERS = 6
        D_INNER = D_MODEL * EXPAND
        N_SSM = sum((1 for i in range(N_LAYERS) if i % ATTN_EVERY != ATTN_EVERY - 1))
        CHUNK = 128

        def layer_norm(x, g, b, eps=1e-05):
            mu = jnp.mean(x, axis=-1, keepdims=True)
            var = jnp.mean((x - mu) ** 2, axis=-1, keepdims=True)
            return (x - mu) * jax.lax.rsqrt(var + eps) * g + b

        def ssm_layer(x, Wi, cw, cb, Wo, g, b):
            Bsz, T, _ = x.shape
            proj = x @ Wi
            xs = proj[..., :D_INNER]
            Bm = proj[..., D_INNER:D_INNER + D_STATE]
            Cm = proj[..., D_INNER + D_STATE:]
            xc = jax.lax.conv_general_dilated(xs.transpose(0, 2, 1), cw[:, None, :], (1,), [(D_CONV - 1, 0)], feature_group_count=D_INNER, dimension_numbers=('NCH', 'OIH', 'NCH'))
            xc = jax.nn.silu(xc + cb[None, :, None]).transpose(0, 2, 1)
            A = -jnp.exp(jnp.full((D_INNER,), np.float32(np.log(0.5)), x.dtype))
            nC = T // CHUNK
            u = xc.transpose(1, 0, 2).reshape(nC, CHUNK, Bsz, D_INNER)
            bm = Bm.transpose(1, 0, 2).reshape(nC, CHUNK, Bsz, D_STATE)
            cm = Cm.transpose(1, 0, 2).reshape(nC, CHUNK, Bsz, D_STATE)

            def step(h, inp):
                u_t, b_t, c_t = inp
                h = A[None, :, None] * h + u_t[:, :, None] * b_t[:, None, :]
                y = jnp.einsum('bds,bs->bd', h, c_t)
                return (h, y)

            @jax.checkpoint
            def chunk_fn(h, ch):
                return jax.lax.scan(step, h, ch)
            h0 = jnp.zeros((Bsz, D_INNER, D_STATE), x.dtype)
            _, y = jax.lax.scan(chunk_fn, h0, (u, bm, cm))
            y = y.reshape(T, Bsz, D_INNER).transpose(1, 0, 2)
            return layer_norm(y @ Wo + x, g, b)

        def attn_layer(x, wq, wk, wv, wo, g, b):
            Bsz, T, _ = x.shape
            sh = (Bsz, T, N_HEADS, HEAD_DIM)
            q = (x @ wq).reshape(sh)
            k = (x @ wk).reshape(sh)
            v = (x @ wv).reshape(sh)
            scores = jnp.einsum('bqhd,bkhd->bhqk', q, k) * HEAD_DIM ** (-0.5)
            mask = jnp.tril(jnp.ones((T, T), bool))
            scores = jnp.where(mask[None, None], scores, -jnp.inf)
            w = jax.nn.softmax(scores, axis=-1)
            o = jnp.einsum('bhqk,bkhd->bqhd', w, v).reshape(Bsz, T, N_HEADS * HEAD_DIM)
            return layer_norm(o @ wo + x, g, b)
        ssm_idx = 0
        for i in range(N_LAYERS):
            if i % ATTN_EVERY == ATTN_EVERY - 1:
                x = attn_layer(x, wq, wk, wv, wo, attn_ln_g, attn_ln_b)
            else:
                j = ssm_idx
                x = ssm_layer(x, in_proj_w[j], conv_w[j], conv_b[j], out_proj_w[j], ssm_ln_g[j], ssm_ln_b[j])
                ssm_idx += 1
        return x

    def _L0_xattn_ref(query, key, value, W_q, b_q, W_k, b_k, W_v, b_v, W_o, b_o):
        import jax, jax.numpy as jnp
        import numpy as np
        D_MODEL = 256
        NUM_HEADS = 16
        D_K = D_MODEL // NUM_HEADS
        B, S, _ = query.shape
        Q = query @ W_q.T + b_q
        K = key @ W_k.T + b_k
        V = value @ W_v.T + b_v
        Q = Q.reshape(B, S, NUM_HEADS, D_K).transpose(0, 2, 1, 3)
        K = K.reshape(B, S, NUM_HEADS, D_K).transpose(0, 2, 1, 3)
        V = V.reshape(B, S, NUM_HEADS, D_K).transpose(0, 2, 1, 3)
        scale = 1.0 / jnp.sqrt(jnp.asarray(D_K, Q.dtype))
        qk = jnp.einsum('bhqd,bhkd->bhqk', Q, K) * scale
        attn = jax.nn.softmax(qk, axis=-1)
        out = jnp.einsum('bhqk,bhkd->bhqd', attn, V)
        out = out.transpose(0, 2, 1, 3).reshape(B, S, D_MODEL)
        return out @ W_o.T + b_o

    def _L0_ffn_ref(x, router_kernel_DE, kernel_gating_EDF, kernel_up_EDF, kernel_down_EFD):
        import jax, jax.numpy as jnp
        import numpy as np
        TOP_K = 2
        E = router_kernel_DE.shape[-1]
        x = x.astype(jnp.float32)
        logits_BSE = jnp.einsum('BSD,DE->BSE', x, router_kernel_DE)
        probs_BSE = jax.nn.softmax(logits_BSE.astype(jnp.float32), axis=-1)
        weights_BSK, indices_BSK = jax.lax.top_k(probs_BSE, TOP_K)
        norm_weights_BSK = jax.nn.softmax(weights_BSK, axis=-1)
        one_hot_BSKE = jax.nn.one_hot(indices_BSK, num_classes=E, dtype=x.dtype)
        full_weights_BSE = jnp.sum(one_hot_BSKE * norm_weights_BSK[..., None], axis=2)
        gating_BSEF = jnp.einsum('BSD,EDF->BSEF', x, kernel_gating_EDF)
        act_BSEF = jax.nn.silu(gating_BSEF)
        up_BSEF = jnp.einsum('BSD,EDF->BSEF', x, kernel_up_EDF)
        fuse_BSEF = act_BSEF * up_BSEF
        down_BSED = jnp.einsum('BSEF,EFD->BSED', fuse_BSEF, kernel_down_EFD)
        out_BSD = jnp.einsum('BSED,BSE->BSD', down_BSED, full_weights_BSE)
        return out_BSD.astype(jnp.float32)

    def _L1_attn_ref(x, Wq, Wk, Wv):
        import jax, jax.numpy as jnp
        import numpy as np
        B, T, D = (4, 512, 256)
        q = jnp.einsum('btd,od->bto', x, Wq)
        k = jnp.einsum('btd,od->bto', x, Wk)
        v = jnp.einsum('btd,od->bto', x, Wv)
        scores = jnp.einsum('bqd,bkd->bqk', q, k)
        inv_sqrt_d = 1.0 / np.sqrt(k.shape[-1]).astype(np.float32)
        weights = jax.nn.softmax(scores * inv_sqrt_d, axis=-1)
        return jnp.einsum('bqk,bkd->bqd', weights, v)

    def _L1_xattn_ref(query, key, value, inv_scale_factor, ln1_w, ln1_b, ln2_w, ln2_b, ln3_w, ln3_b, ln4_w, ln4_b, dropout_p):
        import jax, jax.numpy as jnp
        import numpy as np
        B, S, D = (8, 512, 256)
        EPS = 1e-05

        def _layernorm(x, w, b):
            mu = jnp.mean(x, axis=-1, keepdims=True)
            var = jnp.mean(jnp.square(x - mu), axis=-1, keepdims=True)
            return (x - mu) * jax.lax.rsqrt(var + EPS) * w + b
        q = _layernorm(query, ln1_w, ln1_b)
        k = _layernorm(key, ln2_w, ln2_b)
        v = _layernorm(value, ln3_w, ln3_b)
        qk = jnp.einsum('bqd,bkd->bqk', q, k)
        scaled = qk / inv_scale_factor
        probs = jax.nn.softmax(scaled, axis=2)
        out = jnp.einsum('bqk,bkd->bqd', probs, v)
        return _layernorm(out, ln4_w, ln4_b)

    def _L1_ffn_ref(lhs, rhs):
        import jax, jax.numpy as jnp
        import numpy as np
        INT8_MAX = 127.0

        def _absmax_scale(x, axes):
            amax = jnp.max(jnp.abs(x), axis=axes, keepdims=True)
            return jnp.maximum(amax, 1e-12) / INT8_MAX
        lhs_scale = _absmax_scale(lhs, (2,))
        rhs_scale = _absmax_scale(rhs, (0,))
        q_lhs = jnp.clip(jnp.round(lhs / lhs_scale), -INT8_MAX, INT8_MAX).astype(jnp.int8)
        q_rhs = jnp.clip(jnp.round(rhs / rhs_scale), -INT8_MAX, INT8_MAX).astype(jnp.int8)
        acc = jax.lax.dot_general(q_lhs, q_rhs, (((2,), (0,)), ((), ())), preferred_element_type=jnp.int32)
        return acc.astype(jnp.float32) * lhs_scale * rhs_scale
    x = x + _L0_attn_ref(_layernorm(x, axis=-1), L0_attn_in_proj_w, L0_attn_conv_w, L0_attn_conv_b, L0_attn_out_proj_w, L0_attn_ssm_ln_g, L0_attn_ssm_ln_b, L0_attn_wq, L0_attn_wk, L0_attn_wv, L0_attn_wo, L0_attn_attn_ln_g, L0_attn_attn_ln_b)
    x = x + _L0_xattn_ref(_layernorm(x, axis=-1), ctx_1024, ctx_1024, L0_xattn_W_q, L0_xattn_b_q, L0_xattn_W_k, L0_xattn_b_k, L0_xattn_W_v, L0_xattn_b_v, L0_xattn_W_o, L0_xattn_b_o)
    x = x + _L0_ffn_ref(_layernorm(x, axis=-1), L0_ffn_router_kernel_DE, L0_ffn_kernel_gating_EDF, L0_ffn_kernel_up_EDF, L0_ffn_kernel_down_EFD)
    x = x + _L1_attn_ref(_layernorm(x, axis=-1), L1_attn_Wq, L1_attn_Wk, L1_attn_Wv)
    x = x + _L1_xattn_ref(_layernorm(x, axis=-1), ctx_1024, ctx_1024, L1_xattn_inv_scale_factor, L1_xattn_ln1_w, L1_xattn_ln1_b, L1_xattn_ln2_w, L1_xattn_ln2_b, L1_xattn_ln3_w, L1_xattn_ln3_b, L1_xattn_ln4_w, L1_xattn_ln4_b, 0)
    x = x + _L1_ffn_ref(_layernorm(x, axis=-1), L1_ffn_rhs)
    return x

_drawn_inputs = setup_inputs


def setup_inputs(seed=0):
    import zlib

    import numpy as np

    out = dict(_drawn_inputs(seed))
    spreads = {'L0_attn_conv_b': (0.0, 0.308),
     'L0_attn_ssm_ln_g': (1.0, 0.2),
     'L0_attn_ssm_ln_b': (0.0, 0.1),
     'L0_attn_attn_ln_g': (1.0, 0.2),
     'L0_attn_attn_ln_b': (0.0, 0.1),
     'L0_xattn_b_q': (0.0, 0.496),
     'L0_xattn_b_k': (0.0, 0.8),
     'L0_xattn_b_v': (0.0, 0.1),
     'L0_xattn_b_o': (0.0, 0.1)}
    factors = {'L0_attn_conv_w': 8.0,
     'L0_attn_wq': 8.0,
     'L0_attn_wk': 8.0,
     'L0_ffn_router_kernel_DE': 5.617,
     'L0_ffn_kernel_gating_EDF': 5.138,
     'L0_ffn_kernel_up_EDF': 5.108,
     'L0_ffn_kernel_down_EFD': 5.098,
     'L1_xattn_ln1_w': 8.0,
     'L1_xattn_ln1_b': 8.0,
     'L1_xattn_ln2_w': 8.0,
     'L1_xattn_ln2_b': 8.0,
     'L1_xattn_ln3_w': 5.051,
     'L1_xattn_ln3_b': 3.181,
     'L1_xattn_ln4_w': 5.048,
     'L1_xattn_ln4_b': 4.754}
    for name, (base, spread) in spreads.items():
        noise = np.random.default_rng([zlib.crc32(name.encode()), seed]).standard_normal(out[name].shape)
        drawn = base * np.exp(spread * noise) if base else spread * noise
        out[name] = jnp.asarray(drawn.astype(out[name].dtype))
    for name, factor in factors.items():
        out[name] = (out[name] * factor).astype(out[name].dtype)
    return out
```

```python
from contextlib import ExitStack

import concourse.bass as bass
from concourse import mybir

F32 = mybir.dt.float32
F32R = mybir.dt.float32r
BF16 = mybir.dt.bfloat16
I32 = mybir.dt.int32
ALU = mybir.AluOpType
ACT = mybir.ActivationFunctionType
AX = mybir.AxisListType

P = 128
SEQS = 16
D = 256
KD = D // P
GS = 4
GROUPS = SEQS // GS
GT = GS * P
INNER = 512
KI = INNER // P
STATE = 64
PROJ = INNER + 2 * STATE
TAPS = 4
SSM_LAYERS = 5
EPS = 1e-5
BANK = 512
HI, LO = 0, 1


def stage_load_and_norm(nc, ctx, io, mem):
    X, ACTV, ACT_T, ident, neghalf = mem["x"], mem["act"], mem["act_t"], mem["ident"], mem["neghalf"]
    sem = lambda name: mem["sems"](name)
    x_loaded = [sem(f"n0_x_loaded{g}") for g in range(GROUPS)]
    const_step = sem("n0_const_step")
    consts_ready = sem("n0_consts_ready")
    stats_ready = sem("n0_stats_ready")
    aggr_ready = sem("n0_aggr_ready")
    var_ready = sem("n0_var_ready")
    rstd_ready = sem("n0_rstd_ready")
    normed = sem("n0_normed")
    tr_ready = sem("n0_tr_ready")
    tr_copied = sem("n0_tr_copied")
    psum, stats, mv, ve = mem["psum"], mem["stats"], mem["mv"], mem["ve"]

    with nc.Block() as block:
        @block.sync
        def _(sp):
            for g in range(GROUPS):
                sp.dma_start(X[:, GS * g:GS * g + GS, :],
                             io["x"][GS * g:GS * g + GS].rearrange("b t d -> t b d")).then_inc(x_loaded[g], 16)
            mem["prefetch_ssm"](sp)

        @block.gpsimd
        def _(pool):
            pool.memset(ident[:, :], 0.0).then_inc(const_step, 1)
            pool.memset(mem["ident_bf"][:, :], 0.0).then_inc(const_step, 1)
            pool.memset(mem["causal"][:, :], 0.0).then_inc(const_step, 1)
            pool.memset(neghalf[:, :], -0.5).then_inc(consts_ready, 1)
            pool.wait_ge(const_step, 3)
            for t in (ident, mem["ident_bf"]):
                pool.affine_select(out=t[:, :], in_=t[:, :], compare_op=ALU.not_equal, fill=1.0, base=0,
                                   pattern=[[-1, P]], channel_multiplier=1).then_inc(consts_ready, 1)
            pool.affine_select(out=mem["causal"][:, :], in_=mem["causal"][:, :], compare_op=ALU.is_ge,
                               fill=-1e30, base=0, pattern=[[-1, P]], channel_multiplier=1).then_inc(consts_ready, 1)
            pool.wait_ge(consts_ready, 4)
            for g in range(GROUPS):
                pool.wait_ge(var_ready, g + 1)
                pool.tensor_tensor(ve[:, GS * g:GS * g + GS], ve[:, GS * g:GS * g + GS],
                                   neghalf[:, 0:GS], ALU.pow).then_inc(rstd_ready, 1)

        @block.vector
        def _(dve):
            for g in range(GROUPS):
                dve.wait_ge(x_loaded[g], 16)
                for b in range(GS * g, GS * g + GS):
                    dve.bn_stats(stats[:, b, :], X[:, b, :]).then_inc(stats_ready, 1)
                dve.wait_ge(stats_ready, GS * (g + 1))
                for b in range(GS * g, GS * g + GS):
                    dve.bn_aggr(mv[:, b, :], stats[:, b, :]).then_inc(aggr_ready, 1)
                dve.wait_ge(aggr_ready, GS * (g + 1))
                dve.tensor_scalar(ve[:, GS * g:GS * g + GS], mv[:, GS * g:GS * g + GS, 1], EPS, None,
                                  ALU.add).then_inc(var_ready, 1)
            for g in range(GROUPS):
                dve.wait_ge(rstd_ready, g + 1)
                for b in range(GS * g, GS * g + GS):
                    dve.tensor_scalar(ACTV[:, b, :], X[:, b, :], mv[:, b, 0:1], ve[:, b:b + 1],
                                      ALU.subtract, ALU.mult).then_inc(normed, 1)

        @block.tensor
        def _(pe):
            pe.wait_ge(consts_ready, 4)
            for h in range(SEQS // 2):
                pe.wait_ge(normed, 2 * h + 2)
                if h >= 2:
                    pe.wait_ge(tr_copied, h - 1)
                for s in range(2):
                    for k in range(KD):
                        col = k * D + s * P
                        tr = pe.transpose(psum[6 + h % 2][:, col:col + P],
                                          ACTV[:, 2 * h + s, k * P:(k + 1) * P], ident[:, :])
                tr.then_inc(tr_ready, 1)

        @block.scalar
        def _(act):
            for h in range(SEQS // 2):
                act.wait_ge(tr_ready, h + 1)
                nc.scalar.activation(ACT_T[:, :, 2 * h * P:(2 * h + 2) * P],
                                     psum[6 + h % 2][:, :].rearrange("p (k t) -> p k t", k=KD),
                                     ACT.Copy).then_inc(tr_copied, 1)


def stage_ssm(nc, ctx, io, mem):
    ACTV, ACT_T, ident, neghalf, psum = mem["act"], mem["act_t"], mem["ident"], mem["neghalf"], mem["psum"]
    names = mem["ssm_sems"]
    w_in, w_out, conv_w, conv_b, ln_g, ln_b, decay = (mem[k] for k in (
        "w_in", "w_out", "conv_w", "conv_b", "ln_g", "ln_b", "decay"))
    sb = lambda name, shape: ctx.enter_context(nc.sbuf_tensor(name, shape, F32))
    sem = lambda name: mem["sems"]("s_" + name)
    conv = sb("ssm_conv", [P, KI, GT])
    u = sb("ssm_u", [P, 2, KI, GT])
    b_t = sb("ssm_b_t", [STATE, 2, GT])
    c_t = sb("ssm_c_t", [STATE, 2, GT])
    mix = sb("ssm_mix", [P, GS, P])
    uw = sb("ssm_uw", [P, 2, 2 * D])
    res = sb("ssm_res", [P, 2, 2 * D])
    z = sb("ssm_z", [P, 2, 2, D])
    zg = sb("ssm_zg", [P, 2, 2, D])
    stats, mv, ve = mem["stats"], mem["mv"], mem["ve"]

    bc_ready = sem("bc_ready")
    xs_ready = sem("xs_ready")
    bt_copied = sem("bt_copied")
    ct_copied = sem("ct_copied")
    tap_last = sem("tap_last")
    tap_step = sem("tap_step")
    conv_done = sem("conv_done")
    u_ready = sem("u_ready")
    g_ready = sem("g_ready")
    mix_ready = sem("mix_ready")
    uw_ready = sem("uw_ready")
    uw_copied = sem("uw_copied")
    y_ready = sem("y_ready")
    res_ready = sem("res_ready")
    stats_ready = sem("stats_ready")
    stats_seen = sem("stats_seen")
    aggr_ready = sem("aggr_ready")
    var_ready = sem("var_ready")
    rstd_ready = sem("rstd_ready")
    z_ready = sem("z_ready")
    zg_ready = sem("zg_ready")
    act_ready = sem("act_ready")
    tr_ready = sem("tr_ready")
    tr_copied = sem("tr_copied")
    attn_hi_ready = sem("attn_hi_ready")

    XS = lambda c: psum[c]
    BC, UWY, TR = psum[4], (psum[5], psum[6]), psum[7]
    LAST = SSM_LAYERS - 1

    def layers(eng, body):
        body(0)
        with eng.Fori(1, LAST) as layer:
            body(layer)
        body(LAST)

    with nc.Block() as block:
        @block.sync
        def _(sp):
            def reload(layer):
                done = layer * GROUPS * 1 + 0
                sp.wait_ge(xs_ready, layer * (GROUPS * KI) + GROUPS * KI)
                mem["load_w_in"](sp, layer + 1)
                sp.wait_ge(tap_last, layer * (GROUPS * KI) + GROUPS * KI)
                sp.wait_ge(conv_done, layer * (GROUPS * KI) + GROUPS * KI)
                mem["load_conv"](sp, layer + 1)
                sp.wait_ge(uw_ready, layer * (2 * GROUPS) + 2 * GROUPS)
                mem["load_w_out"](sp, layer + 1)
                sp.wait_ge(mem["attn_w_split"], layer * GROUPS + GROUPS)
                sp.wait_ge(act_ready, layer * (2 * GROUPS) + 2 * GROUPS)
                mem["load_ln"](sp, layer + 1)
            with sp.Fori(0, LAST) as layer:
                sp.dma_start(mem["attn_raw"][:, :], io["attn_w_laid"][bass.ds(layer, 1)].rearrange(
                    "a p n -> p (a n)")).then_inc(mem["attn_w_loaded"], 16)
                reload(layer)
            for tile, name in ((mem["attn_g"], "L0_attn_attn_ln_g"), (mem["attn_b"], "L0_attn_attn_ln_b")):
                sp.dma_start(tile[:, :], io[name].unsqueeze(0).broadcast_to([P, D])).then_inc(mem["attn_ln_loaded"], 16)

        @block.tensor
        def _(pe):
            def project(layer, g, first=False):
                n = layer * GROUPS + g
                pe.wait_ge(names["w_in_loaded"], layer * 16 + 16)
                if not first:
                    pe.wait_ge(tr_copied, n * 2 - 2 * GROUPS + 2)
                tokens = slice(g * GT, (g + 1) * GT)
                if g >= 2 or not first:
                    pe.wait_ge(mix_ready, n - 1)
                elif g == 1:
                    pe.wait_ge(bt_copied, 1)
                    pe.wait_ge(ct_copied, 1)
                for k in range(KD):
                    mm = pe.matmul(BC[:, :], w_in[:, k, INNER:PROJ], ACT_T[:, k, tokens],
                                   start=(k == 0), stop=(k == KD - 1))
                mm.then_inc(bc_ready, 1)
                for c in range(KI):
                    if g >= 1 or not first:
                        pe.wait_ge(tap_last, n * KI - KI + c + 1)
                        pe.wait_ge(conv_done, n * KI - KI + c + 1)
                    for k in range(KD):
                        mm = pe.matmul(XS(c)[:, :], w_in[:, k, c * P:(c + 1) * P], ACT_T[:, k, tokens],
                                       start=(k == 0), stop=(k == KD - 1))
                    mm.then_inc(xs_ready, 1)

            def turn(layer, g):
                n = layer * GROUPS + g
                for h in range(2):
                    pe.wait_ge(act_ready, n * 2 + h + 1)
                    if not (layer_is(layer, 0) and g == 0 and h == 0):
                        pe.wait_ge(tr_copied, n * 2 + h)
                    for s in range(2):
                        for k in range(KD):
                            tr = pe.transpose(TR[:, k * D + s * P:k * D + (s + 1) * P],
                                              ACTV[:, g * GS + 2 * h + s, k * P:(k + 1) * P], ident[:, :])
                    tr.then_inc(tr_ready, 1)

            def mix_tokens(layer, g, first=False, last=False):
                n = layer * GROUPS + g
                ahead = 1 if last else 2
                pe.wait_ge(bt_copied, n + ahead)
                pe.wait_ge(ct_copied, n + ahead)
                for s in range(GS):
                    mm = pe.matmul(BC[:, s * P:(s + 1) * P], b_t[:, g % 2, s * P:(s + 1) * P],
                                   c_t[:, g % 2, s * P:(s + 1) * P], start=True, stop=True)
                mm.then_inc(g_ready, 1)
                pe.wait_ge(u_ready, n * KI + KI)
                if g == 0:
                    pe.wait_ge(names["w_out_loaded"], layer * 16 + 16)
                for h in range(2):
                    if not (first and g == 0):
                        pe.wait_ge(res_ready, n * 2 - 1 + h)
                    for s in range(2):
                        t = (2 * h + s) * P
                        for c in range(KI):
                            mm = pe.matmul(UWY[h][:, s * D:(s + 1) * D], u[:, g % 2, c, t:t + P],
                                           w_out[:, c, :], start=(c == 0), stop=(c == KI - 1))
                    mm.then_inc(uw_ready, 1)
                pe.wait_ge(mix_ready, n + 1)
                for h in range(2):
                    pe.wait_ge(uw_copied, n * 2 + h + 1)
                    for s in range(2):
                        mm = pe.matmul(UWY[h][:, s * D:(s + 1) * D], mix[:, 2 * h + s, :],
                                       uw[:, h, s * D:(s + 1) * D], start=True, stop=True)
                    mm.then_inc(y_ready, 1)

            project(0, 0, first=True)

            def layer_steps(layer):
                first, last = layer_is(layer, 0), layer_is(layer, LAST)
                for g in range(GROUPS):
                    if g < GROUPS - 1:
                        project(layer, g + 1, first)
                    elif not last:
                        project(layer + 1, 0)
                    if g > 0:
                        turn(layer, g - 1)
                    elif not first:
                        turn(layer - 1, GROUPS - 1)
                    mix_tokens(layer, g, first, last and g == GROUPS - 1)
            layers(pe, layer_steps)
            turn(LAST, GROUPS - 1)

        @block.scalar
        def _(act):
            def front(layer, g, first=False):
                n = layer * GROUPS + g
                act.wait_ge(bc_ready, n + 1)
                if not (first and g < 2):
                    act.wait_ge(g_ready, n - 1)
                nc.scalar.activation(b_t[:, g % 2, :], BC[0:STATE, :], ACT.Copy).then_inc(bt_copied, 1)
                if g == 0:
                    act.wait_ge(names["conv_loaded"], layer * 32 + 32)
                for c in range(KI):
                    act.wait_ge(xs_ready, n * KI + c + 1)
                    if not (first and g == 0):
                        act.wait_ge(u_ready, n * KI - KI + c + 1)
                    nc.scalar.activation(conv[:, c, :], XS(c)[:, :], ACT.Identity, bias=conv_b[:, c:c + 1],
                                         scale=conv_w[:, c, TAPS - 1:TAPS]).then_inc(tap_last, 1)

            def silu(layer, g, chunks, first=False):
                n = layer * GROUPS + g
                for c in chunks:
                    act.wait_ge(conv_done, n * KI + c + 1)
                    if not (first and g < 2):
                        act.wait_ge(uw_ready, n * 2 - 2)
                    nc.scalar.activation(u[:, g % 2, c, :], conv[:, c, :], ACT.Silu).then_inc(u_ready, 1)

            def copy_uw(layer, g, h):
                n = layer * GROUPS + g
                act.wait_ge(uw_ready, n * 2 + h + 1)
                nc.scalar.activation(uw[:, h, :], UWY[h][:, :], ACT.Copy).then_inc(uw_copied, 1)

            def copy_turned(layer, g):
                n = layer * GROUPS + g
                for h in range(2):
                    act.wait_ge(tr_ready, n * 2 + h + 1)
                    t = g * GT + 2 * h * P
                    nc.scalar.activation(ACT_T[:, :, t:t + 2 * P],
                                         TR[:, :].rearrange("p (k t) -> p k t", k=KD),
                                         ACT.Copy).then_inc(tr_copied, 1)

            front(0, 0, first=True)
            silu(0, 0, range(KI), first=True)

            def layer_steps(layer):
                first, last = layer_is(layer, 0), layer_is(layer, LAST)
                for g in range(GROUPS):
                    ahead = (layer, g + 1, first) if g < GROUPS - 1 else None if last else (layer + 1, 0)
                    if ahead:
                        front(*ahead)
                    if g > 0:
                        copy_turned(layer, g - 1)
                    elif not first:
                        copy_turned(layer - 1, GROUPS - 1)
                    if ahead:
                        silu(*ahead[:2], range(0, 2), *ahead[2:])
                    copy_uw(layer, g, 0)
                    copy_uw(layer, g, 1)
                    if ahead:
                        silu(*ahead[:2], range(2, KI), *ahead[2:])
            layers(act, layer_steps)
            copy_turned(LAST, GROUPS - 1)

        @block.vector
        def _(dve):
            def copy_c(layer, g, first=False):
                n = layer * GROUPS + g
                dve.wait_ge(bc_ready, n + 1)
                if not (first and g < 2):
                    dve.wait_ge(g_ready, n - 1)
                dve.tensor_copy(c_t[:, g % 2, :], BC[STATE:P, :]).then_inc(ct_copied, 1)

            def convolve(layer, g, pair):
                n = layer * GROUPS + g
                for back in range(1, TAPS):
                    for c in (2 * pair, 2 * pair + 1):
                        acc = conv[:, c, :].rearrange("p (s t) -> p s t", s=GS)[:, :, back:]
                        xs = XS(c)[:, :].rearrange("p (s t) -> p s t", s=GS)[:, :, 0:P - back]
                        if back == 1:
                            dve.wait_ge(tap_last, n * KI + c + 1)
                        else:
                            dve.wait_ge(tap_step, (n * 2 + pair) * 4 + (back - 2) * 2 + (c - 2 * pair) + 1)
                        op = dve.scalar_tensor_tensor(out=acc, in0=xs, scalar=conv_w[:, c, TAPS - 1 - back:TAPS - back],
                                                      in1=acc, op0=ALU.mult, op1=ALU.add)
                        op.then_inc(conv_done if back == TAPS - 1 else tap_step, 1)

            def decayed(layer, g):
                n = layer * GROUPS + g
                dve.wait_ge(g_ready, n + 1)
                if g == 0 and layer_is(layer, 0):
                    dve.wait_ge(names["decay_loaded"], 16)
                dve.tensor_tensor(mix[:, :, :], BC[:, :].rearrange("p (s t) -> p s t", s=GS),
                                  decay[:, :].unsqueeze(1).broadcast_to([P, GS, P]), ALU.mult).then_inc(mix_ready, 1)

            def norm(layer, g):
                n = layer * GROUPS + g
                for h in range(2):
                    b = g * GS + 2 * h
                    dve.wait_ge(y_ready, n * 2 + h + 1)
                    dve.tensor_tensor(res[:, h, :].rearrange("p (s d) -> p s d", s=2),
                                      UWY[h][:, :].rearrange("p (s d) -> p s d", s=2),
                                      ACTV[:, b:b + 2, :], ALU.add).then_inc(res_ready, 1)
                    dve.wait_ge(res_ready, n * 2 + h + 1)
                    for s in range(2):
                        dve.bn_stats(stats[:, 2 * h + s, :], res[:, h, s * D:(s + 1) * D]).then_inc(stats_ready, 1)
                    dve.wait_ge(stats_ready, n * 4 + 2 * h + 2)
                    dve.sem_inc(stats_seen, 1)
                    for s in range(2):
                        dve.bn_aggr(mv[:, 2 * h + s, :], stats[:, 2 * h + s, :]).then_inc(aggr_ready, 1)
                    dve.wait_ge(aggr_ready, n * 4 + 2 * h + 2)
                    dve.tensor_scalar(ve[:, 2 * h:2 * h + 2], mv[:, 2 * h:2 * h + 2, 1], EPS, None,
                                      ALU.add).then_inc(var_ready, 1)
                for h in range(2):
                    dve.wait_ge(rstd_ready, n * 2 + h + 1)
                    for s in range(2):
                        i = 2 * h + s
                        dve.tensor_scalar(z[:, h, s, :], res[:, h, s * D:(s + 1) * D], mv[:, i, 0:1],
                                          ve[:, i:i + 1], ALU.subtract, ALU.mult).then_inc(z_ready, 1)

            copy_c(0, 0, True)
            convolve(0, 0, 0)
            convolve(0, 0, 1)

            def layer_steps(layer):
                first, last = layer_is(layer, 0), layer_is(layer, LAST)
                for g in range(GROUPS):
                    ahead = (layer, g + 1) if g < GROUPS - 1 else None if last else (layer + 1, 0)
                    if ahead:
                        copy_c(*ahead, first and g < GROUPS - 1)
                        convolve(*ahead, 0)
                    decayed(layer, g)
                    if ahead:
                        convolve(*ahead, 1)
                    norm(layer, g)
            layers(dve, layer_steps)

        @block.gpsimd
        def _(pool):
            def finish(layer, g):
                n = layer * GROUPS + g
                for h in range(2):
                    pool.wait_ge(var_ready, n * 2 + h + 1)
                    pool.tensor_tensor(ve[:, 2 * h:2 * h + 2], ve[:, 2 * h:2 * h + 2], neghalf[:, 0:2],
                                       ALU.pow).then_inc(rstd_ready, 1)
                if g == 0:
                    pool.wait_ge(names["ln_loaded"], layer * 32 + 32)
                for h in range(2):
                    b = g * GS + 2 * h
                    pool.wait_ge(z_ready, n * 4 + 2 * h + 2)
                    pool.tensor_tensor(zg[:, h, :, :], z[:, h, :, :],
                                       ln_g[:, :].unsqueeze(1).broadcast_to([P, 2, D]), ALU.mult).then_inc(zg_ready, 1)
                    pool.wait_ge(zg_ready, n * 2 + h + 1)
                    pool.tensor_tensor(ACTV[:, b:b + 2, :], zg[:, h, :, :],
                                       ln_b[:, :].unsqueeze(1).broadcast_to([P, 2, D]), ALU.add).then_inc(act_ready, 1)

            def split_attention_weight(layer, g):
                n = layer * GROUPS + g
                cols = slice(g * 2 * KI * P // 2, (g + 1) * 2 * KI * P // 2)
                w = mem["attn_w"]
                if g == 0:
                    pool.wait_ge(mem["attn_w_loaded"], layer * 16 + 16)
                part = lambda x: x[:, bass.ds(layer, 1), cols].rearrange("p a n -> p (a n)")
                pool.tensor_copy(part(w[HI]), mem["attn_raw"][:, cols]).then_inc(attn_hi_ready, 1)
                pool.wait_ge(attn_hi_ready, n + 1)
                pool.tensor_tensor(part(w[LO]), mem["attn_raw"][:, cols], part(w[HI]).bitcast(F32),
                                   ALU.subtract).then_inc(mem["attn_w_split"], 1)

            with pool.Fori(0, LAST) as layer:
                for g in range(GROUPS):
                    finish(layer, g)
                    split_attention_weight(layer, g)
            for g in range(GROUPS):
                finish(LAST, g)


def layer_is(layer, value):
    return isinstance(layer, int) and layer == value


def product(pe, out, lhs, rhs, start, stop):
    pe.matmul(out, lhs[HI], rhs[HI], start=start, stop=False)
    pe.matmul(out, lhs[HI], rhs[LO], start=False, stop=False)
    return pe.matmul(out, lhs[LO], rhs[HI], start=False, stop=stop)


def chunks_of(pair, i, chunks):
    return [x[:, i, :].rearrange("p (k n) -> p k n", k=chunks) for x in pair]


HEADS = 16
HEAD = 64
WIDE = HEADS * HEAD
KW = WIDE // P
OCTETS = SEQS * 2
GU = GS * 2


def stage_self_attention(nc, ctx, io, mem):
    X, ACTV, ACT_T, ident, neghalf, psum = mem["x"], mem["act"], mem["act_t"], mem["ident"], mem["neghalf"], mem["psum"]
    sb = lambda name, shape, dt=F32: ctx.enter_context(nc.sbuf_tensor("a_" + name, shape, dt))
    sem = lambda name: mem["sems"]("a_" + name)
    pair = lambda name, shape: (sb(name + "_hi", shape, F32R), sb(name + "_lo", shape, F32R))
    w = mem["attn_w"]
    wq, wk, wv = (chunks_of(w, i, KD) for i in range(3))
    wo = chunks_of(w, 3, KW)
    ln_g, ln_b = mem["attn_g"], mem["attn_b"]
    xg = pair("xg", [P, KD, GT])
    q_t = sb("q_t", [P, KW, GT])
    k_t = sb("k_t", [P, KW, GT])
    v = sb("v", [P, GS, WIDE])
    prob = sb("prob", [P, 2, 8, P])
    prob_t = sb("prob_t", [P, 2, 8, P])
    o = sb("o", [P, 8, HEAD])
    o_t = pair("o_t", [P, KW, P])
    neg_max = sb("neg_max", [P, 2, 8])
    total = sb("total", [P, 2, 8])
    inv = sb("inv", [P, 2, 8])
    res = sb("res", [P, D])
    z = sb("z", [P, 2, D])
    zg = sb("zg", [P, D])
    zb = sb("zb", [P, D])
    stats, mv, ve = mem["stats"], mem["mv"], mem["ve"]

    xh_ready, xl_ready = sem("xh_ready"), sem("xl_ready")
    proj_ready = sem("proj_ready")
    proj_act, proj_dve = sem("proj_act"), sem("proj_dve")
    s_ready = sem("s_ready")
    max_ready = sem("max_ready")
    exp_ready = sem("exp_ready")
    pt_ready = sem("pt_ready")
    pt_act, pt_dve = sem("pt_act"), sem("pt_dve")
    o_ready = sem("o_ready")
    inv_ready = sem("inv_ready")
    o_scaled = sem("o_scaled")
    ot_ready = sem("ot_ready")
    ot_hi, ot_lo = sem("ot_hi"), sem("ot_lo")
    y_ready = sem("y_ready")
    res_ready = sem("res_ready")
    stats_ready = sem("stats_ready")
    stats_seen = sem("stats_seen")
    aggr_ready = sem("aggr_ready")
    var_ready = sem("var_ready")
    rstd_ready = sem("rstd_ready")
    z_ready = sem("z_ready")
    zg_ready = sem("zg_ready")
    zb_ready = sem("zb_ready")
    x_ready = sem("x_ready")

    RING = 4
    PROJS = 2 * KW + 2 * GS
    S = lambda u, par: psum[2 * (u % 2) + par]
    PT = (psum[4], psum[5])
    O, OTY = psum[6], psum[7]

    with nc.Block() as block:
        @block.tensor
        def _(pe):
            pe.wait_ge(mem["attn_w_split"], 16)

            def projections(G):
                pe.wait_ge(xh_ready, G + 1)
                pe.wait_ge(xl_ready, G + 1)
                for r in range(PROJS):
                    if r < RING:
                        pass
                    elif r % 2 == 0:
                        pe.wait_ge(proj_act, G * (PROJS // 2) + (r - RING) // 2 + 1)
                    else:
                        pe.wait_ge(proj_dve, G * (PROJS // 2) + (r - RING) // 2 + 1)
                    bank = psum[r % RING]
                    if r < 2 * KW:
                        weights, c = (wq, wk)[r % 2], r // 2
                        for k in range(KD):
                            mm = product(pe, bank[:, :], [x[:, k, c * P:(c + 1) * P] for x in weights], [x[:, k, :] for x in xg],
                                         k == 0, k == KD - 1)
                    else:
                        s, half = (r - 2 * KW) // 2, r % 2
                        for k in range(KD):
                            mm = product(pe, bank[:, :], [x[:, k, s * P:(s + 1) * P] for x in xg],
                                         [x[:, k, half * BANK:(half + 1) * BANK] for x in wv], k == 0, k == KD - 1)
                    mm.then_inc(proj_ready, 1)

            def scores(G, u):
                U = G * GU + u
                s, octet = u // 2, u % 2
                if u < 2:
                    pe.wait_ge(proj_act, G * (PROJS // 2) + PROJS // 2)
                    pe.wait_ge(proj_dve, G * (PROJS // 2) + PROJS // 2)
                else:
                    pe.wait_ge(exp_ready, U * 2 - 2)
                for par in range(2):
                    pe.matmul(S(u, par)[:, :], mem["ident_bf"][:, :],
                              mem["causal"][:, :].unsqueeze(1).broadcast_to([P, 4, P]),
                              start=True, stop=False, skip_group_check=True)
                for i in range(4):
                    for par in range(2):
                        rows = slice(par * HEAD, (par + 1) * HEAD)
                        mm = pe.matmul(S(u, par)[:, i * P:(i + 1) * P],
                                       q_t[rows, 4 * octet + i, s * P:(s + 1) * P],
                                       k_t[rows, 4 * octet + i, s * P:(s + 1) * P],
                                       start=False, stop=True, skip_group_check=True)
                        if i == 3:
                            mm.then_inc(s_ready, 1)

            def attend(G, u):
                U = G * GU + u
                s, octet = u // 2, u % 2
                for par in range(2):
                    pe.wait_ge(exp_ready, U * 2 + par + 1)
                    for i in range(4):
                        tr = pe.transpose(PT[par][:, i * P:(i + 1) * P], prob[:, u % 2, 2 * i + par, :], ident[:, :])
                    tr.then_inc(pt_ready, 1)
                for par in range(2):
                    pe.wait_ge((pt_dve, pt_act)[par], U + 1)
                    if par == 0 and not (u == 0 and isinstance(G, int)):
                        pe.wait_ge(o_scaled, U)
                    for i in range(4):
                        j = 2 * i + par
                        head = octet * 8 + j
                        mm = pe.matmul(O[:, j * HEAD:(j + 1) * HEAD], prob_t[:, u % 2, j, :],
                                       v[:, s, head * HEAD:(head + 1) * HEAD], start=True, stop=True)
                mm.then_inc(o_ready, 1)

            def turn_outputs(G, u, first):
                U = G * GU + u
                s, octet = u // 2, u % 2
                pe.wait_ge(o_scaled, U + 1)
                if octet == 1:
                    pe.wait_ge(ot_hi, U)
                    pe.wait_ge(ot_lo, U)
                elif not (first and u == 0):
                    pe.wait_ge(res_ready, G * GS + s)
                for i in range(4):
                    tr = pe.transpose(OTY[:, i * P:(i + 1) * P], o[:, 2 * i:2 * i + 2, :].rearrange("p a b -> p (a b)"),
                                      ident[:, :])
                tr.then_inc(ot_ready, 1)

            def out_project(G, s):
                U = G * GU + 2 * s + 1
                pe.wait_ge(ot_hi, U + 1)
                pe.wait_ge(ot_lo, U + 1)
                for c in range(KW):
                    mm = product(pe, OTY[:, 0:D], [x[:, c, :] for x in o_t], [x[:, c, :] for x in wo], c == 0, c == KW - 1)
                mm.then_inc(y_ready, 1)

            def group(G, first):
                projections(G)
                for step in range(GU + 2):
                    if step >= 4 and step % 2 == 0:
                        out_project(G, step // 2 - 2)
                    if step < GU:
                        scores(G, step)
                    if 1 <= step <= GU:
                        attend(G, step - 1)
                    if 2 <= step:
                        turn_outputs(G, step - 2, first)
                out_project(G, GS - 1)
            group(0, True)
            with pe.Fori(1, GROUPS) as G:
                group(G, False)

        @block.scalar
        def _(act):
            def group(G, first):
                if not first:
                    act.wait_ge(proj_ready, G * PROJS)
                act.activation(xg[HI][:, :, :], ACT_T[:, :, bass.ds(G * GT, GT)], ACT.Copy).then_inc(xh_ready, 1)
                for r in range(0, PROJS, 2):
                    act.wait_ge(proj_ready, G * PROJS + r + 1)
                    if r < 2 * KW:
                        act.activation(q_t[:, r // 2, :], psum[r % RING][:, :], ACT.Copy,
                                       scale=HEAD ** -0.5).then_inc(proj_act, 1)
                    else:
                        act.activation(v[:, (r - 2 * KW) // 2, 0:BANK], psum[r % RING][:, :],
                                       ACT.Copy).then_inc(proj_act, 1)
                for step in range(GU + 2):
                    if 1 <= step <= GU:
                        u = step - 1
                        act.wait_ge(pt_ready, (G * GU + u) * 2 + 2)
                        act.activation(prob_t[:, u % 2, 1:8:2, :], PT[1][:, :].rearrange("p (i k) -> p i k", i=4),
                                       ACT.Copy).then_inc(pt_act, 1)
                    if step < GU:
                        U = G * GU + step
                        for par in range(2):
                            act.wait_ge(max_ready, U * 2 + par + 1)
                            for i in range(4):
                                j = 2 * i + par
                                e = act.activation(prob[:, step % 2, j, :], S(step, par)[:, i * P:(i + 1) * P],
                                                   ACT.Exp, bias=neg_max[:, step % 2, j:j + 1],
                                                   accum_out=total[:, step % 2, j:j + 1])
                            e.then_inc(exp_ready, 1)
                    if step >= 2:
                        u = step - 2
                        U = G * GU + u
                        act.wait_ge(ot_ready, U + 1)
                        if u % 2 == 0 and not (first and u == 0):
                            act.wait_ge(y_ready, G * GS + u // 2)
                        act.activation(o_t[HI][:, 4 * (u % 2):4 * (u % 2) + 4, :],
                                       OTY[:, :].rearrange("p (i k) -> p i k", i=4), ACT.Copy).then_inc(ot_hi, 1)
            group(0, True)
            with act.Fori(1, GROUPS) as G:
                group(G, False)

        @block.vector
        def _(dve):
            def finish(G, s):
                b = G * GS + s
                i = s % 2
                dve.wait_ge(y_ready, b + 1)
                dve.tensor_tensor(res[:, :], OTY[:, 0:D],
                                  ACTV[:, bass.ds(b, 1), :].rearrange("p a d -> p (a d)"), ALU.add).then_inc(res_ready, 1)
                dve.wait_ge(res_ready, b + 1)
                dve.bn_stats(stats[:, i, :], res[:, :]).then_inc(stats_ready, 1)
                dve.wait_ge(stats_ready, b + 1)
                dve.sem_inc(stats_seen, 1)
                dve.bn_aggr(mv[:, i, :], stats[:, i, :]).then_inc(aggr_ready, 1)
                dve.wait_ge(aggr_ready, b + 1)
                dve.tensor_scalar(ve[:, i:i + 1], mv[:, i, 1:2], EPS, None, ALU.add).then_inc(var_ready, 1)
                dve.wait_ge(rstd_ready, b + 1)
                dve.tensor_scalar(z[:, i, :], res[:, :], mv[:, i, 0:1], ve[:, i:i + 1],
                                  ALU.subtract, ALU.mult).then_inc(z_ready, 1)

            def group(G, first):
                if not first:
                    dve.wait_ge(proj_ready, G * PROJS)
                dve.wait_ge(xh_ready, G + 1)
                dve.tensor_tensor(xg[LO][:, :, :], ACT_T[:, :, bass.ds(G * GT, GT)], xg[HI][:, :, :].bitcast(F32),
                                  ALU.subtract).then_inc(xl_ready, 1)
                for r in range(1, PROJS, 2):
                    dve.wait_ge(proj_ready, G * PROJS + r + 1)
                    out = k_t[:, r // 2, :] if r < 2 * KW else v[:, (r - 2 * KW) // 2, BANK:2 * BANK]
                    dve.tensor_copy(out, psum[r % RING][:, :]).then_inc(proj_dve, 1)
                for step in range(GU + 2):
                    if step >= 4 and step % 2 == 0:
                        finish(G, step // 2 - 2)
                    if step < GU:
                        U = G * GU + step
                        for par in range(2):
                            dve.wait_ge(s_ready, U * 2 + par + 1)
                            dve.tensor_reduce(neg_max[:, step % 2, par:8:2],
                                              S(step, par)[:, :].rearrange("p (i k) -> p i k", i=4), AX.X, ALU.max,
                                              negate=True).then_inc(max_ready, 1)
                    if 1 <= step <= GU:
                        u = step - 1
                        U = G * GU + u
                        dve.wait_ge(pt_ready, U * 2 + 1)
                        dve.tensor_copy(prob_t[:, u % 2, 0:8:2, :],
                                        PT[0][:, :].rearrange("p (i k) -> p i k", i=4)).then_inc(pt_dve, 1)
                        dve.wait_ge(exp_ready, U * 2 + 2)
                        dve.reciprocal(inv[:, u % 2, :], total[:, u % 2, :]).then_inc(inv_ready, 1)
                        dve.wait_ge(inv_ready, U + 1)
                        dve.wait_ge(o_ready, U + 1)
                        if not (first and u == 0):
                            dve.wait_ge(ot_ready, U)
                        dve.tensor_tensor(o[:, :, :], O[:, :].rearrange("p (j d) -> p j d", j=8),
                                          inv[:, u % 2, :].unsqueeze(2).broadcast_to([P, 8, HEAD]),
                                          ALU.mult).then_inc(o_scaled, 1)
                    if step >= 2:
                        u = step - 2
                        U = G * GU + u
                        dve.wait_ge(ot_hi, U + 1)
                        cs = slice(4 * (u % 2), 4 * (u % 2) + 4)
                        dve.tensor_tensor(o_t[LO][:, cs, :], OTY[:, :].rearrange("p (i k) -> p i k", i=4),
                                          o_t[HI][:, cs, :].bitcast(F32), ALU.subtract).then_inc(ot_lo, 1)
                finish(G, GS - 1)
            group(0, True)
            with dve.Fori(1, GROUPS) as G:
                group(G, False)

        @block.gpsimd
        def _(pool):
            def sequence(b, i):
                pool.wait_ge(var_ready, b + 1)
                pool.tensor_tensor(ve[:, i:i + 1], ve[:, i:i + 1], neghalf[:, 0:1], ALU.pow).then_inc(rstd_ready, 1)
                pool.wait_ge(z_ready, b + 1)
                pool.tensor_tensor(zg[:, :], z[:, i, :], ln_g[:, :], ALU.mult).then_inc(zg_ready, 1)
                pool.wait_ge(zg_ready, b + 1)
                pool.tensor_tensor(zb[:, :], zg[:, :], ln_b[:, :], ALU.add).then_inc(zb_ready, 1)
                pool.wait_ge(zb_ready, b + 1)
                xb = X[:, bass.ds(b, 1), :].rearrange("p a d -> p (a d)")
                pool.tensor_tensor(xb, xb, zb[:, :], ALU.add).then_inc(x_ready, 1)
            pool.wait_ge(mem["attn_ln_loaded"], 32)
            with pool.Fori(0, SEQS // 2) as pairs:
                for i in range(2):
                    sequence(pairs * 2 + i, i)


def norm_state(nc, ctx, mem, name, width):
    norm = {"width": width, "neghalf": mem["neghalf"]}
    for what, shape in (("stats", [P, width, 6]), ("mv", [P, width, 2]), ("ve", [P, width])):
        norm[what] = ctx.enter_context(nc.sbuf_tensor(f"{name}_{what}", shape, F32))
    for what in ("stats_ready", "stats_seen", "aggr_ready", "var_ready", "rstd_ready", "z_ready"):
        norm[what] = mem["sems"](f"{name}_{what}")
    return norm


def norm_measure(dve, norm, n, rows):
    w = norm["width"]
    for i in range(w):
        dve.bn_stats(norm["stats"][:, i, :], rows(i)).then_inc(norm["stats_ready"], 1)
    dve.wait_ge(norm["stats_ready"], n * w + w)
    dve.sem_inc(norm["stats_seen"], 1)
    for i in range(w):
        dve.bn_aggr(norm["mv"][:, i, :], norm["stats"][:, i, :]).then_inc(norm["aggr_ready"], 1)
    dve.wait_ge(norm["aggr_ready"], n * w + w)
    dve.tensor_scalar(norm["ve"][:, :], norm["mv"][:, :, 1], EPS, None, ALU.add).then_inc(norm["var_ready"], 1)


def norm_invert(pool, norm, n):
    ve = norm["ve"][:, :]
    pool.wait_ge(norm["var_ready"], n + 1)
    pool.tensor_tensor(ve, ve, norm["neghalf"][:, 0:norm["width"]], ALU.pow).then_inc(norm["rstd_ready"], 1)


def norm_apply(dve, norm, n, rows, outs):
    dve.wait_ge(norm["rstd_ready"], n + 1)
    for i in range(norm["width"]):
        dve.tensor_scalar(outs(i), rows(i), norm["mv"][:, i, 0:1], norm["ve"][:, i:i + 1],
                          ALU.subtract, ALU.mult).then_inc(norm["z_ready"], 1)


def row_of(tensor, index):
    return tensor[:, bass.ds(index, 1), :].rearrange("p a d -> p (a d)")


XHEAD = D // HEADS
HPC = P // XHEAD
ROWT = 32
TILES = P // ROWT


def stage_cross_attention(nc, ctx, io, mem):
    X, ident, neghalf, psum = mem["x"], mem["ident"], mem["neghalf"], mem["psum"]
    sb = lambda name, shape, dt=F32: ctx.enter_context(nc.sbuf_tensor("x_" + name, shape, dt))
    sem = lambda name: mem["sems"]("x_" + name)
    pair = lambda name, shape: (sb(name + "_hi", shape, F32R), sb(name + "_lo", shape, F32R))
    norm = norm_state(nc, ctx, mem, "xn", GS)
    w_raw = sb("w_raw", [P, 4, KD * D])
    w = pair("w", [P, 4, KD * D])
    wq, wk, wv, wo = (chunks_of(w, i, KD) for i in range(4))
    bq, bk = sb("bq", [P, KD]), sb("bk", [P, KD])
    bq_scaled = sb("bq_scaled", [P, KD])
    bv, bo = sb("bv", [P, D]), sb("bo", [P, D])
    sel = sb("sel", [P, 2])
    ctx_raw = sb("ctx_raw", [P, 2, KD, GT])
    cg = pair("cg", [P, KD, GT])
    z = sb("z", [P, GS, D])
    xg = pair("xg", [P, KD, GT])
    q_t = sb("q_t", [P, KD, GT])
    k_t = sb("k_t", [P, 2, KD, GT])
    v = sb("v", [P, GS, D])
    prob = sb("prob", [P, 2, TILES, 4, P])
    prob_t = sb("prob_t", [P, 2, TILES, 4, P])
    neg_max, total, inv = sb("neg_max", [P, 2, HEADS]), sb("total", [P, 2, HEADS]), sb("inv", [P, 2, HEADS])
    o = sb("o", [P, 2, D])
    o_t = pair("o_t", [P, KD, P])

    w_loaded, bias_loaded, ctx_loaded = sem("w_loaded"), sem("bias_loaded"), sem("ctx_loaded")
    w_hi, w_split = sem("w_hi"), sem("w_split")
    ctx_hi, ctx_lo = sem("ctx_hi"), sem("ctx_lo")
    setup, bq_ready = sem("setup"), sem("bq_ready")
    sel_step = sem("sel_step")
    tr_ready, xh_ready, xl_ready = sem("tr_ready"), sem("xh_ready"), sem("xl_ready")
    q_ready, k_ready, v_ready = sem("q_ready"), sem("k_ready"), sem("v_ready")
    q_copied, k_copied, v_copied = sem("q_copied"), sem("k_copied"), sem("v_copied")
    s_ready, max_ready, exp_ready = sem("s_ready"), sem("max_ready"), sem("exp_ready")
    pt_ready, pt_act, pt_dve = sem("pt_ready"), sem("pt_act"), sem("pt_dve")
    o_ready, inv_ready, o_scaled = sem("o_ready"), sem("inv_ready"), sem("o_scaled")
    ot_ready, ot_hi, ot_lo = sem("ot_ready"), sem("ot_hi"), sem("ot_lo")
    y_ready, y_added, x_ready = sem("y_ready"), sem("y_added"), sem("x_ready")

    PT = (psum[4], psum[5])
    O, OTY = psum[6], psum[7]
    B16 = lambda G, s: G * GS + s
    HEAD_OF = lambda r, i: (i // 2) * HPC + 2 * r + i % 2

    with nc.Block() as block:
        @block.sync
        def _(sp):
            for i, name in enumerate(("W_q", "W_k", "W_v", "W_o")):
                sp.dma_start(w_raw[:, i, :], io["L0_xattn_" + name + "_laid"]).then_inc(w_loaded, 16)
            for tile, name in ((bq, "b_q"), (bk, "b_k")):
                sp.dma_start(tile[:, :], io["L0_xattn_" + name + "_laid"]).then_inc(bias_loaded, 16)
            for tile, name in ((bv, "b_v"), (bo, "b_o")):
                sp.dma_start(tile[:, :], io["L0_xattn_" + name].unsqueeze(0).broadcast_to([P, D])).then_inc(bias_loaded, 16)
            with sp.Fori(0, GROUPS // 2) as pairs:
                for par in range(2):
                    G = pairs * 2 + par
                    sp.wait_ge(ctx_lo, G)
                    sp.dma_start(ctx_raw[:, par, :, :], io["ctx_t_laid"][:, :, bass.ds(G * GT, GT)]).then_inc(ctx_loaded, 16)

        @block.gpsimd
        def _(pool):
            pool.memset(sel[:, :], 0.0).then_inc(sel_step, 1)
            pool.wait_ge(sel_step, 1)
            for r in range(TILES):
                if r > 0:
                    pool.wait_ge(setup, 2 * r)
                rows = slice(r * ROWT, (r + 1) * ROWT)
                pool.affine_select(out=sel[rows, 0:1], in_=sel[rows, 0:1], compare_op=ALU.is_ge, fill=1.0,
                                   base=-XHEAD, pattern=[[1, 1]], channel_multiplier=1).then_inc(setup, 1)
                pool.wait_ge(setup, 2 * r + 1)
                pool.affine_select(out=sel[rows, 1:2], in_=sel[rows, 1:2], compare_op=ALU.is_ge, fill=1.0,
                                   base=XHEAD - 1, pattern=[[1, 1]], channel_multiplier=-1).then_inc(setup, 1)
            pool.wait_ge(setup, 2 * TILES)
            pool.wait_ge(w_loaded, 64)
            for i in (1, 2, 0, 3):
                pool.tensor_copy(w[HI][:, i, :], w_raw[:, i, :]).then_inc(w_hi, 1)
            for n, i in enumerate((1, 2, 0, 3)):
                pool.wait_ge(w_hi, n + 1)
                pool.tensor_tensor(w[LO][:, i, :], w_raw[:, i, :], w[HI][:, i, :].bitcast(F32), ALU.subtract).then_inc(w_split, 1)

            def group(G, par, first):
                norm_invert(pool, norm, G)
                pool.wait_ge(ctx_loaded, G * 16 + 16)
                if not first:
                    pool.wait_ge(v_ready, G * 2)
                    pool.wait_ge(k_ready, G * KD)
                pool.tensor_copy(cg[HI][:, :, :], ctx_raw[:, par, :, :]).then_inc(ctx_hi, 1)
                pool.wait_ge(ctx_hi, G + 1)
                pool.tensor_tensor(cg[LO][:, :, :], ctx_raw[:, par, :, :], cg[HI][:, :, :].bitcast(F32),
                                   ALU.subtract).then_inc(ctx_lo, 1)
                for s in range(GS):
                    b = B16(G, s)
                    pool.wait_ge(y_added, b + 1)
                    pool.tensor_tensor(row_of(X, b), row_of(X, b), bo[:, :], ALU.add).then_inc(x_ready, 1)
            pool.wait_ge(bias_loaded, 64)
            group(0, 0, True)
            group(1, 1, False)
            with pool.Fori(1, GROUPS // 2) as pairs:
                for par in range(2):
                    group(pairs * 2 + par, par, False)

        @block.vector
        def _(dve):
            dve.wait_ge(bias_loaded, 64)
            dve.tensor_scalar(bq_scaled[:, :], bq[:, :], XHEAD ** -0.5, None, ALU.mult).then_inc(bq_ready, 1)
            dve.wait_ge(setup, 2 * TILES)

            def group(G, first):
                norm_measure(dve, norm, G, lambda i: row_of(X, B16(G, i)))
                if not first:
                    dve.wait_ge(tr_ready, G * KD)
                norm_apply(dve, norm, G, lambda i: row_of(X, B16(G, i)), lambda i: z[:, i, :])
                for k in range(KD):
                    dve.wait_ge(k_ready, G * KD + k + 1)
                    for par in range(2):
                        kc = dve.tensor_scalar(k_t[:, par, k, :], psum[k][:, :], bk[:, k:k + 1], sel[:, par:par + 1],
                                               ALU.add, ALU.mult)
                    kc.then_inc(k_copied, 1)
                for h in range(2):
                    dve.wait_ge(v_ready, G * 2 + h + 1)
                    dve.tensor_tensor(v[:, 2 * h:2 * h + 2, :], psum[2 + h][:, :].rearrange("p (s d) -> p s d", s=2),
                                      bv[:, :].unsqueeze(1).broadcast_to([P, 2, D]), ALU.add).then_inc(v_copied, 1)
                for k in range(KD):
                    dve.wait_ge(xh_ready, G * KD + k + 1)
                    dve.tensor_tensor(xg[LO][:, k, :], psum[4 + k][:, :], xg[HI][:, k, :].bitcast(F32),
                                      ALU.subtract).then_inc(xl_ready, 1)
                for step in range(GS + 2):
                    if step < GS:
                        b = B16(G, step)
                        for r in range(TILES):
                            dve.wait_ge(s_ready, b * TILES + r + 1)
                            out = neg_max[:, step % 2, :].rearrange("p (c r a) -> p r c a", c=KD, r=TILES)[:, r, :, :]
                            dve.tensor_reduce(out, psum[r][:, :].rearrange("p (c a k) -> p c a k", c=KD, a=2), AX.X,
                                              ALU.max, negate=True).then_inc(max_ready, 1)
                            if step >= 1 and r % 2 == 1:
                                copy_turned(G, step - 1, r // 2)
                    elif step == GS:
                        for half in range(2):
                            copy_turned(G, step - 1, half)
                    if 1 <= step <= GS:
                        s = step - 1
                        b = B16(G, s)
                        dve.wait_ge(exp_ready, b * TILES + TILES)
                        dve.reciprocal(inv[:, s % 2, :], total[:, s % 2, :]).then_inc(inv_ready, 1)
                        dve.wait_ge(inv_ready, b + 1)
                        dve.wait_ge(o_ready, b + 1)
                        dve.tensor_tensor(o[:, s % 2, :].rearrange("p (h d) -> p h d", h=HEADS),
                                          O[:, 0:D].rearrange("p (h d) -> p h d", h=HEADS),
                                          inv[:, s % 2, :].unsqueeze(2).broadcast_to([P, HEADS, XHEAD]),
                                          ALU.mult).then_inc(o_scaled, 1)
                    if step >= 2:
                        b = B16(G, step - 2)
                        dve.wait_ge(ot_hi, b + 1)
                        dve.tensor_tensor(o_t[LO][:, :, :], OTY[:, 0:D].rearrange("p (k t) -> p k t", k=KD),
                                          o_t[HI][:, :, :].bitcast(F32), ALU.subtract).then_inc(ot_lo, 1)
                        dve.wait_ge(y_ready, b + 1)
                        dve.tensor_tensor(row_of(X, b), OTY[:, D:2 * D], row_of(X, b), ALU.add).then_inc(y_added, 1)

            def copy_turned(G, s, half):
                b = B16(G, s)
                r = 2 * half
                dve.wait_ge(pt_ready, b * TILES + r + 1)
                dve.tensor_copy(prob_t[:, s % 2, r, :, :], PT[0][:, :].rearrange("p (i k) -> p i k", i=4)).then_inc(pt_dve, 1)
            group(0, True)
            with dve.Fori(1, GROUPS) as G:
                group(G, False)

        @block.scalar
        def _(act):
            act.wait_ge(bq_ready, 1)

            def group(G, first):
                for k in range(KD):
                    act.wait_ge(tr_ready, G * KD + k + 1)
                    act.activation(xg[HI][:, k, :], psum[4 + k][:, :], ACT.Copy).then_inc(xh_ready, 1)
                for k in range(KD):
                    act.wait_ge(q_ready, G * KD + k + 1)
                    act.activation(q_t[:, k, :], psum[6 + k][:, :], ACT.Identity, bias=bq_scaled[:, k:k + 1],
                                   scale=XHEAD ** -0.5).then_inc(q_copied, 1)
                for step in range(GS + 2):
                    if step < GS:
                        b = B16(G, step)
                        for r in range(TILES):
                            act.wait_ge(max_ready, b * TILES + r + 1)
                            for i in range(4):
                                h = HEAD_OF(r, i)
                                e = act.activation(prob[:, step % 2, r, i, :], psum[r][:, i * P:(i + 1) * P], ACT.Exp,
                                                   bias=neg_max[:, step % 2, h:h + 1],
                                                   accum_out=total[:, step % 2, h:h + 1])
                            e.then_inc(exp_ready, 1)
                            if step >= 1 and r % 2 == 1:
                                copy_turned(G, step - 1, r // 2)
                    elif step == GS:
                        for half in range(2):
                            copy_turned(G, step - 1, half)
                    if step >= 2:
                        b = B16(G, step - 2)
                        act.wait_ge(ot_ready, b + 1)
                        act.activation(o_t[HI][:, :, :], OTY[:, 0:D].rearrange("p (k t) -> p k t", k=KD),
                                       ACT.Copy).then_inc(ot_hi, 1)

            def copy_turned(G, s, half):
                b = B16(G, s)
                r = 2 * half + 1
                act.wait_ge(pt_ready, b * TILES + r + 1)
                act.activation(prob_t[:, s % 2, r, :, :], PT[1][:, :].rearrange("p (i k) -> p i k", i=4),
                               ACT.Copy).then_inc(pt_act, 1)
            group(0, True)
            with act.Fori(1, GROUPS) as G:
                group(G, False)

        @block.tensor
        def _(pe):
            pe.wait_ge(w_split, 4)

            def group(G, first):
                pe.wait_ge(ctx_lo, G + 1)
                for k in range(KD):
                    for i in range(KD):
                        mm = product(pe, psum[k][:, :], [x[:, i, k * P:(k + 1) * P] for x in wk], [x[:, i, :] for x in cg], i == 0, i == KD - 1)
                    mm.then_inc(k_ready, 1)
                for h in range(2):
                    for s in (2 * h, 2 * h + 1):
                        for i in range(KD):
                            mm = product(pe, psum[2 + h][:, (s % 2) * D:(s % 2 + 1) * D], [x[:, i, s * P:(s + 1) * P] for x in cg],
                                         [x[:, i, :] for x in wv], i == 0, i == KD - 1)
                    mm.then_inc(v_ready, 1)
                pe.wait_ge(norm["z_ready"], G * GS + GS)
                for k in range(KD):
                    for s in range(GS):
                        tr = pe.transpose(psum[4 + k][:, s * P:(s + 1) * P], z[:, s, k * P:(k + 1) * P], ident[:, :])
                    tr.then_inc(tr_ready, 1)
                pe.wait_ge(xh_ready, G * KD + KD)
                pe.wait_ge(xl_ready, G * KD + KD)
                if not first:
                    pe.wait_ge(y_added, G * GS)
                for k in range(KD):
                    for i in range(KD):
                        mm = product(pe, psum[6 + k][:, :], [x[:, i, k * P:(k + 1) * P] for x in wq], [x[:, i, :] for x in xg], i == 0, i == KD - 1)
                    mm.then_inc(q_ready, 1)
                pe.wait_ge(k_copied, G * KD + KD)
                pe.wait_ge(v_copied, G * 2 + 2)
                pe.wait_ge(q_copied, G * KD + KD)
                for step in range(GS + 2):
                    if step < GS:
                        b = B16(G, step)
                        for r in range(TILES):
                            if step > 0:
                                pe.wait_ge(exp_ready, b * TILES - TILES + r + 1)
                            rows = slice(r * ROWT, (r + 1) * ROWT)
                            for i in range(4):
                                mm = pe.matmul(psum[r][:, i * P:(i + 1) * P],
                                               q_t[rows, i // 2, step * P:(step + 1) * P],
                                               k_t[rows, i % 2, i // 2, step * P:(step + 1) * P], start=True, stop=True,
                                               tile_position=(r * ROWT, 0))
                            mm.then_inc(s_ready, 1)
                            if step >= 1:
                                turn(G, step - 1, r)
                    elif step == GS:
                        for r in range(TILES):
                            turn(G, step - 1, r)
                    if 1 <= step <= GS:
                        s = step - 1
                        b = B16(G, s)
                        if not (first and s == 0):
                            pe.wait_ge(o_scaled, b)
                        for r in range(TILES):
                            pe.wait_ge((pt_dve, pt_act)[r % 2], b * 2 + r // 2 + 1)
                            for i in range(4):
                                h = HEAD_OF(r, i)
                                mm = pe.matmul(O[:, h * XHEAD:(h + 1) * XHEAD], prob_t[:, s % 2, r, i, :],
                                               v[:, s, h * XHEAD:(h + 1) * XHEAD], start=True, stop=True)
                        mm.then_inc(o_ready, 1)
                    if step >= 2:
                        s = step - 2
                        b = B16(G, s)
                        pe.wait_ge(o_scaled, b + 1)
                        if not (first and s == 0):
                            pe.wait_ge(y_added, b)
                        for k in range(KD):
                            tr = pe.transpose(OTY[:, k * P:(k + 1) * P], o[:, s % 2, k * P:(k + 1) * P], ident[:, :])
                        tr.then_inc(ot_ready, 1)
                        pe.wait_ge(ot_hi, b + 1)
                        pe.wait_ge(ot_lo, b + 1)
                        for k in range(KD):
                            mm = product(pe, OTY[:, D:2 * D], [x[:, k, :] for x in o_t], [x[:, k, :] for x in wo], k == 0, k == KD - 1)
                        mm.then_inc(y_ready, 1)

            def turn(G, s, r):
                b = B16(G, s)
                pe.wait_ge(exp_ready, b * TILES + r + 1)
                if r >= 2:
                    pe.wait_ge((pt_dve, pt_act)[r % 2], b * 2 + 1)
                for i in range(4):
                    tr = pe.transpose(PT[r % 2][:, i * P:(i + 1) * P], prob[:, s % 2, r, i, :], ident[:, :])
                tr.then_inc(pt_ready, 1)
            group(0, True)
            with pe.Fori(1, GROUPS) as G:
                group(G, False)


EXPERTS = 8
FFN = 512
KF = FFN // P
W_PARTS = 3
W_COLS = KD * FFN


def stage_experts(nc, ctx, io, mem):
    X, ident, neghalf, psum = mem["x"], mem["ident"], mem["neghalf"], mem["psum"]
    sb = lambda name, shape, dt=F32: ctx.enter_context(nc.sbuf_tensor("e_" + name, shape, dt))
    sem = lambda name: mem["sems"]("e_" + name)
    pair = lambda name, shape: (sb(name + "_hi", shape, F32R), sb(name + "_lo", shape, F32R))
    norm = norm_state(nc, ctx, mem, "en", GS)
    raw = sb("raw", [P, W_PARTS, W_COLS])
    w = pair("w", [P, 2, W_PARTS, W_COLS])
    router_raw = sb("router_raw", [P, KD * EXPERTS])
    router = pair("router", [P, KD * EXPERTS])
    z = sb("z", [P, GS, D])
    xn = pair("xn", [P, KD, SEQS * P])
    gate = sb("gate", [P, 2, GT])
    h_raw = sb("h_raw", [P, 2, GT])
    h = pair("h", [P, 2, KF, GT])
    table = lambda name: sb(name, [P, SEQS, EXPERTS])
    column = lambda name: sb(name, [P, SEQS])
    logit, prob, left, cand, first_hot, second_hot, share, iota = (table(x) for x in (
        "logit", "prob", "left", "cand", "first_hot", "second_hot", "share", "iota"))
    col = {name: column(name) for name in ("max", "sum", "inv", "p1", "p2", "at1", "at2", "e", "w1", "w2", "gap")}

    w_loaded, hi_ready, w_split = sem("w_loaded"), sem("hi_ready"), sem("w_split")
    split_seen = sem("split_seen")
    r_loaded, r_hi, r_split = sem("r_loaded"), sem("r_hi"), sem("r_split")
    iota_ready = sem("iota_ready")
    tr_ready, xh_ready, xl_ready = sem("tr_ready"), sem("xh_ready"), sem("xl_ready")
    logit_ready = sem("logit_ready")
    route_step, route_exp, route_sem = sem("route_step"), sem("route_exp"), sem("route_ready")
    gate_ready, up_ready = sem("gate_ready"), sem("up_ready")
    silu_ready, prod_ready = sem("silu_ready"), sem("prod_ready")
    h_hi, h_lo = sem("h_hi"), sem("h_lo")
    down_ready, added = sem("down_ready"), sem("added")
    GATE, UP = (psum[0], psum[1]), (psum[2], psum[3])
    DOWN = lambda G, half: psum[4 + 2 * (G % 2) + half]
    PAIRS = EXPERTS // 2

    def steps(eng, ahead, rest):
        ahead(0, 0, 0)

        def body(pairs, last):
            for slot in range(2):
                e = pairs * 2 + slot
                for G in range(GROUPS):
                    if G < GROUPS - 1:
                        ahead(e, slot, G + 1)
                    elif not (last and slot == 1):
                        ahead(e + 1, 1 - slot, 0)
                    rest(e, slot, G)
        body(0, False)
        with eng.Fori(1, PAIRS - 1) as pairs:
            body(pairs, False)
        body(PAIRS - 1, True)

    early = lambda n, least: isinstance(n, int) and n < least

    with nc.Block() as block:
        @block.sync
        def _(sp):
            sp.dma_start(router_raw[:, :], io["router_laid"]).then_inc(r_loaded, 16)
            sp.dma_start(raw[:, :, :].rearrange("p a n -> p (a n)"), io["experts_laid"][0]).then_inc(w_loaded, 16)
            with sp.Fori(1, EXPERTS) as e:
                sp.wait_ge(w_split, e * W_PARTS)
                sp.dma_start(raw[:, :, :], io["experts_laid"][bass.ds(e, 1)].rearrange(
                    "e p (a n) -> p (e a) n", a=W_PARTS)).then_inc(w_loaded, 16)

        @block.gpsimd
        def _(pool):
            def split(e, slot, part):
                if part == 0:
                    pool.wait_ge(w_loaded, e * 16 + 16)
                    if not early(e, 2):
                        pool.wait_ge(down_ready, e * GROUPS - GROUPS)
                    pool.sem_inc(split_seen, 1)
                pool.tensor_copy(w[HI][:, slot, part, :], raw[:, part, :]).then_inc(hi_ready, 1)
                pool.wait_ge(hi_ready, e * W_PARTS + part + 1)
                pool.tensor_tensor(w[LO][:, slot, part, :], raw[:, part, :], w[HI][:, slot, part, :].bitcast(F32),
                                   ALU.subtract).then_inc(w_split, 1)

            def h_low(e, slot, G):
                n = e * GROUPS + G
                for f in range(KF):
                    pool.wait_ge(h_hi, n * KF + f + 1)
                    pool.tensor_tensor(h[LO][:, G % 2, f, :], h_raw[:, f % 2, :], h[HI][:, G % 2, f, :].bitcast(F32),
                                       ALU.subtract).then_inc(h_lo, 1)

            pool.iota(iota[:, :, :], pattern=[[0, SEQS], [1, EXPERTS]], base=0, channel_multiplier=0,
                      allow_small_or_imprecise_dtypes=True).then_inc(iota_ready, 1)
            for G in range(GROUPS):
                norm_invert(pool, norm, G)
            pool.wait_ge(r_loaded, 16)
            pool.tensor_copy(router[HI][:, :], router_raw[:, :]).then_inc(r_hi, 1)
            pool.wait_ge(r_hi, 1)
            pool.tensor_tensor(router[LO][:, :], router_raw[:, :], router[HI][:, :].bitcast(F32),
                               ALU.subtract).then_inc(r_split, 1)
            for part in range(W_PARTS):
                split(0, 0, part)

            def body(pairs, last):
                for slot in range(2):
                    e = pairs * 2 + slot
                    for G in range(GROUPS):
                        h_low(e, slot, G)
                        if G < W_PARTS and not (last and slot == 1):
                            split(e + 1, 1 - slot, G)
            body(0, False)
            with pool.Fori(1, PAIRS - 1) as pairs:
                body(pairs, False)
            body(PAIRS - 1, True)

        @block.tensor
        def _(pe):
            for G in range(GROUPS):
                pe.wait_ge(norm["z_ready"], G * GS + GS)
                if G > 0:
                    pe.wait_ge(xl_ready, G * KD)
                for k in range(KD):
                    for s in range(GS):
                        tr = pe.transpose(psum[6 + k][:, s * P:(s + 1) * P], z[:, s, k * P:(k + 1) * P], ident[:, :])
                    tr.then_inc(tr_ready, 1)
            pe.wait_ge(r_split, 1)
            pe.wait_ge(xh_ready, GROUPS * KD)
            pe.wait_ge(xl_ready, GROUPS * KD)
            for b in range(SEQS):
                for k in range(KD):
                    mm = product(pe, psum[5][:, b * EXPERTS:(b + 1) * EXPERTS], [x[:, k, b * P:(b + 1) * P] for x in xn],
                                 [x[:, k * EXPERTS:(k + 1) * EXPERTS] for x in router], k == 0, k == KD - 1)
            mm.then_inc(logit_ready, 1)

            def widen(e, slot, G):
                n = e * GROUPS + G
                tokens = slice(G * GT, (G + 1) * GT)
                if G == 0:
                    pe.wait_ge(w_split, e * W_PARTS + 2)
                for f in range(KF):
                    for part, bank, ready, read in ((0, GATE[f % 2], gate_ready, silu_ready),
                                                    (1, UP[f % 2], up_ready, prod_ready)):
                        if not early(n * KF + f, 2):
                            pe.wait_ge(read, n * KF + f - 1)
                        for k in range(KD):
                            mm = product(pe, bank[:, :], [x[:, slot, part, k * FFN + f * P:k * FFN + (f + 1) * P] for x in w],
                                         [x[:, k, tokens] for x in xn], k == 0, k == KD - 1)
                        mm.then_inc(ready, 1)

            def down(e, slot, G):
                n = e * GROUPS + G
                if G == 0:
                    pe.wait_ge(w_split, e * W_PARTS + 3)
                if not early(n, 2):
                    pe.wait_ge(added, n * GS - GS)
                if early(n, 2):
                    pe.wait_ge(route_step, 1)
                pe.wait_ge(h_hi, n * KF + KF)
                pe.wait_ge(h_lo, n * KF + KF)
                for s in range(GS):
                    out = DOWN(G, s // 2)[:, (s % 2) * D:(s % 2 + 1) * D]
                    for f in range(KF):
                        mm = product(pe, out, [x[:, G % 2, f, s * P:(s + 1) * P] for x in h], [x[:, slot, 2, f * D:(f + 1) * D] for x in w],
                                     f == 0, f == KF - 1)
                mm.then_inc(down_ready, 1)
            steps(pe, widen, down)

        @block.scalar
        def _(act):
            for G in range(GROUPS):
                for k in range(KD):
                    act.wait_ge(tr_ready, G * KD + k + 1)
                    act.activation(xn[HI][:, k, G * GT:(G + 1) * GT], psum[6 + k][:, :], ACT.Copy).then_inc(xh_ready, 1)
            for i, (out, in_) in enumerate(((prob[:, :, :], logit[:, :, :]), (col["e"][:, :], col["gap"][:, :]))):
                act.wait_ge(route_exp, i + 1)
                act.activation(out, in_, ACT.Exp).then_inc(route_sem, 1)

            def silu(n, f):
                act.wait_ge(gate_ready, n * KF + f + 1)
                if not early(n * KF + f, 2):
                    act.wait_ge(prod_ready, n * KF + f - 1)
                act.activation(gate[:, f % 2, :], GATE[f % 2][:, :], ACT.Silu).then_inc(silu_ready, 1)

            def high(n, G, f):
                act.wait_ge(prod_ready, n * KF + f + 1)
                if f == 0 and not early(n, 2):
                    act.wait_ge(down_ready, n - 1)
                act.activation(h[HI][:, G % 2, f, :], h_raw[:, f % 2, :], ACT.Copy).then_inc(h_hi, 1)

            def step(e, slot, G):
                n = e * GROUPS + G
                silu(n, 0)
                for f in range(1, KF):
                    silu(n, f)
                    high(n, G, f - 1)
                high(n, G, KF - 1)
            for G in range(GROUPS):
                step(0, 0, G)
            with act.Fori(1, EXPERTS) as e:
                for G in range(GROUPS):
                    step(e, None, G)

        @block.vector
        def _(dve):
            x_row = lambda G: lambda i: X[:, G * GS + i, :]
            for G in range(GROUPS):
                norm_measure(dve, norm, G, x_row(G))
                if G > 0:
                    dve.wait_ge(tr_ready, G * KD)
                norm_apply(dve, norm, G, x_row(G), lambda i: z[:, i, :])
                for k in range(KD):
                    dve.wait_ge(xh_ready, G * KD + k + 1)
                    tokens = slice(G * GT, (G + 1) * GT)
                    dve.tensor_tensor(xn[LO][:, k, tokens], psum[6 + k][:, :], xn[HI][:, k, tokens].bitcast(F32),
                                      ALU.subtract).then_inc(xl_ready, 1)

            count = [0]

            def then(op):
                count[0] += 1
                op.then_inc(route_step, 1)
                dve.wait_ge(route_step, count[0])
            wide = lambda name: col[name][:, :].unsqueeze(2).broadcast_to([P, SEQS, EXPERTS])
            dve.wait_ge(logit_ready, 1)
            dve.wait_ge(iota_ready, 1)
            then(dve.tensor_copy(logit[:, :, :], psum[5][:, 0:SEQS * EXPERTS].rearrange("p (b e) -> p b e", b=SEQS)))
            then(dve.tensor_reduce(col["max"][:, :], logit[:, :, :], AX.X, ALU.max))
            dve.tensor_tensor(logit[:, :, :], logit[:, :, :], wide("max"), ALU.subtract).then_inc(route_exp, 1)
            dve.wait_ge(route_sem, 1)
            then(dve.tensor_reduce(col["sum"][:, :], prob[:, :, :], AX.X, ALU.add))
            then(dve.reciprocal(col["inv"][:, :], col["sum"][:, :]))
            then(dve.tensor_tensor(prob[:, :, :], prob[:, :, :], wide("inv"), ALU.mult))

            def largest(values, value, at, hot):
                then(dve.tensor_reduce(col[value][:, :], values[:, :, :], AX.X, ALU.max))
                then(dve.tensor_tensor(cand[:, :, :], values[:, :, :], wide(value), ALU.is_equal))
                then(dve.scalar_tensor_tensor(out=cand[:, :, :], in0=cand[:, :, :], scalar=-float(EXPERTS),
                                              in1=iota[:, :, :], op0=ALU.mult, op1=ALU.add))
                then(dve.tensor_reduce(col[at][:, :], cand[:, :, :], AX.X, ALU.min))
                then(dve.tensor_tensor(hot[:, :, :], cand[:, :, :], wide(at), ALU.is_equal))
            largest(prob, "p1", "at1", first_hot)
            then(dve.scalar_tensor_tensor(out=left[:, :, :], in0=first_hot[:, :, :], scalar=-4.0, in1=prob[:, :, :],
                                          op0=ALU.mult, op1=ALU.add))
            largest(left, "p2", "at2", second_hot)
            dve.tensor_tensor(col["gap"][:, :], col["p2"][:, :], col["p1"][:, :], ALU.subtract).then_inc(route_exp, 1)
            dve.wait_ge(route_sem, 2)
            then(dve.tensor_scalar(col["sum"][:, :], col["e"][:, :], 1.0, None, ALU.add))
            then(dve.reciprocal(col["w1"][:, :], col["sum"][:, :]))
            then(dve.tensor_tensor(col["w2"][:, :], col["e"][:, :], col["w1"][:, :], ALU.mult))
            then(dve.tensor_tensor(first_hot[:, :, :], first_hot[:, :, :], wide("w1"), ALU.mult))
            then(dve.tensor_tensor(second_hot[:, :, :], second_hot[:, :, :], wide("w2"), ALU.mult))
            then(dve.tensor_tensor(share[:, :, :], first_hot[:, :, :], second_hot[:, :, :], ALU.add))

            def fuse(e, slot, G):
                n = e * GROUPS + G
                for f in range(KF):
                    dve.wait_ge(silu_ready, n * KF + f + 1)
                    dve.wait_ge(up_ready, n * KF + f + 1)
                    if not early(n * KF + f, 2):
                        dve.wait_ge(h_hi, n * KF + f - 1)
                        dve.wait_ge(h_lo, n * KF + f - 1)
                    dve.tensor_tensor(h_raw[:, f % 2, :], gate[:, f % 2, :], UP[f % 2][:, :], ALU.mult).then_inc(prod_ready, 1)

            def add(e, slot, G):
                n = e * GROUPS + G
                dve.wait_ge(down_ready, n + 1)
                if not early(n, GROUPS):
                    dve.wait_ge(added, n * GS - (GROUPS - 1) * GS)
                for s in range(GS):
                    b = G * GS + s
                    dve.scalar_tensor_tensor(out=X[:, b, :], in0=DOWN(G, s // 2)[:, (s % 2) * D:(s % 2 + 1) * D],
                                             scalar=share[:, b, bass.ds(e, 1)], in1=X[:, b, :], op0=ALU.mult,
                                             op1=ALU.add).then_inc(added, 1)
            steps(dve, fuse, add)


def stage_wide_attention(nc, ctx, io, mem):
    X, ident, neghalf, psum = mem["x"], mem["ident"], mem["neghalf"], mem["psum"]
    sb = lambda name, shape, dt=F32: ctx.enter_context(nc.sbuf_tensor("s_" + name, shape, dt))
    sem = lambda name: mem["sems"]("w_" + name)
    pair = lambda name, shape: (sb(name + "_hi", shape, F32R), sb(name + "_lo", shape, F32R))
    norm = norm_state(nc, ctx, mem, "wn", GS)
    w_raw = sb("w_raw", [P, 3, KD * D])
    w = pair("w", [P, 3, KD * D])
    wq, wk, wv = (chunks_of(w, i, KD) for i in range(3))
    z = sb("z", [P, GS, D])
    xg = pair("xg", [P, KD, GT])
    q_t, k_t = sb("q_t", [P, 2, KD, GT]), sb("k_t", [P, 2, KD, GT])
    v = sb("v", [P, 2, GS, D])
    prob, prob_t = sb("prob", [P, GS, P]), sb("prob_t", [P, GS, P])
    neg_max, total, inv = sb("neg_max", [P, GS]), sb("total", [P, GS]), sb("inv", [P, GS])

    w_loaded, w_hi, w_split = sem("w_loaded"), sem("w_hi"), sem("w_split")
    tr_ready, xh_ready, xl_ready = sem("tr_ready"), sem("xh_ready"), sem("xl_ready")
    q_ready, k_ready, v_ready = sem("q_ready"), sem("k_ready"), sem("v_ready")
    q_copied, k_copied, v_copied = sem("q_copied"), sem("k_copied"), sem("v_copied")
    s_ready, max_ready, exp_ready = sem("s_ready"), sem("max_ready"), sem("exp_ready")
    pt_ready, pt_copied = sem("pt_ready"), sem("pt_copied")
    o_ready, inv_ready, added = sem("o_ready"), sem("inv_ready"), sem("added")
    Q, K, TRV, S, PT, O = psum[0:2], psum[2:4], psum[4:6], psum[6], psum[7], psum[6:8]

    with nc.Block() as block:
        @block.sync
        def _(sp):
            for i, name in enumerate(("Wq", "Wk", "Wv")):
                sp.dma_start(w_raw[:, i, :], io["L1_attn_" + name + "_laid"]).then_inc(w_loaded, 16)

        @block.gpsimd
        def _(pool):
            norm_invert(pool, norm, 0)
            pool.wait_ge(w_loaded, 48)
            for i in range(3):
                pool.tensor_copy(w[HI][:, i, :], w_raw[:, i, :]).then_inc(w_hi, 1)
                pool.wait_ge(w_hi, i + 1)
                pool.tensor_tensor(w[LO][:, i, :], w_raw[:, i, :], w[HI][:, i, :].bitcast(F32), ALU.subtract).then_inc(w_split, 1)
            for G in range(1, GROUPS):
                norm_invert(pool, norm, G)

        @block.tensor
        def _(pe):
            def project(G):
                if G > 0:
                    pe.wait_ge(v_copied, 2 * G)
                pe.wait_ge(norm["z_ready"], G * GS + GS)
                for k in range(KD):
                    for s in range(GS):
                        tr = pe.transpose(TRV[k][:, s * P:(s + 1) * P], z[:, s, k * P:(k + 1) * P], ident[:, :])
                    tr.then_inc(tr_ready, 1)
                pe.wait_ge(xh_ready, G * KD + KD)
                pe.wait_ge(xl_ready, G * KD + KD)
                for banks, weights, i, ready, copied in ((Q, wq, 0, q_ready, q_copied), (K, wk, 1, k_ready, k_copied)):
                    pe.wait_ge(w_split, i + 1)
                    if G > 0:
                        pe.wait_ge(copied, G * KD)
                    for k in range(KD):
                        for j in range(KD):
                            mm = product(pe, banks[k][:, :], [x[:, j, k * P:(k + 1) * P] for x in weights], [x[:, j, :] for x in xg],
                                         j == 0, j == KD - 1)
                        mm.then_inc(ready, 1)
                pe.wait_ge(w_split, 3)
                for h in range(2):
                    for s in (2 * h, 2 * h + 1):
                        for j in range(KD):
                            mm = product(pe, TRV[h][:, (s % 2) * D:(s % 2 + 1) * D], [x[:, j, s * P:(s + 1) * P] for x in xg],
                                         [x[:, j, :] for x in wv], j == 0, j == KD - 1)
                    mm.then_inc(v_ready, 1)

            def attend(G):
                par = G % 2
                pe.wait_ge(q_copied, G * KD + KD)
                pe.wait_ge(k_copied, G * KD + KD)
                if G > 0:
                    pe.wait_ge(added, G * GS)
                for s in range(GS):
                    for k in range(KD):
                        t = slice(s * P, (s + 1) * P)
                        mm = pe.matmul(S[:, t], q_t[:, par, k, t], k_t[:, par, k, t], start=(k == 0), stop=(k == KD - 1))
                mm.then_inc(s_ready, 1)
                pe.wait_ge(exp_ready, G + 1)
                for s in range(GS):
                    tr = pe.transpose(PT[:, s * P:(s + 1) * P], prob[:, s, :], ident[:, :])
                tr.then_inc(pt_ready, 1)
                pe.wait_ge(pt_copied, G + 1)
                pe.wait_ge(v_copied, 2 * G + 2)
                for s in range(GS):
                    mm = pe.matmul(O[s // 2][:, (s % 2) * D:(s % 2 + 1) * D], prob_t[:, s, :], v[:, par, s, :],
                                   start=True, stop=True)
                mm.then_inc(o_ready, 1)
            project(0)
            for G in range(GROUPS):
                if G < GROUPS - 1:
                    project(G + 1)
                attend(G)

        @block.scalar
        def _(act):
            def project(G):
                par = G % 2
                for k in range(KD):
                    act.wait_ge(tr_ready, G * KD + k + 1)
                    act.activation(xg[HI][:, k, :], TRV[k][:, :], ACT.Copy).then_inc(xh_ready, 1)
                for k in range(KD):
                    act.wait_ge(q_ready, G * KD + k + 1)
                    act.activation(q_t[:, par, k, :], Q[k][:, :], ACT.Copy, scale=D ** -0.5).then_inc(q_copied, 1)
                for h in range(2):
                    act.wait_ge(v_ready, G * 2 + h + 1)
                    act.activation(v[:, par, 2 * h:2 * h + 2, :], TRV[h][:, :].rearrange("p (s d) -> p s d", s=2),
                                   ACT.Copy).then_inc(v_copied, 1)

            def attend(G):
                act.wait_ge(max_ready, G + 1)
                for s in range(GS):
                    e = act.activation(prob[:, s, :], S[:, s * P:(s + 1) * P], ACT.Exp, bias=neg_max[:, s:s + 1],
                                       accum_out=total[:, s:s + 1])
                e.then_inc(exp_ready, 1)
            project(0)
            for G in range(GROUPS):
                if G < GROUPS - 1:
                    project(G + 1)
                attend(G)

        @block.vector
        def _(dve):
            def project(G):
                par = G % 2
                rows = lambda i: X[:, G * GS + i, :]
                norm_measure(dve, norm, G, rows)
                if G > 0:
                    dve.wait_ge(tr_ready, G * KD)
                norm_apply(dve, norm, G, rows, lambda i: z[:, i, :])
                for k in range(KD):
                    dve.wait_ge(xh_ready, G * KD + k + 1)
                    dve.tensor_tensor(xg[LO][:, k, :], TRV[k][:, :], xg[HI][:, k, :].bitcast(F32),
                                      ALU.subtract).then_inc(xl_ready, 1)
                for k in range(KD):
                    dve.wait_ge(k_ready, G * KD + k + 1)
                    dve.tensor_copy(k_t[:, par, k, :], K[k][:, :]).then_inc(k_copied, 1)

            def attend(G):
                par = G % 2
                dve.wait_ge(s_ready, G + 1)
                dve.tensor_reduce(neg_max[:, :], S[:, :].rearrange("p (s k) -> p s k", s=GS), AX.X, ALU.max,
                                  negate=True).then_inc(max_ready, 1)
                dve.wait_ge(pt_ready, G + 1)
                dve.tensor_copy(prob_t[:, :, :], PT[:, :].rearrange("p (s k) -> p s k", s=GS)).then_inc(pt_copied, 1)
                dve.reciprocal(inv[:, :], total[:, :]).then_inc(inv_ready, 1)
                dve.wait_ge(inv_ready, G + 1)
                dve.wait_ge(o_ready, G + 1)
                for s in range(GS):
                    b = G * GS + s
                    dve.scalar_tensor_tensor(out=X[:, b, :], in0=O[s // 2][:, (s % 2) * D:(s % 2 + 1) * D],
                                             scalar=inv[:, s:s + 1], in1=X[:, b, :], op0=ALU.mult,
                                             op1=ALU.add).then_inc(added, 1)
            project(0)
            for G in range(GROUPS):
                if G < GROUPS - 1:
                    project(G + 1)
                attend(G)


def stage_wide_cross_attention(nc, ctx, io, mem):
    X, ident, neghalf, psum = mem["x"], mem["ident"], mem["neghalf"], mem["psum"]
    sb = lambda name, shape, dt=F32: ctx.enter_context(nc.sbuf_tensor("c_" + name, shape, dt))
    sem = lambda name: mem["sems"]("c_" + name)
    norm_x, norm_q = norm_state(nc, ctx, mem, "cx", GS), norm_state(nc, ctx, mem, "cq", GS)
    norm_c, norm_o = norm_state(nc, ctx, mem, "cc", GS), norm_state(nc, ctx, mem, "co", GS)
    context = sb("context", [P, 2, GS, D])
    gains = sb("gains", [P, 4, KD])
    scaled = sb("scaled", [P, 2, KD])
    factor, inv_factor = sb("factor", [P, 1]), sb("inv_factor", [P, 1])
    rows = sb("rows", [P, 4, D])
    z1, z2, cn = sb("z1", [P, GS, D]), sb("z2", [P, GS, D]), sb("cn", [P, GS, D])
    q_t, k_t = sb("q_t", [P, 2, KD, GT]), sb("k_t", [P, 2, KD, GT])
    v = sb("v", [P, 2, GS, D])
    vg = sb("vg", [P, GS, D])
    prob, prob_t = sb("prob", [P, GS, P]), sb("prob_t", [P, GS, P])
    neg_max, total, inv = sb("neg_max", [P, GS]), sb("total", [P, GS]), sb("inv", [P, GS])
    o, oz, og, ob = (sb(n, [P, GS, D]) for n in ("o", "oz", "og", "ob"))

    c_loaded = [sem(f"c_loaded{i}") for i in range(2)]
    p_loaded = sem("p_loaded")
    inv_ready_f, scaled_ready = sem("inv_factor_ready"), sem("scaled_ready")
    qtr_ready, ktr_ready = sem("qtr_ready"), sem("ktr_ready")
    q_ready, k_ready, vg_ready, v_ready = sem("q_ready"), sem("k_ready"), sem("vg_ready"), sem("v_ready")
    s_ready, max_ready, exp_ready = sem("s_ready"), sem("max_ready"), sem("exp_ready")
    pt_ready, pt_copied = sem("pt_ready"), sem("pt_copied")
    o_ready, inv_ready, o_scaled = sem("o_ready"), sem("inv_ready"), sem("o_scaled")
    og_ready, ob_ready, x_ready = sem("og_ready"), sem("ob_ready"), sem("x_ready")
    QT, KT, S, PT, O = psum[0:2], psum[2:4], psum[4], psum[5], psum[6:8]
    wide = lambda i: rows[:, i, :].unsqueeze(1).broadcast_to([P, GS, D])

    with nc.Block() as block:
        @block.sync
        def _(sp):
            sp.dma_start(gains[:, :, :], io["qk_gains_laid"]).then_inc(p_loaded, 16)
            sp.dma_start(factor[:, :], io["L1_xattn_inv_scale_factor"].broadcast_to([P, 1])).then_inc(p_loaded, 16)
            for i, name in enumerate(("ln3_w", "ln3_b", "ln4_w", "ln4_b")):
                sp.dma_start(rows[:, i, :], io["L1_xattn_" + name].unsqueeze(0).broadcast_to([P, D])).then_inc(p_loaded, 16)
            for G in range(GROUPS):
                if G >= 2:
                    sp.wait_ge(norm_c["z_ready"], (G - 1) * GS)
                sp.dma_start(context[:, G % 2, :, :], io["ctx_1024"][G * GS:(G + 1) * GS].rearrange(
                    "b t d -> t b d")).then_inc(c_loaded[G % 2], 16)

        @block.gpsimd
        def _(pool):
            def prepare(G):
                norm_invert(pool, norm_c, G)
                norm_invert(pool, norm_x, G)
                norm_invert(pool, norm_q, G)
                pool.wait_ge(norm_c["z_ready"], G * GS + GS)
                pool.tensor_tensor(vg[:, :, :], cn[:, :, :], wide(0), ALU.mult).then_inc(vg_ready, 1)
                pool.wait_ge(vg_ready, G + 1)
                if G >= 2:
                    pool.wait_ge(o_ready, G - 1)
                pool.tensor_tensor(v[:, G % 2, :, :], vg[:, :, :], wide(1), ALU.add).then_inc(v_ready, 1)

            def finish(G):
                norm_invert(pool, norm_o, G)
                pool.wait_ge(norm_o["z_ready"], G * GS + GS)
                pool.tensor_tensor(og[:, :, :], oz[:, :, :], wide(2), ALU.mult).then_inc(og_ready, 1)
                pool.wait_ge(og_ready, G + 1)
                pool.tensor_tensor(ob[:, :, :], og[:, :, :], wide(3), ALU.add).then_inc(ob_ready, 1)
                pool.wait_ge(ob_ready, G + 1)
                xg = X[:, G * GS:(G + 1) * GS, :]
                pool.tensor_tensor(xg, xg, ob[:, :, :], ALU.add).then_inc(x_ready, 1)
            pool.wait_ge(p_loaded, 96)
            prepare(0)
            for G in range(GROUPS):
                if G < GROUPS - 1:
                    prepare(G + 1)
                finish(G)

        @block.tensor
        def _(pe):
            def turn(G):
                pe.wait_ge(norm_c["z_ready"], G * GS + GS)
                if G > 0:
                    pe.wait_ge(k_ready, G * KD)
                for k in range(KD):
                    for s in range(GS):
                        tr = pe.transpose(KT[k][:, s * P:(s + 1) * P], cn[:, s, k * P:(k + 1) * P], ident[:, :])
                    tr.then_inc(ktr_ready, 1)
                pe.wait_ge(norm_q["z_ready"], G * GS + GS)
                if G > 0:
                    pe.wait_ge(q_ready, G * KD)
                for k in range(KD):
                    for s in range(GS):
                        tr = pe.transpose(QT[k][:, s * P:(s + 1) * P], z2[:, s, k * P:(k + 1) * P], ident[:, :])
                    tr.then_inc(qtr_ready, 1)

            def attend(G):
                par = G % 2
                pe.wait_ge(q_ready, G * KD + KD)
                pe.wait_ge(k_ready, G * KD + KD)
                if G > 0:
                    pe.wait_ge(exp_ready, G)
                for s in range(GS):
                    for k in range(KD):
                        t = slice(s * P, (s + 1) * P)
                        mm = pe.matmul(S[:, t], q_t[:, par, k, t], k_t[:, par, k, t], start=(k == 0), stop=(k == KD - 1))
                mm.then_inc(s_ready, 1)
                pe.wait_ge(exp_ready, G + 1)
                if G > 0:
                    pe.wait_ge(pt_copied, G)
                for s in range(GS):
                    tr = pe.transpose(PT[:, s * P:(s + 1) * P], prob[:, s, :], ident[:, :])
                tr.then_inc(pt_ready, 1)
                pe.wait_ge(pt_copied, G + 1)
                pe.wait_ge(v_ready, G + 1)
                if G > 0:
                    pe.wait_ge(o_scaled, 2 * G)
                for s in range(GS):
                    mm = pe.matmul(O[s // 2][:, (s % 2) * D:(s % 2 + 1) * D], prob_t[:, s, :], v[:, par, s, :],
                                   start=True, stop=True)
                mm.then_inc(o_ready, 1)
            turn(0)
            for G in range(GROUPS):
                if G < GROUPS - 1:
                    turn(G + 1)
                attend(G)

        @block.scalar
        def _(act):
            def prepare(G):
                par = G % 2
                if G >= 2:
                    act.wait_ge(s_ready, G - 1)
                for k in range(KD):
                    act.wait_ge(ktr_ready, G * KD + k + 1)
                    act.activation(k_t[:, par, k, :], KT[k][:, :], ACT.Identity, bias=gains[:, 3, k:k + 1],
                                   scale=gains[:, 2, k:k + 1]).then_inc(k_ready, 1)
                for k in range(KD):
                    act.wait_ge(qtr_ready, G * KD + k + 1)
                    act.activation(q_t[:, par, k, :], QT[k][:, :], ACT.Identity, bias=scaled[:, 1, k:k + 1],
                                   scale=scaled[:, 0, k:k + 1]).then_inc(q_ready, 1)

            def attend(G):
                act.wait_ge(max_ready, G + 1)
                for s in range(GS):
                    e = act.activation(prob[:, s, :], S[:, s * P:(s + 1) * P], ACT.Exp, bias=neg_max[:, s:s + 1],
                                       accum_out=total[:, s:s + 1])
                e.then_inc(exp_ready, 1)
            act.wait_ge(scaled_ready, 1)
            prepare(0)
            for G in range(GROUPS):
                if G < GROUPS - 1:
                    prepare(G + 1)
                attend(G)

        @block.vector
        def _(dve):
            def prepare(G):
                dve.wait_ge(c_loaded[G % 2], 16 * (G // 2) + 16)
                crow = lambda i: context[:, G % 2, i, :]
                xrow = lambda i: X[:, G * GS + i, :]
                norm_measure(dve, norm_c, G, crow)
                norm_measure(dve, norm_x, G, xrow)
                if G > 0:
                    dve.wait_ge(ktr_ready, G * KD)
                    dve.wait_ge(vg_ready, G)
                norm_apply(dve, norm_c, G, crow, lambda i: cn[:, i, :])
                norm_apply(dve, norm_x, G, xrow, lambda i: z1[:, i, :])
                dve.wait_ge(norm_x["z_ready"], G * GS + GS)
                norm_measure(dve, norm_q, G, lambda i: z1[:, i, :])
                if G > 0:
                    dve.wait_ge(qtr_ready, G * KD)
                norm_apply(dve, norm_q, G, lambda i: z1[:, i, :], lambda i: z2[:, i, :])

            def attend(G):
                dve.wait_ge(s_ready, G + 1)
                dve.tensor_reduce(neg_max[:, :], S[:, :].rearrange("p (s k) -> p s k", s=GS), AX.X, ALU.max,
                                  negate=True).then_inc(max_ready, 1)
                dve.wait_ge(pt_ready, G + 1)
                dve.tensor_copy(prob_t[:, :, :], PT[:, :].rearrange("p (s k) -> p s k", s=GS)).then_inc(pt_copied, 1)
                dve.reciprocal(inv[:, :], total[:, :]).then_inc(inv_ready, 1)
                dve.wait_ge(inv_ready, G + 1)
                dve.wait_ge(o_ready, G + 1)
                for h in range(2):
                    dve.tensor_tensor(o[:, 2 * h:2 * h + 2, :], O[h][:, :].rearrange("p (s d) -> p s d", s=2),
                                      inv[:, 2 * h:2 * h + 2].unsqueeze(2).broadcast_to([P, 2, D]),
                                      ALU.mult).then_inc(o_scaled, 1)
                dve.wait_ge(o_scaled, 2 * G + 2)
                orow = lambda i: o[:, i, :]
                norm_measure(dve, norm_o, G, orow)
                if G > 0:
                    dve.wait_ge(og_ready, G)
                norm_apply(dve, norm_o, G, orow, lambda i: oz[:, i, :])
            dve.wait_ge(p_loaded, 96)
            dve.reciprocal(inv_factor[:, :], factor[:, :]).then_inc(inv_ready_f, 1)
            dve.wait_ge(inv_ready_f, 1)
            dve.tensor_scalar(scaled[:, :, :], gains[:, 0:2, :], inv_factor[:, 0:1], None, ALU.mult).then_inc(scaled_ready, 1)
            prepare(0)
            for G in range(GROUPS):
                if G < GROUPS - 1:
                    prepare(G + 1)
                attend(G)


MAGIC = 1.5 * 2.0 ** 23
INT8_MAX = 127.0


def stage_quantised(nc, ctx, io, mem, out):
    X, ident_bf, neghalf, psum = mem["x"], mem["ident_bf"], mem["neghalf"], mem["psum"]
    sb = lambda name, shape, dt=F32: ctx.enter_context(nc.sbuf_tensor("f_" + name, shape, dt))
    sem = lambda name: mem["sems"]("f_" + name)
    norm = norm_state(nc, ctx, mem, "fn", GS)
    z, t1, t2 = (sb(n, [P, GS, D]) for n in ("z", "t1", "t2"))
    zq = sb("zq", [P, GS, D], BF16)
    xq_t = sb("xq_t", [P, 2, GS * KD, P], BF16)
    amax, scale, inv = (sb(n, [P, 2, GS]) for n in ("amax", "scale", "inv"))
    scaled = sb("scaled", [P, 2, GS, D])
    w, wt1, wt2 = (sb(n, [P, KD, D]) for n in ("w", "wt1", "wt2"))
    wq = sb("wq", [P, KD, D], BF16)
    wq_t = sb("wq_t", [P, KD, D], BF16)
    w_amax, w_scale, w_inv = (sb(n, [P, KD]) for n in ("w_amax", "w_scale", "w_inv"))
    ones = sb("ones", [P, P])
    diag = sb("diag", [P, KD, P])
    col_scale = sb("col_scale", [P, D])

    w_loaded, ones_ready, w_step = sem("w_loaded"), sem("ones_ready"), sem("w_step")
    wtr_ready, wt_ready, cs_mm, cs_ready = sem("wtr_ready"), sem("wt_ready"), sem("cs_mm"), sem("cs_ready")
    q_step, scale_ready, q_ready = sem("q_step"), sem("scale_ready"), sem("q_ready")
    tr_ready, tr_copied, y_ready, y_scaled, x_ready = (sem(n) for n in (
        "tr_ready", "tr_copied", "y_ready", "y_scaled", "x_ready"))
    stored = sem("stored")
    TR = (psum[0], psum[1])
    Y = lambda G: (psum[2 + 2 * (G % 2)], psum[3 + 2 * (G % 2)])
    WT, CS = psum[6], psum[7]

    with nc.Block() as block:
        @block.sync
        def _(sp):
            sp.dma_start(w[:, :, :], io["rhs_laid"]).then_inc(w_loaded, 16)
            for G in range(GROUPS):
                sp.wait_ge(x_ready, G + 1)
                sp.dma_start(out[G * GS:(G + 1) * GS].rearrange("b t d -> t b d"),
                             X[:, G * GS:(G + 1) * GS, :]).then_inc(stored, 16)
            sp.wait_ge(stored, 16 * GROUPS)

        @block.gpsimd
        def _(pool):
            pool.memset(ones[:, :], 1.0).then_inc(ones_ready, 1)
            norm_invert(pool, norm, 0)
            for G in range(GROUPS):
                if G < GROUPS - 1:
                    norm_invert(pool, norm, G + 1)
                pool.wait_ge(y_scaled, (G + 1) * GS)
                xg = X[:, G * GS:(G + 1) * GS, :]
                pool.tensor_tensor(xg, xg, scaled[:, G % 2, :, :], ALU.add).then_inc(x_ready, 1)

        @block.vector
        def _(dve):
            count = [0]

            def then(op, step):
                count[0] += 1
                op.then_inc(step, 1)
                dve.wait_ge(step, count[0])

            dve.wait_ge(w_loaded, 16)
            then(dve.tensor_reduce(w_amax[:, :], w[:, :, :], AX.X, ALU.max, apply_absolute_value=True), w_step)
            then(dve.tensor_scalar(w_scale[:, :], w_amax[:, :], 1e-12, 1.0 / INT8_MAX, ALU.max, ALU.mult), w_step)
            then(dve.reciprocal(w_inv[:, :], w_scale[:, :]), w_step)
            for c in range(KD):
                then(dve.tensor_scalar(wt1[:, c, :], w[:, c, :], w_inv[:, c:c + 1], MAGIC, ALU.mult, ALU.add), w_step)
            then(dve.tensor_scalar(wt2[:, :, :], wt1[:, :, :], -MAGIC, INT8_MAX, ALU.add, ALU.min), w_step)
            then(dve.tensor_scalar(wq[:, :, :], wt2[:, :, :], -INT8_MAX, None, ALU.max), w_step)
            for c in range(KD):
                then(dve.tensor_scalar(diag[:, c, :], mem["ident"][:, :], w_scale[:, c:c + 1], None, ALU.mult), w_step)

            def quantise(G):
                par = G % 2
                rows = lambda i: X[:, G * GS + i, :]
                norm_measure(dve, norm, G, rows)
                norm_apply(dve, norm, G, rows, lambda i: z[:, i, :])
                dve.wait_ge(norm["z_ready"], G * GS + GS)
                base = G * (3 + GS)
                dve.tensor_reduce(amax[:, par, :], z[:, :, :], AX.X, ALU.max, apply_absolute_value=True).then_inc(q_step, 1)
                dve.wait_ge(q_step, base + 1)
                dve.tensor_scalar(scale[:, par, :], amax[:, par, :], 1e-12, 1.0 / INT8_MAX, ALU.max, ALU.mult).then_inc(q_step, 1)
                dve.wait_ge(q_step, base + 2)
                dve.reciprocal(inv[:, par, :], scale[:, par, :]).then_inc(q_step, 1)
                dve.wait_ge(q_step, base + 3)
                for i in range(GS):
                    dve.tensor_scalar(t1[:, i, :], z[:, i, :], inv[:, par, i:i + 1], MAGIC, ALU.mult, ALU.add).then_inc(q_step, 1)
                dve.wait_ge(q_step, base + 3 + GS)
                dve.tensor_scalar(t2[:, :, :], t1[:, :, :], -MAGIC, INT8_MAX, ALU.add, ALU.min).then_inc(scale_ready, 1)
                dve.wait_ge(scale_ready, G + 1)
                if G > 0:
                    dve.wait_ge(tr_ready, G)
                dve.tensor_scalar(zq[:, :, :], t2[:, :, :], -INT8_MAX, None, ALU.max).then_inc(q_ready, 1)

            def scale_out(G):
                dve.wait_ge(y_ready, G + 1)
                if G >= 2:
                    dve.wait_ge(x_ready, G - 1)
                for s in range(GS):
                    dve.scalar_tensor_tensor(out=scaled[:, G % 2, s, :], in0=Y(G)[s // 2][:, (s % 2) * D:(s % 2 + 1) * D],
                                             scalar=scale[:, G % 2, s:s + 1], in1=col_scale[:, :], op0=ALU.mult,
                                             op1=ALU.mult).then_inc(y_scaled, 1)
            quantise(0)
            dve.wait_ge(cs_ready, 1)
            for G in range(GROUPS):
                if G < GROUPS - 1:
                    quantise(G + 1)
                scale_out(G)

        @block.tensor
        def _(pe):
            pe.wait_ge(w_step, 5 + 2)
            for c in range(KD):
                for k in range(KD):
                    tr = pe.transpose(WT[:, :].bitcast(BF16)[:, k * D + c * P:k * D + (c + 1) * P],
                                      wq[:, c, k * P:(k + 1) * P], ident_bf[:, :])
            tr.then_inc(wtr_ready, 1)
            pe.wait_ge(ones_ready, 1)
            pe.wait_ge(w_step, 5 + 2 + KD)
            for c in range(KD):
                mm = pe.matmul(CS[:, c * P:(c + 1) * P], ones[:, :], diag[:, c, :], start=True, stop=True)
            mm.then_inc(cs_mm, 1)

            def turn(G):
                pe.wait_ge(q_ready, G + 1)
                if G >= 2:
                    pe.wait_ge(tr_copied, G - 1)
                for s in range(GS):
                    for k in range(KD):
                        i = s * KD + k
                        tr = pe.transpose(TR[G % 2][:, :].bitcast(BF16)[:, i * P:(i + 1) * P], zq[:, s, k * P:(k + 1) * P],
                                          ident_bf[:, :])
                tr.then_inc(tr_ready, 1)

            def multiply(G):
                pe.wait_ge(tr_copied, G + 1)
                if G >= 2:
                    pe.wait_ge(y_scaled, (G - 1) * GS)
                for s in range(GS):
                    for k in range(KD):
                        mm = pe.matmul(Y(G)[s // 2][:, (s % 2) * D:(s % 2 + 1) * D], xq_t[:, G % 2, s * KD + k, :],
                                       wq_t[:, k, :], start=(k == 0), stop=(k == KD - 1))
                mm.then_inc(y_ready, 1)
            turn(0)
            pe.wait_ge(wt_ready, 1)
            for G in range(GROUPS):
                if G < GROUPS - 1:
                    turn(G + 1)
                multiply(G)

        @block.scalar
        def _(act):
            act.wait_ge(wtr_ready, 1)
            act.activation(wq_t[:, :, :], WT[:, :].bitcast(BF16)[:, 0:KD * D].rearrange("p (k n) -> p k n", k=KD),
                           ACT.Copy).then_inc(wt_ready, 1)
            act.wait_ge(cs_mm, 1)
            act.activation(col_scale[:, :], CS[:, 0:D], ACT.Copy).then_inc(cs_ready, 1)
            for G in range(GROUPS):
                act.wait_ge(tr_ready, G + 1)
                if G >= 2:
                    act.wait_ge(y_ready, G - 1)
                act.activation(xq_t[:, G % 2, :, :], TR[G % 2][:, :].bitcast(BF16).rearrange("p (i t) -> p i t", t=P),
                               ACT.Copy).then_inc(tr_copied, 1)


def clear_semaphores(nc, handles):
    with nc.Block() as block:
        @block.gpsimd
        def _(pool):
            for handle in handles:
                pool.sem_clear(handle)


def decoder(nc, io, out):
    ctx = ExitStack()
    with ctx:
        sb = lambda name, shape, dt=F32: ctx.enter_context(nc.sbuf_tensor(name, shape, dt))
        sem = lambda name: ctx.enter_context(nc.semaphore(name))

        mem = {"psum": [ctx.enter_context(nc.psum_tensor(f"bank{i}", [P, BANK], F32)) for i in range(8)]}
        mem["sems"] = sem
        mem["x"] = sb("x_res", [P, SEQS, D])
        mem["ident"] = sb("ident", [P, P])
        mem["ident_bf"] = sb("ident_bf", [P, P], BF16)
        mem["causal"] = sb("causal", [P, P], BF16)
        mem["neghalf"] = sb("neghalf", [P, SEQS])
        mem["stats"] = sb("stats", [P, SEQS, 6])
        mem["mv"] = sb("mv", [P, SEQS, 2])
        mem["ve"] = sb("ve", [P, SEQS])
        attn_ctx = ExitStack()
        asb = lambda name, shape, dt=F32: attn_ctx.enter_context(nc.sbuf_tensor(name, shape, dt))
        mem["act"] = asb("act", [P, SEQS, D])
        mem["act_t"] = asb("act_t", [P, KD, SEQS * P])
        mem["attn_w"] = (asb("attn_w_hi", [P, 4, KD * WIDE], F32R), asb("attn_w_lo", [P, 4, KD * WIDE], F32R))
        mem["attn_g"], mem["attn_b"] = asb("attn_g", [P, D]), asb("attn_b", [P, D])
        for name in ("attn_w_loaded", "attn_w_split", "attn_ln_loaded"):
            mem[name] = sem(name)
        with ExitStack() as ssm_ctx:
            mem["attn_raw"] = ssm_ctx.enter_context(nc.sbuf_tensor("attn_raw", [P, KD * WIDE], F32))
            ssb = lambda name, shape: ssm_ctx.enter_context(nc.sbuf_tensor(name, shape, F32))
            w_in = mem["w_in"] = ssb("w_in", [P, KD, PROJ])
            w_out = mem["w_out"] = ssb("w_out", [P, KI, D])
            conv_w = mem["conv_w"] = ssb("conv_w", [P, KI, TAPS])
            conv_b = mem["conv_b"] = ssb("conv_b", [P, KI])
            ln_g = mem["ln_g"] = ssb("ln_g", [P, D])
            ln_b = mem["ln_b"] = ssb("ln_b", [P, D])
            decay = mem["decay"] = ssb("decay", [P, P])
            names = mem["ssm_sems"] = {k: sem("s_" + k) for k in (
                "w_in_loaded", "w_out_loaded", "conv_loaded", "ln_loaded", "decay_loaded")}

            def one(ap, layer):
                return ap[layer] if isinstance(layer, int) else ap[bass.ds(layer, 1)]

            def load_w_in(sp, layer):
                sp.dma_start(w_in[:, :, :], io["L0_attn_in_proj_w"][bass.ds(layer, 1)].rearrange(
                    "l (k p) n -> p (l k) n", p=P)).then_inc(names["w_in_loaded"], 16)

            def load_w_out(sp, layer):
                sp.dma_start(w_out[:, :, :], io["L0_attn_out_proj_w"][bass.ds(layer, 1)].rearrange(
                    "l (k p) n -> p (l k) n", p=P)).then_inc(names["w_out_loaded"], 16)

            def load_conv(sp, layer):
                sp.dma_start(conv_w[:, :, :], io["conv_w_laid"][bass.ds(layer, 1)].rearrange(
                    "l p c t -> p (l c) t")).then_inc(names["conv_loaded"], 16)
                sp.dma_start(conv_b[:, :], io["conv_b_laid"][bass.ds(layer, 1)].rearrange(
                    "l p c -> p (l c)")).then_inc(names["conv_loaded"], 16)

            def load_ln(sp, layer):
                for tile, name in ((ln_g, "L0_attn_ssm_ln_g"), (ln_b, "L0_attn_ssm_ln_b")):
                    sp.dma_start(tile[:, :], io[name][bass.ds(layer, 1), :].broadcast_to([P, D])).then_inc(
                        names["ln_loaded"], 16)

            def prefetch_ssm(sp):
                load_w_in(sp, 0)
                load_conv(sp, 0)
                sp.dma_start(decay[:, :], io["decay"]).then_inc(names["decay_loaded"], 16)
                load_w_out(sp, 0)
                load_ln(sp, 0)
            mem.update(load_w_in=load_w_in, load_w_out=load_w_out, load_conv=load_conv, load_ln=load_ln,
                       prefetch_ssm=prefetch_ssm, prefetch_attn=lambda sp: None)
            stage_load_and_norm(nc, ctx, io, mem)
            stage_ssm(nc, ssm_ctx, io, mem)
        with attn_ctx:
            stage_self_attention(nc, attn_ctx, io, mem)
        for stage in (stage_cross_attention, stage_experts, stage_wide_attention,
                      stage_wide_cross_attention):
            with ExitStack() as stage_ctx:
                handles = []

                def stage_sem(name):
                    handles.append(stage_ctx.enter_context(nc.semaphore(name)))
                    return handles[-1]
                mem["sems"] = stage_sem
                stage(nc, stage_ctx, io, mem)
                clear_semaphores(nc, handles)
        with ExitStack() as stage_ctx:
            mem["sems"] = lambda name: stage_ctx.enter_context(nc.semaphore(name))
            stage_quantised(nc, stage_ctx, io, mem, out)


def kernel(**inputs):
    import numpy as np
    import concourse.bacc as bacc
    from concourse.bass_utils import run_bass_kernel_spmd

    nc = bacc.Bacc("TRN2", target_bir_lowering=False, num_devices=1)
    laid = {name: np.ascontiguousarray(a) for name, a in inputs.items()}
    laid["conv_w_laid"] = np.ascontiguousarray(laid.pop("L0_attn_conv_w").reshape(SSM_LAYERS, KI, P, TAPS).transpose(0, 2, 1, 3))
    laid["conv_b_laid"] = np.ascontiguousarray(laid.pop("L0_attn_conv_b").reshape(SSM_LAYERS, KI, P).transpose(0, 2, 1))
    laid["attn_w_laid"] = np.stack([laid.pop(f"L0_attn_{w}").reshape(k, P, -1).transpose(1, 0, 2).reshape(P, -1)
                                    for w, k in (("wq", KD), ("wk", KD), ("wv", KD), ("wo", KW))])
    feature_rows = lambda a: a.reshape(-1, P, a.shape[-1]).transpose(1, 0, 2).reshape(P, -1)
    for name in ("W_q", "W_k", "W_v", "W_o"):
        laid[f"L0_xattn_{name}_laid"] = np.ascontiguousarray(feature_rows(laid.pop("L0_xattn_" + name).T))
    for name in ("b_q", "b_k"):
        laid[f"L0_xattn_{name}_laid"] = np.ascontiguousarray(laid.pop("L0_xattn_" + name).reshape(KD, P).T)
    laid["router_laid"] = np.ascontiguousarray(feature_rows(laid.pop("L0_ffn_router_kernel_DE")))
    laid["experts_laid"] = np.stack([np.concatenate(
        [feature_rows(laid[f"L0_ffn_kernel_{w}"][e]) for w in ("gating_EDF", "up_EDF", "down_EFD")], axis=1)
        for e in range(EXPERTS)])
    for w in ("gating_EDF", "up_EDF", "down_EFD"):
        del laid[f"L0_ffn_kernel_{w}"]
    for name in ("Wq", "Wk", "Wv"):
        laid[f"L1_attn_{name}_laid"] = np.ascontiguousarray(feature_rows(laid.pop("L1_attn_" + name).T))
    laid["qk_gains_laid"] = np.ascontiguousarray(np.stack(
        [laid.pop("L1_xattn_" + name).reshape(KD, P).T for name in ("ln1_w", "ln1_b", "ln2_w", "ln2_b")], axis=1))
    laid["rhs_laid"] = np.ascontiguousarray(laid.pop("L1_ffn_rhs").T.reshape(KD, P, D).transpose(1, 0, 2))
    laid["ctx_t_laid"] = np.ascontiguousarray(laid["ctx_1024"].reshape(SEQS * P, KD, P).transpose(2, 1, 0))
    steps = np.arange(P)[None, :] - np.arange(P)[:, None]
    laid["decay"] = np.where(steps >= 0, np.float64(-0.5) ** np.maximum(steps, 0), 0.0).astype(np.float32)
    io = {name: nc.dram_tensor(f"in_{name}", a.shape, mybir.dt.from_np(a.dtype), kind="ExternalInput").ap()
          for name, a in laid.items()}
    out = nc.dram_tensor("out_x", (SEQS, P, D), F32, kind="ExternalOutput").ap()
    decoder(nc, io, out)
    ran = run_bass_kernel_spmd(nc, [{f"in_{name}": a for name, a in laid.items()}], core_ids=[0])
    return ran.results[0]["out_x"]
```

```python
from contextlib import ExitStack

import concourse.bass as bass
from concourse import mybir

F32 = mybir.dt.float32
F32R = mybir.dt.float32r
BF16 = mybir.dt.bfloat16
I32 = mybir.dt.int32
ALU = mybir.AluOpType
ACT = mybir.ActivationFunctionType
AX = mybir.AxisListType

P = 128
SEQS = 16
D = 256
KD = D // P
GS = 4
GROUPS = SEQS // GS
GT = GS * P
INNER = 512
KI = INNER // P
STATE = 64
PROJ = INNER + 2 * STATE
TAPS = 4
SSM_LAYERS = 5
EPS = 1e-5
BANK = 512
HI, LO = 0, 1


def stage_load_and_norm(nc, ctx, io, mem):
    X, ACTV, ACT_T, ident, neghalf = mem["x"], mem["act"], mem["act_t"], mem["ident"], mem["neghalf"]
    sem = lambda name: mem["sems"](name)
    x_loaded = [sem(f"n0_x_loaded{g}") for g in range(GROUPS)]
    const_step = sem("n0_const_step")
    consts_ready = sem("n0_consts_ready")
    stats_ready = sem("n0_stats_ready")
    aggr_ready = sem("n0_aggr_ready")
    var_ready = sem("n0_var_ready")
    rstd_ready = sem("n0_rstd_ready")
    normed = sem("n0_normed")
    tr_ready = sem("n0_tr_ready")
    tr_copied = sem("n0_tr_copied")
    psum, stats, mv, ve = mem["psum"], mem["stats"], mem["mv"], mem["ve"]

    with nc.Block() as block:
        @block.sync
        def _(sp):
            for g in range(GROUPS):
                sp.dma_start(X[:, GS * g:GS * g + GS, :],
                             io["x"][GS * g:GS * g + GS].rearrange("b t d -> t b d")).then_inc(x_loaded[g], 16)
            mem["prefetch_ssm"](sp)

        @block.gpsimd
        def _(pool):
            pool.memset(ident[:, :], 0.0).then_inc(const_step, 1)
            pool.memset(mem["ident_bf"][:, :], 0.0).then_inc(const_step, 1)
            pool.memset(mem["causal"][:, :], 0.0).then_inc(const_step, 1)
            pool.memset(neghalf[:, :], -0.5).then_inc(consts_ready, 1)
            pool.wait_ge(const_step, 3)
            for t in (ident, mem["ident_bf"]):
                pool.affine_select(out=t[:, :], in_=t[:, :], compare_op=ALU.not_equal, fill=1.0, base=0,
                                   pattern=[[-1, P]], channel_multiplier=1).then_inc(consts_ready, 1)
            pool.affine_select(out=mem["causal"][:, :], in_=mem["causal"][:, :], compare_op=ALU.is_ge,
                               fill=-1e30, base=0, pattern=[[-1, P]], channel_multiplier=1).then_inc(consts_ready, 1)
            pool.wait_ge(consts_ready, 4)
            for g in range(GROUPS):
                pool.wait_ge(var_ready, g + 1)
                pool.tensor_tensor(ve[:, GS * g:GS * g + GS], ve[:, GS * g:GS * g + GS],
                                   neghalf[:, 0:GS], ALU.pow).then_inc(rstd_ready, 1)

        @block.vector
        def _(dve):
            for g in range(GROUPS):
                dve.wait_ge(x_loaded[g], 16)
                for b in range(GS * g, GS * g + GS):
                    dve.bn_stats(stats[:, b, :], X[:, b, :]).then_inc(stats_ready, 1)
                dve.wait_ge(stats_ready, GS * (g + 1))
                for b in range(GS * g, GS * g + GS):
                    dve.bn_aggr(mv[:, b, :], stats[:, b, :]).then_inc(aggr_ready, 1)
                dve.wait_ge(aggr_ready, GS * (g + 1))
                dve.tensor_scalar(ve[:, GS * g:GS * g + GS], mv[:, GS * g:GS * g + GS, 1], EPS, None,
                                  ALU.add).then_inc(var_ready, 1)
            for g in range(GROUPS):
                dve.wait_ge(rstd_ready, g + 1)
                for b in range(GS * g, GS * g + GS):
                    dve.tensor_scalar(ACTV[:, b, :], X[:, b, :], mv[:, b, 0:1], ve[:, b:b + 1],
                                      ALU.subtract, ALU.mult).then_inc(normed, 1)

        @block.tensor
        def _(pe):
            pe.wait_ge(consts_ready, 4)
            for h in range(SEQS // 2):
                pe.wait_ge(normed, 2 * h + 2)
                if h >= 2:
                    pe.wait_ge(tr_copied, h - 1)
                for s in range(2):
                    for k in range(KD):
                        col = k * D + s * P
                        tr = pe.transpose(psum[6 + h % 2][:, col:col + P],
                                          ACTV[:, 2 * h + s, k * P:(k + 1) * P], ident[:, :])
                tr.then_inc(tr_ready, 1)

        @block.scalar
        def _(act):
            for h in range(SEQS // 2):
                act.wait_ge(tr_ready, h + 1)
                nc.scalar.activation(ACT_T[:, :, 2 * h * P:(2 * h + 2) * P],
                                     psum[6 + h % 2][:, :].rearrange("p (k t) -> p k t", k=KD),
                                     ACT.Copy).then_inc(tr_copied, 1)


def stage_ssm(nc, ctx, io, mem):
    ACTV, ACT_T, ident, neghalf, psum = mem["act"], mem["act_t"], mem["ident"], mem["neghalf"], mem["psum"]
    names = mem["ssm_sems"]
    w_in, w_out, conv_w, conv_b, ln_g, ln_b, decay = (mem[k] for k in (
        "w_in", "w_out", "conv_w", "conv_b", "ln_g", "ln_b", "decay"))
    sb = lambda name, shape: ctx.enter_context(nc.sbuf_tensor(name, shape, F32))
    sem = lambda name: mem["sems"]("s_" + name)
    conv = sb("ssm_conv", [P, KI, GT])
    u = sb("ssm_u", [P, 2, KI, GT])
    b_t = sb("ssm_b_t", [STATE, 2, GT])
    c_t = sb("ssm_c_t", [STATE, 2, GT])
    mix = sb("ssm_mix", [P, GS, P])
    uw = sb("ssm_uw", [P, 2, 2 * D])
    res = sb("ssm_res", [P, 2, 2 * D])
    z = sb("ssm_z", [P, 2, 2, D])
    zg = sb("ssm_zg", [P, 2, 2, D])
    stats, mv, ve = mem["stats"], mem["mv"], mem["ve"]

    bc_ready = sem("bc_ready")
    xs_ready = sem("xs_ready")
    bt_copied = sem("bt_copied")
    ct_copied = sem("ct_copied")
    tap_last = sem("tap_last")
    tap_step = sem("tap_step")
    conv_done = sem("conv_done")
    u_ready = sem("u_ready")
    g_ready = sem("g_ready")
    mix_ready = sem("mix_ready")
    uw_ready = sem("uw_ready")
    uw_copied = sem("uw_copied")
    y_ready = sem("y_ready")
    res_ready = sem("res_ready")
    stats_ready = sem("stats_ready")
    stats_seen = sem("stats_seen")
    aggr_ready = sem("aggr_ready")
    var_ready = sem("var_ready")
    rstd_ready = sem("rstd_ready")
    z_ready = sem("z_ready")
    zg_ready = sem("zg_ready")
    act_ready = sem("act_ready")
    tr_ready = sem("tr_ready")
    tr_copied = sem("tr_copied")
    attn_hi_ready = sem("attn_hi_ready")

    XS = lambda c: psum[c]
    BC, UWY, TR = psum[4], (psum[5], psum[6]), psum[7]
    LAST = SSM_LAYERS - 1

    def layers(eng, body):
        body(0)
        with eng.Fori(1, LAST) as layer:
            body(layer)
        body(LAST)

    with nc.Block() as block:
        @block.sync
        def _(sp):
            def reload(layer):
                done = layer * GROUPS * 1 + 0
                sp.wait_ge(xs_ready, layer * (GROUPS * KI) + GROUPS * KI)
                mem["load_w_in"](sp, layer + 1)
                sp.wait_ge(tap_last, layer * (GROUPS * KI) + GROUPS * KI)
                sp.wait_ge(conv_done, layer * (GROUPS * KI) + GROUPS * KI)
                mem["load_conv"](sp, layer + 1)
                sp.wait_ge(uw_ready, layer * (2 * GROUPS) + 2 * GROUPS)
                mem["load_w_out"](sp, layer + 1)
                sp.wait_ge(mem["attn_w_split"], layer * GROUPS + GROUPS)
                sp.wait_ge(act_ready, layer * (2 * GROUPS) + 2 * GROUPS)
                mem["load_ln"](sp, layer + 1)
            with sp.Fori(0, LAST) as layer:
                sp.dma_start(mem["attn_raw"][:, :], io["attn_w_laid"][bass.ds(layer, 1)].rearrange(
                    "a p n -> p (a n)")).then_inc(mem["attn_w_loaded"], 16)
                reload(layer)
            for tile, name in ((mem["attn_g"], "L0_attn_attn_ln_g"), (mem["attn_b"], "L0_attn_attn_ln_b")):
                sp.dma_start(tile[:, :], io[name].unsqueeze(0).broadcast_to([P, D])).then_inc(mem["attn_ln_loaded"], 16)

        @block.tensor
        def _(pe):
            def project(layer, g, first=False):
                n = layer * GROUPS + g
                pe.wait_ge(names["w_in_loaded"], layer * 16 + 16)
                if not first:
                    pe.wait_ge(tr_copied, n * 2 - 2 * GROUPS + 2)
                tokens = slice(g * GT, (g + 1) * GT)
                if g >= 2 or not first:
                    pe.wait_ge(mix_ready, n - 1)
                elif g == 1:
                    pe.wait_ge(bt_copied, 1)
                    pe.wait_ge(ct_copied, 1)
                for k in range(KD):
                    mm = pe.matmul(BC[:, :], w_in[:, k, INNER:PROJ], ACT_T[:, k, tokens],
                                   start=(k == 0), stop=(k == KD - 1))
                mm.then_inc(bc_ready, 1)
                for c in range(KI):
                    if g >= 1 or not first:
                        pe.wait_ge(tap_last, n * KI - KI + c + 1)
                        pe.wait_ge(conv_done, n * KI - KI + c + 1)
                    for k in range(KD):
                        mm = pe.matmul(XS(c)[:, :], w_in[:, k, c * P:(c + 1) * P], ACT_T[:, k, tokens],
                                       start=(k == 0), stop=(k == KD - 1))
                    mm.then_inc(xs_ready, 1)

            def turn(layer, g):
                n = layer * GROUPS + g
                for h in range(2):
                    pe.wait_ge(act_ready, n * 2 + h + 1)
                    if not (layer_is(layer, 0) and g == 0 and h == 0):
                        pe.wait_ge(tr_copied, n * 2 + h)
                    for s in range(2):
                        for k in range(KD):
                            tr = pe.transpose(TR[:, k * D + s * P:k * D + (s + 1) * P],
                                              ACTV[:, g * GS + 2 * h + s, k * P:(k + 1) * P], ident[:, :])
                    tr.then_inc(tr_ready, 1)

            def mix_tokens(layer, g, first=False, last=False):
                n = layer * GROUPS + g
                ahead = 1 if last else 2
                pe.wait_ge(bt_copied, n + ahead)
                pe.wait_ge(ct_copied, n + ahead)
                for s in range(GS):
                    mm = pe.matmul(BC[:, s * P:(s + 1) * P], b_t[:, g % 2, s * P:(s + 1) * P],
                                   c_t[:, g % 2, s * P:(s + 1) * P], start=True, stop=True)
                mm.then_inc(g_ready, 1)
                pe.wait_ge(u_ready, n * KI + KI)
                if g == 0:
                    pe.wait_ge(names["w_out_loaded"], layer * 16 + 16)
                for h in range(2):
                    if not (first and g == 0):
                        pe.wait_ge(res_ready, n * 2 - 1 + h)
                    for s in range(2):
                        t = (2 * h + s) * P
                        for c in range(KI):
                            mm = pe.matmul(UWY[h][:, s * D:(s + 1) * D], u[:, g % 2, c, t:t + P],
                                           w_out[:, c, :], start=(c == 0), stop=(c == KI - 1))
                    mm.then_inc(uw_ready, 1)
                pe.wait_ge(mix_ready, n + 1)
                for h in range(2):
                    pe.wait_ge(uw_copied, n * 2 + h + 1)
                    for s in range(2):
                        mm = pe.matmul(UWY[h][:, s * D:(s + 1) * D], mix[:, 2 * h + s, :],
                                       uw[:, h, s * D:(s + 1) * D], start=True, stop=True)
                    mm.then_inc(y_ready, 1)

            project(0, 0, first=True)

            def layer_steps(layer):
                first, last = layer_is(layer, 0), layer_is(layer, LAST)
                for g in range(GROUPS):
                    if g < GROUPS - 1:
                        project(layer, g + 1, first)
                    elif not last:
                        project(layer + 1, 0)
                    if g > 0:
                        turn(layer, g - 1)
                    elif not first:
                        turn(layer - 1, GROUPS - 1)
                    mix_tokens(layer, g, first, last and g == GROUPS - 1)
            layers(pe, layer_steps)
            turn(LAST, GROUPS - 1)

        @block.scalar
        def _(act):
            def front(layer, g, first=False):
                n = layer * GROUPS + g
                act.wait_ge(bc_ready, n + 1)
                if not (first and g < 2):
                    act.wait_ge(g_ready, n - 1)
                nc.scalar.activation(b_t[:, g % 2, :], BC[0:STATE, :], ACT.Copy).then_inc(bt_copied, 1)
                if g == 0:
                    act.wait_ge(names["conv_loaded"], layer * 32 + 32)
                for c in range(KI):
                    act.wait_ge(xs_ready, n * KI + c + 1)
                    if not (first and g == 0):
                        act.wait_ge(u_ready, n * KI - KI + c + 1)
                    nc.scalar.activation(conv[:, c, :], XS(c)[:, :], ACT.Identity, bias=conv_b[:, c:c + 1],
                                         scale=conv_w[:, c, TAPS - 1:TAPS]).then_inc(tap_last, 1)

            def silu(layer, g, chunks, first=False):
                n = layer * GROUPS + g
                for c in chunks:
                    act.wait_ge(conv_done, n * KI + c + 1)
                    if not (first and g < 2):
                        act.wait_ge(uw_ready, n * 2 - 2)
                    nc.scalar.activation(u[:, g % 2, c, :], conv[:, c, :], ACT.Silu).then_inc(u_ready, 1)

            def copy_uw(layer, g, h):
                n = layer * GROUPS + g
                act.wait_ge(uw_ready, n * 2 + h + 1)
                nc.scalar.activation(uw[:, h, :], UWY[h][:, :], ACT.Copy).then_inc(uw_copied, 1)

            def copy_turned(layer, g):
                n = layer * GROUPS + g
                for h in range(2):
                    act.wait_ge(tr_ready, n * 2 + h + 1)
                    t = g * GT + 2 * h * P
                    nc.scalar.activation(ACT_T[:, :, t:t + 2 * P],
                                         TR[:, :].rearrange("p (k t) -> p k t", k=KD),
                                         ACT.Copy).then_inc(tr_copied, 1)

            front(0, 0, first=True)
            silu(0, 0, range(KI), first=True)

            def layer_steps(layer):
                first, last = layer_is(layer, 0), layer_is(layer, LAST)
                for g in range(GROUPS):
                    ahead = (layer, g + 1, first) if g < GROUPS - 1 else None if last else (layer + 1, 0)
                    if ahead:
                        front(*ahead)
                    if g > 0:
                        copy_turned(layer, g - 1)
                    elif not first:
                        copy_turned(layer - 1, GROUPS - 1)
                    if ahead:
                        silu(*ahead[:2], range(0, 2), *ahead[2:])
                    copy_uw(layer, g, 0)
                    copy_uw(layer, g, 1)
                    if ahead:
                        silu(*ahead[:2], range(2, KI), *ahead[2:])
            layers(act, layer_steps)
            copy_turned(LAST, GROUPS - 1)

        @block.vector
        def _(dve):
            def copy_c(layer, g, first=False):
                n = layer * GROUPS + g
                dve.wait_ge(bc_ready, n + 1)
                if not (first and g < 2):
                    dve.wait_ge(g_ready, n - 1)
                dve.tensor_copy(c_t[:, g % 2, :], BC[STATE:P, :]).then_inc(ct_copied, 1)

            def convolve(layer, g, pair):
                n = layer * GROUPS + g
                for back in range(1, TAPS):
                    for c in (2 * pair, 2 * pair + 1):
                        acc = conv[:, c, :].rearrange("p (s t) -> p s t", s=GS)[:, :, back:]
                        xs = XS(c)[:, :].rearrange("p (s t) -> p s t", s=GS)[:, :, 0:P - back]
                        if back == 1:
                            dve.wait_ge(tap_last, n * KI + c + 1)
                        else:
                            dve.wait_ge(tap_step, (n * 2 + pair) * 4 + (back - 2) * 2 + (c - 2 * pair) + 1)
                        op = dve.scalar_tensor_tensor(out=acc, in0=xs, scalar=conv_w[:, c, TAPS - 1 - back:TAPS - back],
                                                      in1=acc, op0=ALU.mult, op1=ALU.add)
                        op.then_inc(conv_done if back == TAPS - 1 else tap_step, 1)

            def decayed(layer, g):
                n = layer * GROUPS + g
                dve.wait_ge(g_ready, n + 1)
                if g == 0 and layer_is(layer, 0):
                    dve.wait_ge(names["decay_loaded"], 16)
                dve.tensor_tensor(mix[:, :, :], BC[:, :].rearrange("p (s t) -> p s t", s=GS),
                                  decay[:, :].unsqueeze(1).broadcast_to([P, GS, P]), ALU.mult).then_inc(mix_ready, 1)

            def norm(layer, g):
                n = layer * GROUPS + g
                for h in range(2):
                    b = g * GS + 2 * h
                    dve.wait_ge(y_ready, n * 2 + h + 1)
                    dve.tensor_tensor(res[:, h, :].rearrange("p (s d) -> p s d", s=2),
                                      UWY[h][:, :].rearrange("p (s d) -> p s d", s=2),
                                      ACTV[:, b:b + 2, :], ALU.add).then_inc(res_ready, 1)
                    dve.wait_ge(res_ready, n * 2 + h + 1)
                    for s in range(2):
                        dve.bn_stats(stats[:, 2 * h + s, :], res[:, h, s * D:(s + 1) * D]).then_inc(stats_ready, 1)
                    dve.wait_ge(stats_ready, n * 4 + 2 * h + 2)
                    dve.sem_inc(stats_seen, 1)
                    for s in range(2):
                        dve.bn_aggr(mv[:, 2 * h + s, :], stats[:, 2 * h + s, :]).then_inc(aggr_ready, 1)
                    dve.wait_ge(aggr_ready, n * 4 + 2 * h + 2)
                    dve.tensor_scalar(ve[:, 2 * h:2 * h + 2], mv[:, 2 * h:2 * h + 2, 1], EPS, None,
                                      ALU.add).then_inc(var_ready, 1)
                for h in range(2):
                    dve.wait_ge(rstd_ready, n * 2 + h + 1)
                    for s in range(2):
                        i = 2 * h + s
                        dve.tensor_scalar(z[:, h, s, :], res[:, h, s * D:(s + 1) * D], mv[:, i, 0:1],
                                          ve[:, i:i + 1], ALU.subtract, ALU.mult).then_inc(z_ready, 1)

            copy_c(0, 0, True)
            convolve(0, 0, 0)
            convolve(0, 0, 1)

            def layer_steps(layer):
                first, last = layer_is(layer, 0), layer_is(layer, LAST)
                for g in range(GROUPS):
                    ahead = (layer, g + 1) if g < GROUPS - 1 else None if last else (layer + 1, 0)
                    if ahead:
                        copy_c(*ahead, first and g < GROUPS - 1)
                        convolve(*ahead, 0)
                    decayed(layer, g)
                    if ahead:
                        convolve(*ahead, 1)
                    norm(layer, g)
            layers(dve, layer_steps)

        @block.gpsimd
        def _(pool):
            def finish(layer, g):
                n = layer * GROUPS + g
                for h in range(2):
                    pool.wait_ge(var_ready, n * 2 + h + 1)
                    pool.tensor_tensor(ve[:, 2 * h:2 * h + 2], ve[:, 2 * h:2 * h + 2], neghalf[:, 0:2],
                                       ALU.pow).then_inc(rstd_ready, 1)
                if g == 0:
                    pool.wait_ge(names["ln_loaded"], layer * 32 + 32)
                for h in range(2):
                    b = g * GS + 2 * h
                    pool.wait_ge(z_ready, n * 4 + 2 * h + 2)
                    pool.tensor_tensor(zg[:, h, :, :], z[:, h, :, :],
                                       ln_g[:, :].unsqueeze(1).broadcast_to([P, 2, D]), ALU.mult).then_inc(zg_ready, 1)
                    pool.wait_ge(zg_ready, n * 2 + h + 1)
                    pool.tensor_tensor(ACTV[:, b:b + 2, :], zg[:, h, :, :],
                                       ln_b[:, :].unsqueeze(1).broadcast_to([P, 2, D]), ALU.add).then_inc(act_ready, 1)

            def split_attention_weight(layer, g):
                n = layer * GROUPS + g
                cols = slice(g * 2 * KI * P // 2, (g + 1) * 2 * KI * P // 2)
                w = mem["attn_w"]
                if g == 0:
                    pool.wait_ge(mem["attn_w_loaded"], layer * 16 + 16)
                part = lambda x: x[:, bass.ds(layer, 1), cols].rearrange("p a n -> p (a n)")
                pool.tensor_copy(part(w[HI]), mem["attn_raw"][:, cols]).then_inc(attn_hi_ready, 1)
                pool.wait_ge(attn_hi_ready, n + 1)
                pool.tensor_tensor(part(w[LO]), mem["attn_raw"][:, cols], part(w[HI]).bitcast(F32),
                                   ALU.subtract).then_inc(mem["attn_w_split"], 1)

            with pool.Fori(0, LAST) as layer:
                for g in range(GROUPS):
                    finish(layer, g)
                    split_attention_weight(layer, g)
            for g in range(GROUPS):
                finish(LAST, g)


def layer_is(layer, value):
    return isinstance(layer, int) and layer == value


def product(pe, out, lhs, rhs, start, stop):
    pe.matmul(out, lhs[HI], rhs[HI], start=start, stop=False)
    pe.matmul(out, lhs[HI], rhs[LO], start=False, stop=False)
    return pe.matmul(out, lhs[LO], rhs[HI], start=False, stop=stop)


def chunks_of(pair, i, chunks):
    return [x[:, i, :].rearrange("p (k n) -> p k n", k=chunks) for x in pair]


HEADS = 16
HEAD = 64
WIDE = HEADS * HEAD
KW = WIDE // P
OCT = KW // 2


def stage_self_attention(nc, ctx, io, mem):
    X, ACTV, ACT_T, ident, neghalf, psum = mem["x"], mem["act"], mem["act_t"], mem["ident"], mem["neghalf"], mem["psum"]
    sb = lambda name, shape, dt=F32: ctx.enter_context(nc.sbuf_tensor("a_" + name, shape, dt))
    sem = lambda name: mem["sems"]("a_" + name)
    pair = lambda name, shape: (sb(name + "_hi", shape, F32R), sb(name + "_lo", shape, F32R))
    w = mem["attn_w"]
    wq, wk, wv = (chunks_of(w, i, KD) for i in range(3))
    wo = chunks_of(w, 3, KW)
    ln_g, ln_b = mem["attn_g"], mem["attn_b"]
    xg = pair("xg", [P, KD, GT])
    q_t = sb("q_t", [P, KW, GT])
    k_t = sb("k_t", [P, KW, GT])
    v = sb("v", [P, GS, WIDE])
    prob = sb("prob", [P, 4, 4, P])
    prob_t = sb("prob_t", [P, 4, 4, P])
    o_t = pair("o_t", [P, OCT, P])
    neg_max, total, inv = (sb(name, [P, 4, 4]) for name in ("neg_max", "total", "inv"))
    res = sb("res", [P, 2, D])
    z = sb("z", [P, 2, D])
    zg = sb("zg", [P, D])
    zb = sb("zb", [P, D])
    stats, mv, ve = mem["stats"], mem["mv"], mem["ve"]

    xh_ready, xl_ready = sem("xh_ready"), sem("xl_ready")
    job_ready = sem("job_ready")
    job_act, job_dve = sem("job_act"), sem("job_dve")
    s_ready = sem("s_ready")
    max_ready, exp_ready = sem("max_ready"), sem("exp_ready")
    inv_ready, prob_ready = sem("inv_ready"), sem("prob_ready")
    pt_ready = sem("pt_ready")
    pt_act, pt_dve = sem("pt_act"), sem("pt_dve")
    ot_ready = sem("ot_ready")
    ot_hi, ot_lo = sem("ot_hi"), sem("ot_lo")
    y_ready, y_added = sem("y_ready"), sem("y_added")
    stats_ready, aggr_ready, var_ready, rstd_ready = (sem(n) for n in (
        "stats_ready", "aggr_ready", "var_ready", "rstd_ready"))
    z_ready, zg_ready, zb_ready, x_ready = sem("z_ready"), sem("zg_ready"), sem("zb_ready"), sem("x_ready")

    HALF_TICKS = 2 * GS
    HALVES = 2 * GROUPS
    TICKS = HALVES * HALF_TICKS
    JOBS = 2 * OCT + GS
    JOB_TICKS = (0, 0, 1, 1, 2, 2, 3, 3, 4, 5, 6, 7)
    INVERT, NORM, TURN, MEAN, SPLIT, OUT, NORM_OUT = 1, 2, 3, 5, 7, 8, 10
    LAST_TICK = TICKS - 2 + NORM_OUT
    S, JOB, PT = psum[0:2], psum[2:4], psum[4:6]
    OT = lambda U: psum[6 + U % 2][:, :]
    Y = lambda U: psum[6 + U % 2][:, 0:D]

    def place(m):
        half, i = divmod(m, HALF_TICKS)
        return half // 2, half % 2, i // 2, i % 2

    def behind(m, ticks):
        t = m - ticks
        return (t // 2, *place(t)[:3]) if t % 2 == 0 and 0 <= t < TICKS else None

    def jobs_at(m):
        half, i = divmod(m, HALF_TICKS)
        return [(half + 1, j) for j in range(JOBS) if JOB_TICKS[j] == i] if half < HALVES - 1 else []

    with nc.Block() as block:
        @block.tensor
        def _(pe):
            def job(half, j):
                n = half * JOBS + j
                G, octet = divmod(half, 2)
                if octet == 0 and j == 0:
                    pe.wait_ge(xl_ready, G + 1)
                if n >= 2:
                    pe.wait_ge((job_act, job_dve)[j % 2], n // 2)
                bank = JOB[j % 2]
                if j < 2 * OCT:
                    weights, c = (wq, wk)[j % 2], octet * OCT + j // 2
                    for k in range(KD):
                        mm = product(pe, bank[:, :], [x[:, k, c * P:(c + 1) * P] for x in weights], [x[:, k, :] for x in xg],
                                     k == 0, k == KD - 1)
                else:
                    s = j - 2 * OCT
                    for k in range(KD):
                        mm = product(pe, bank[:, :], [x[:, k, s * P:(s + 1) * P] for x in xg],
                                     [x[:, k, octet * BANK:(octet + 1) * BANK] for x in wv], k == 0, k == KD - 1)
                mm.then_inc(job_ready, 1)

            pe.wait_ge(mem["attn_w_split"], 16)
            for j in range(JOBS):
                job(0, j)
            for m in range(LAST_TICK + 1):
                if m < TICKS:
                    G, octet, s, par = place(m)
                    if m % HALF_TICKS == 0:
                        jobs = (m // HALF_TICKS) * (JOBS // 2) + OCT
                        pe.wait_ge(job_act, jobs)
                        pe.wait_ge(job_dve, jobs)
                    if m >= 2:
                        pe.wait_ge(exp_ready, m - 1)
                    pe.matmul(S[par][:, :], mem["ident_bf"][:, :], mem["causal"][:, :].unsqueeze(1).broadcast_to([P, 4, P]),
                              start=True, stop=False, skip_group_check=True)
                    rows = slice(par * HEAD, (par + 1) * HEAD)
                    for i in range(4):
                        mm = pe.matmul(S[par][:, i * P:(i + 1) * P], q_t[rows, OCT * octet + i, s * P:(s + 1) * P],
                                       k_t[rows, OCT * octet + i, s * P:(s + 1) * P],
                                       start=False, stop=True, skip_group_check=True)
                    mm.then_inc(s_ready, 1)
                t = m - TURN
                if 0 <= t < TICKS:
                    pe.wait_ge(prob_ready, t + 1)
                    if t >= 2:
                        pe.wait_ge((pt_dve, pt_act)[t % 2], t // 2)
                    for i in range(4):
                        tr = pe.transpose(PT[t % 2][:, i * P:(i + 1) * P], prob[:, t % 4, i, :], ident[:, :])
                    tr.then_inc(pt_ready, 1)
                t = m - MEAN
                if 0 <= t < TICKS:
                    G, octet, s, par = place(t)
                    U = t // 2
                    if t % HALF_TICKS == 0:
                        jobs = (t // HALF_TICKS + 1) * (JOBS // 2)
                        pe.wait_ge(job_act, jobs)
                        pe.wait_ge(job_dve, jobs)
                    if par == 0 and U >= 2:
                        pe.wait_ge(y_added, U - 1)
                    pe.wait_ge((pt_dve, pt_act)[t % 2], t // 2 + 1)
                    rows = slice(par * HEAD, (par + 1) * HEAD)
                    for i in range(4):
                        head = octet * 8 + 2 * i + par
                        mm = pe.matmul(OT(U)[rows, i * P:(i + 1) * P], v[:, s, head * HEAD:(head + 1) * HEAD],
                                       prob_t[:, t % 4, i, :], start=True, stop=True, tile_position=(0, par * HEAD))
                    if par == 1:
                        mm.then_inc(ot_ready, 1)
                unit = behind(m, OUT)
                if unit:
                    U, G, octet, s = unit
                    pe.wait_ge(ot_hi, U + 1)
                    pe.wait_ge(ot_lo, U + 1)
                    for c in range(OCT):
                        mm = product(pe, Y(U), [x[:, c, :] for x in o_t], [x[:, octet * OCT + c, :] for x in wo],
                                     c == 0, c == OCT - 1)
                    mm.then_inc(y_ready, 1)
                for half, j in jobs_at(m):
                    job(half, j)

        @block.scalar
        def _(act):
            def take_group(G):
                if G > 0:
                    act.wait_ge(job_ready, G * 2 * JOBS)
                act.activation(xg[HI][:, :, :], ACT_T[:, :, G * GT:(G + 1) * GT], ACT.Copy).then_inc(xh_ready, 1)

            def job(half, j):
                G, octet = divmod(half, 2)
                act.wait_ge(job_ready, half * JOBS + j + 1)
                if j < 2 * OCT:
                    act.activation(q_t[:, octet * OCT + j // 2, :], JOB[0][:, :], ACT.Copy, scale=HEAD ** -0.5).then_inc(job_act, 1)
                else:
                    act.activation(v[:, j - 2 * OCT, octet * BANK:(octet + 1) * BANK], JOB[0][:, :], ACT.Copy).then_inc(job_act, 1)

            take_group(0)
            for j in range(0, JOBS, 2):
                job(0, j)
            for m in range(LAST_TICK + 1):
                if m < TICKS:
                    act.wait_ge(max_ready, m + 1)
                    for i in range(4):
                        e = act.activation(prob[:, m % 4, i, :], S[m % 2][:, i * P:(i + 1) * P], ACT.Exp,
                                           bias=neg_max[:, m % 4, i:i + 1], accum_out=total[:, m % 4, i:i + 1])
                    e.then_inc(exp_ready, 1)
                t = m - TURN
                if 0 <= t < TICKS and t % 2 == 1:
                    act.wait_ge(pt_ready, t + 1)
                    act.activation(prob_t[:, t % 4, :, :], PT[1][:, :].rearrange("p (i k) -> p i k", i=4),
                                   ACT.Copy).then_inc(pt_act, 1)
                unit = behind(m, SPLIT)
                if unit:
                    U = unit[0]
                    act.wait_ge(ot_ready, U + 1)
                    if U > 0:
                        act.wait_ge(y_ready, U)
                    act.activation(o_t[HI][:, :, :], OT(U).rearrange("p (i k) -> p i k", i=OCT), ACT.Copy).then_inc(ot_hi, 1)
                for half, j in jobs_at(m):
                    if j % 2 == 0:
                        job(half, j)
                G, i = divmod(m + 1, 2 * HALF_TICKS)
                if i == HALF_TICKS and G + 1 < GROUPS:
                    take_group(G + 1)

        @block.vector
        def _(dve):
            def take_group(G):
                dve.wait_ge(xh_ready, G + 1)
                dve.tensor_tensor(xg[LO][:, :, :], ACT_T[:, :, G * GT:(G + 1) * GT], xg[HI][:, :, :].bitcast(F32),
                                  ALU.subtract).then_inc(xl_ready, 1)

            def job(half, j):
                G, octet = divmod(half, 2)
                dve.wait_ge(job_ready, half * JOBS + j + 1)
                out = k_t[:, octet * OCT + j // 2, :] if j < 2 * OCT else v[:, j - 2 * OCT, octet * BANK:(octet + 1) * BANK]
                dve.tensor_copy(out, JOB[1][:, :]).then_inc(job_dve, 1)

            def measure(b):
                i = b % 2
                dve.bn_stats(stats[:, i, :], res[:, i, :]).then_inc(stats_ready, 1)
                dve.wait_ge(stats_ready, b + 1)
                dve.bn_aggr(mv[:, i, :], stats[:, i, :]).then_inc(aggr_ready, 1)
                dve.wait_ge(aggr_ready, b + 1)
                dve.tensor_scalar(ve[:, i:i + 1], mv[:, i, 1:2], EPS, None, ALU.add).then_inc(var_ready, 1)

            take_group(0)
            for j in range(1, JOBS, 2):
                job(0, j)
            for m in range(LAST_TICK + 1):
                if m < TICKS:
                    dve.wait_ge(s_ready, m + 1)
                    dve.tensor_reduce(neg_max[:, m % 4, :], S[m % 2][:, :].rearrange("p (i k) -> p i k", i=4), AX.X, ALU.max,
                                      negate=True).then_inc(max_ready, 1)
                t = m - INVERT
                if 0 <= t < TICKS:
                    dve.wait_ge(exp_ready, t + 1)
                    dve.reciprocal(inv[:, t % 4, :], total[:, t % 4, :]).then_inc(inv_ready, 1)
                t = m - TURN
                if 0 <= t < TICKS and t % 2 == 0:
                    dve.wait_ge(pt_ready, t + 1)
                    dve.tensor_copy(prob_t[:, t % 4, :, :], PT[0][:, :].rearrange("p (i k) -> p i k", i=4)).then_inc(pt_dve, 1)
                unit = behind(m, SPLIT)
                if unit:
                    U = unit[0]
                    dve.wait_ge(ot_hi, U + 1)
                    dve.tensor_tensor(o_t[LO][:, :, :], OT(U).rearrange("p (i k) -> p i k", i=OCT),
                                      o_t[HI][:, :, :].bitcast(F32), ALU.subtract).then_inc(ot_lo, 1)
                unit = behind(m, OUT)
                if unit:
                    U, G, octet, s = unit
                    b = G * GS + s
                    dve.wait_ge(y_ready, U + 1)
                    out = res[:, b % 2, :] if octet else ACTV[:, b, :]
                    dve.tensor_tensor(out, Y(U), ACTV[:, b, :], ALU.add).then_inc(y_added, 1)
                    if octet:
                        dve.wait_ge(y_added, U + 1)
                        measure(b)
                unit = behind(m, NORM_OUT)
                if unit and unit[2]:
                    U, G, octet, s = unit
                    b = G * GS + s
                    i = b % 2
                    dve.wait_ge(rstd_ready, b + 1)
                    dve.tensor_scalar(z[:, i, :], res[:, i, :], mv[:, i, 0:1], ve[:, i:i + 1],
                                      ALU.subtract, ALU.mult).then_inc(z_ready, 1)
                for half, j in jobs_at(m):
                    if j % 2 == 1:
                        job(half, j)
                G, i = divmod(m + 1, 2 * HALF_TICKS)
                if i == HALF_TICKS and G + 1 < GROUPS:
                    take_group(G + 1)

        @block.gpsimd
        def _(pool):
            def finish(b):
                pool.wait_ge(z_ready, b + 1)
                pool.tensor_tensor(zg[:, :], z[:, b % 2, :], ln_g[:, :], ALU.mult).then_inc(zg_ready, 1)
                pool.wait_ge(zg_ready, b + 1)
                pool.tensor_tensor(zb[:, :], zg[:, :], ln_b[:, :], ALU.add).then_inc(zb_ready, 1)
                pool.wait_ge(zb_ready, b + 1)
                pool.tensor_tensor(X[:, b, :], X[:, b, :], zb[:, :], ALU.add).then_inc(x_ready, 1)

            pool.wait_ge(mem["attn_ln_loaded"], 32)
            for m in range(LAST_TICK + 1):
                t = m - NORM
                if 0 <= t < TICKS:
                    pool.wait_ge(inv_ready, t + 1)
                    pool.tensor_tensor(prob[:, t % 4, :, :], prob[:, t % 4, :, :],
                                       inv[:, t % 4, :].unsqueeze(2).broadcast_to([P, 4, P]), ALU.mult).then_inc(prob_ready, 1)
                unit = behind(m, OUT)
                if unit and unit[2]:
                    b = unit[1] * GS + unit[3]
                    i = b % 2
                    pool.wait_ge(var_ready, b + 1)
                    pool.tensor_tensor(ve[:, i:i + 1], ve[:, i:i + 1], neghalf[:, 0:1], ALU.pow).then_inc(rstd_ready, 1)
                unit = behind(m, NORM_OUT)
                if unit and unit[2]:
                    finish(unit[1] * GS + unit[3])


def norm_state(nc, ctx, mem, name, width):
    norm = {"width": width, "neghalf": mem["neghalf"]}
    for what, shape in (("stats", [P, width, 6]), ("mv", [P, width, 2]), ("ve", [P, width])):
        norm[what] = ctx.enter_context(nc.sbuf_tensor(f"{name}_{what}", shape, F32))
    for what in ("stats_ready", "stats_seen", "aggr_ready", "var_ready", "rstd_ready", "z_ready"):
        norm[what] = mem["sems"](f"{name}_{what}")
    return norm


def norm_measure(dve, norm, n, rows):
    w = norm["width"]
    for i in range(w):
        dve.bn_stats(norm["stats"][:, i, :], rows(i)).then_inc(norm["stats_ready"], 1)
    dve.wait_ge(norm["stats_ready"], n * w + w)
    dve.sem_inc(norm["stats_seen"], 1)
    for i in range(w):
        dve.bn_aggr(norm["mv"][:, i, :], norm["stats"][:, i, :]).then_inc(norm["aggr_ready"], 1)
    dve.wait_ge(norm["aggr_ready"], n * w + w)
    dve.tensor_scalar(norm["ve"][:, :], norm["mv"][:, :, 1], EPS, None, ALU.add).then_inc(norm["var_ready"], 1)


def norm_invert(pool, norm, n):
    ve = norm["ve"][:, :]
    pool.wait_ge(norm["var_ready"], n + 1)
    pool.tensor_tensor(ve, ve, norm["neghalf"][:, 0:norm["width"]], ALU.pow).then_inc(norm["rstd_ready"], 1)


def norm_apply(dve, norm, n, rows, outs):
    dve.wait_ge(norm["rstd_ready"], n + 1)
    for i in range(norm["width"]):
        dve.tensor_scalar(outs(i), rows(i), norm["mv"][:, i, 0:1], norm["ve"][:, i:i + 1],
                          ALU.subtract, ALU.mult).then_inc(norm["z_ready"], 1)


def row_of(tensor, index):
    return tensor[:, bass.ds(index, 1), :].rearrange("p a d -> p (a d)")


XHEAD = D // HEADS
HPC = P // XHEAD
ROWT = 32
TILES = P // ROWT


def stage_cross_attention(nc, ctx, io, mem):
    X, ident, neghalf, psum = mem["x"], mem["ident"], mem["neghalf"], mem["psum"]
    sb = lambda name, shape, dt=F32: ctx.enter_context(nc.sbuf_tensor("x_" + name, shape, dt))
    sem = lambda name: mem["sems"]("x_" + name)
    pair = lambda name, shape: (sb(name + "_hi", shape, F32R), sb(name + "_lo", shape, F32R))
    norm = norm_state(nc, ctx, mem, "xn", GS)
    w_raw = sb("w_raw", [P, 4, KD * D])
    w = pair("w", [P, 4, KD * D])
    wk, wv, wq, wo = (chunks_of(w, i, KD) for i in range(4))
    bq, bk = sb("bq", [P, KD]), sb("bk", [P, KD])
    bq_scaled = sb("bq_scaled", [P, KD])
    bv, bo = sb("bv", [P, D]), sb("bo", [P, D])
    sel = sb("sel", [P, 2])
    ctx_raw = sb("ctx_raw", [P, 2, KD, GT])
    cg = pair("cg", [P, KD, GT])
    z = sb("z", [P, GS, D])
    xg = pair("xg", [P, KD, GT])
    q_t = sb("q_t", [P, 2, KD, GT])
    k_t = sb("k_t", [P, 2, 2, KD, GT])
    v = sb("v", [P, 2, 2, GS, D])
    prob = sb("prob", [P, 2, TILES, 4, P])
    prob_t = sb("prob_t", [P, 2, TILES, 4, P])
    neg_max, total, inv = (sb(name, [P, 2, TILES, 4]) for name in ("neg_max", "total", "inv"))
    o_t = pair("o_t", [P, KD, P])

    w_loaded = [sem(f"w{i}_loaded") for i in range(4)]
    ctx_loaded = [sem(f"ctx_loaded{i}") for i in range(2)]
    bias_loaded = sem("bias_loaded")
    w_hi, w_split = sem("w_hi"), sem("w_split")
    ctx_hi, ctx_lo = sem("ctx_hi"), sem("ctx_lo")
    setup, bq_ready = sem("setup"), sem("bq_ready")
    sel_step = sem("sel_step")
    tr_ready, xh_ready, xl_ready = sem("tr_ready"), sem("xh_ready"), sem("xl_ready")
    q_ready, k_ready, v_ready = sem("q_ready"), sem("k_ready"), sem("v_ready")
    q_copied, k_copied, v_copied = sem("q_copied"), sem("k_copied"), sem("v_copied")
    s_ready, max_ready, exp_ready = sem("s_ready"), sem("max_ready"), sem("exp_ready")
    pt_ready, pt_act, pt_dve = sem("pt_ready"), sem("pt_act"), sem("pt_dve")
    v_cleared, inv_ready, prob_ready = sem("v_cleared"), sem("inv_ready"), sem("prob_ready")
    ot_ready, ot_hi, ot_lo = sem("ot_ready"), sem("ot_hi"), sem("ot_lo")
    y_ready, y_added, x_ready = sem("y_ready"), sem("y_added"), sem("x_ready")

    S, JOB, PT = psum[0:2], psum[2:4], psum[4:6]
    OT = lambda b: psum[6 + b % 2][:, 0:D]
    Y = lambda b: psum[6 + b % 2][:, D:2 * D]
    TICKS = SEQS * TILES
    GROUP_TICKS = GS * TILES
    JOB_TICKS = (0, 2, 4, 6, 8, 9, 11, 13)
    JOBS = len(JOB_TICKS)
    INVERT, TURN, MEAN, SPLIT_HIGH, SPLIT_LOW, OUT, ADD = 1, 3, 5, 9, 9, 11, 12
    LAST_TICK = TICKS - TILES + ADD

    def behind(m, ticks):
        b, r = divmod(m - ticks, TILES)
        return b if r == 0 and 0 <= b < SEQS else None

    def jobs_at(m):
        G, i = divmod(m, GROUP_TICKS)
        return [(G + 1, JOB_TICKS.index(i))] if G < GROUPS - 1 and i in JOB_TICKS else []

    with nc.Block() as block:
        @block.sync
        def _(sp):
            load = lambda i, name: sp.dma_start(w_raw[:, i, :], io["L0_xattn_" + name + "_laid"]).then_inc(w_loaded[i], 16)

            def load_context(G):
                sp.dma_start(ctx_raw[:, G % 2, :, :], io["ctx_t_laid"][:, :, G * GT:(G + 1) * GT]).then_inc(ctx_loaded[G % 2], 16)
            load(0, "W_k")
            load_context(0)
            load(1, "W_v")
            for tile, name in ((bq, "b_q"), (bk, "b_k")):
                sp.dma_start(tile[:, :], io["L0_xattn_" + name + "_laid"]).then_inc(bias_loaded, 16)
            for tile, name in ((bv, "b_v"), (bo, "b_o")):
                sp.dma_start(tile[:, :], io["L0_xattn_" + name].unsqueeze(0).broadcast_to([P, D])).then_inc(bias_loaded, 16)
            load(2, "W_q")
            load(3, "W_o")
            load_context(1)
            for G in range(2, GROUPS):
                sp.wait_ge(ctx_lo, G - 1)
                load_context(G)

        @block.gpsimd
        def _(pool):
            pool.memset(v[:, 0, :, :, :], 0.0).then_inc(v_cleared, 1)
            pool.memset(sel[:, :], 0.0).then_inc(sel_step, 1)
            pool.wait_ge(sel_step, 1)
            for r in range(TILES):
                if r > 0:
                    pool.wait_ge(setup, 2 * r)
                rows = slice(r * ROWT, (r + 1) * ROWT)
                pool.affine_select(out=sel[rows, 0:1], in_=sel[rows, 0:1], compare_op=ALU.is_ge, fill=1.0,
                                   base=-XHEAD, pattern=[[1, 1]], channel_multiplier=1).then_inc(setup, 1)
                pool.wait_ge(setup, 2 * r + 1)
                pool.affine_select(out=sel[rows, 1:2], in_=sel[rows, 1:2], compare_op=ALU.is_ge, fill=1.0,
                                   base=XHEAD - 1, pattern=[[1, 1]], channel_multiplier=-1).then_inc(setup, 1)
            pool.wait_ge(setup, 2 * TILES)
            norm_invert(pool, norm, 0)

            def add_bias(b):
                if b == 0:
                    pool.wait_ge(bias_loaded, 64)
                pool.wait_ge(y_added, b + 1)
                pool.tensor_tensor(X[:, b, :], X[:, b, :], bo[:, :], ALU.add).then_inc(x_ready, 1)

            def weight_low(i):
                pool.wait_ge(w_hi, i + 1)
                pool.tensor_tensor(w[LO][:, i, :], w_raw[:, i, :], w[HI][:, i, :].bitcast(F32), ALU.subtract).then_inc(w_split, 1)

            def context_low(G):
                pool.wait_ge(ctx_hi, G + 1)
                pool.tensor_tensor(cg[LO][:, :, :], ctx_raw[:, G % 2, :, :], cg[HI][:, :, :].bitcast(F32),
                                   ALU.subtract).then_inc(ctx_lo, 1)
            weight_low(0)
            context_low(0)
            for i in range(1, 4):
                weight_low(i)
            pool.memset(v[:, 1, :, :, :], 0.0).then_inc(v_cleared, 1)

            def context_high(G):
                pool.wait_ge(ctx_loaded[G % 2], 16 * (G // 2) + 16)
                if G > 1:
                    pool.wait_ge(v_ready, G * KD)
                else:
                    pool.wait_ge(v_ready, KD)
                pool.tensor_copy(cg[HI][:, :, :], ctx_raw[:, G % 2, :, :]).then_inc(ctx_hi, 1)
            context_high(1)
            context_low(1)
            for m in range(LAST_TICK + 2):
                t = m - 2
                if 0 <= t < TICKS:
                    b, r = divmod(t, TILES)
                    pool.wait_ge(inv_ready, t + 1)
                    pool.tensor_tensor(prob[:, b % 2, r, :, :], prob[:, b % 2, r, :, :],
                                       inv[:, b % 2, r, :].unsqueeze(2).broadcast_to([P, 4, P]), ALU.mult).then_inc(prob_ready, 1)
                G, i = divmod(m, GROUP_TICKS)
                if i == 4 and G + 1 < GROUPS:
                    norm_invert(pool, norm, G + 1)
                if i == 10 and G + 2 < GROUPS:
                    context_high(G + 2)
                if i == 12 and G + 2 < GROUPS:
                    context_low(G + 2)
                b = behind(m, ADD + 1)
                if b is not None:
                    add_bias(b)

        @block.vector
        def _(dve):
            rows_of = lambda G: lambda i: X[:, G * GS + i, :]

            def normalise(G):
                if G > 0:
                    dve.wait_ge(tr_ready, G * KD)
                norm_apply(dve, norm, G, rows_of(G), lambda i: z[:, i, :])

            def job(G, j):
                kind, k = divmod(j, KD)
                n = G * KD + k
                bank = JOB[k]
                if kind == 0:
                    dve.wait_ge(k_ready, n + 1)
                    for par in range(2):
                        kc = dve.tensor_scalar(k_t[:, G % 2, par, k, :], bank[:, :], bk[:, k:k + 1], sel[:, par:par + 1],
                                               ALU.add, ALU.mult)
                    kc.then_inc(k_copied, 1)
                elif kind == 1:
                    dve.wait_ge(v_ready, n + 1)
                    if k == 0 and G < 2:
                        dve.wait_ge(v_cleared, G + 1)
                    for par in range(2):
                        heads_of = lambda x: x.rearrange("p s (h a d) -> p s h a d", a=2, d=XHEAD)[:, :, :, par, :]
                        vc = dve.tensor_tensor(heads_of(v[:, G % 2, par, 2 * k:2 * k + 2, :]),
                                               heads_of(bank[:, :].rearrange("p (s d) -> p s d", s=2)),
                                               heads_of(bv[:, :].unsqueeze(1).broadcast_to([P, 2, D])), ALU.add)
                    vc.then_inc(v_copied, 1)
                elif kind == 2:
                    dve.wait_ge(xh_ready, n + 1)
                    dve.tensor_tensor(xg[LO][:, k, :], bank[:, :], xg[HI][:, k, :].bitcast(F32),
                                      ALU.subtract).then_inc(xl_ready, 1)

            norm_measure(dve, norm, 0, rows_of(0))
            normalise(0)
            dve.wait_ge(bias_loaded, 64)
            dve.tensor_scalar(bq_scaled[:, :], bq[:, :], XHEAD ** -0.5, None, ALU.mult).then_inc(bq_ready, 1)
            dve.wait_ge(setup, 2 * TILES)
            for j in range(JOBS):
                job(0, j)
            for m in range(LAST_TICK + 1):
                if m < TICKS:
                    b, r = divmod(m, TILES)
                    dve.wait_ge(s_ready, m + 1)
                    dve.tensor_reduce(neg_max[:, b % 2, r, :], S[m % 2][:, :].rearrange("p (i k) -> p i k", i=4), AX.X,
                                      ALU.max, negate=True).then_inc(max_ready, 1)
                t = m - INVERT
                if 0 <= t < TICKS:
                    b, r = divmod(t, TILES)
                    dve.wait_ge(exp_ready, t + 1)
                    dve.reciprocal(inv[:, b % 2, r, :], total[:, b % 2, r, :]).then_inc(inv_ready, 1)
                t = m - TURN
                if 0 <= t < TICKS and t % 2 == 0:
                    b, r = divmod(t, TILES)
                    dve.wait_ge(pt_ready, t + 1)
                    dve.tensor_copy(prob_t[:, b % 2, r, :, :], PT[0][:, :].rearrange("p (i k) -> p i k", i=4)).then_inc(pt_dve, 1)
                b = behind(m, SPLIT_LOW)
                if b is not None:
                    dve.wait_ge(ot_hi, b + 1)
                    dve.tensor_tensor(o_t[LO][:, :, :], OT(b).rearrange("p (k t) -> p k t", k=KD),
                                      o_t[HI][:, :, :].bitcast(F32), ALU.subtract).then_inc(ot_lo, 1)
                b = behind(m, ADD)
                if b is not None:
                    dve.wait_ge(y_ready, b + 1)
                    dve.tensor_tensor(X[:, b, :], Y(b), X[:, b, :], ALU.add).then_inc(y_added, 1)
                for G, j in jobs_at(m - 1):
                    job(G, j)
                for G, j in jobs_at(m):
                    if j == 1:
                        norm_measure(dve, norm, G, rows_of(G))
                    elif j == 3:
                        normalise(G)

        @block.scalar
        def _(act):
            def job(G, j):
                kind, k = divmod(j, KD)
                n = G * KD + k
                if kind == 2:
                    act.wait_ge(tr_ready, n + 1)
                    act.activation(xg[HI][:, k, :], JOB[k][:, :], ACT.Copy).then_inc(xh_ready, 1)
                elif kind == 3:
                    act.wait_ge(q_ready, n + 1)
                    act.activation(q_t[:, G % 2, k, :], JOB[k][:, :], ACT.Identity, bias=bq_scaled[:, k:k + 1],
                                   scale=XHEAD ** -0.5).then_inc(q_copied, 1)

            def split_output(b):
                act.wait_ge(ot_ready, b + 1)
                act.activation(o_t[HI][:, :, :], OT(b).rearrange("p (k t) -> p k t", k=KD), ACT.Copy).then_inc(ot_hi, 1)

            for i in range(4):
                act.wait_ge(w_loaded[i], 16)
                act.activation(w[HI][:, i, :], w_raw[:, i, :], ACT.Copy).then_inc(w_hi, 1)
                if i == 0:
                    act.wait_ge(ctx_loaded[0], 16)
                    act.activation(cg[HI][:, :, :], ctx_raw[:, 0, :, :], ACT.Copy).then_inc(ctx_hi, 1)
            act.wait_ge(bq_ready, 1)
            for j in range(JOBS):
                job(0, j)
            for m in range(LAST_TICK + 1):
                if m < TICKS:
                    b, r = divmod(m, TILES)
                    act.wait_ge(max_ready, m + 1)
                    for i in range(4):
                        e = act.activation(prob[:, b % 2, r, i, :], S[m % 2][:, i * P:(i + 1) * P], ACT.Exp,
                                           bias=neg_max[:, b % 2, r, i:i + 1], accum_out=total[:, b % 2, r, i:i + 1])
                    e.then_inc(exp_ready, 1)
                t = m - TURN
                if 0 <= t < TICKS and t % 2 == 1:
                    b, r = divmod(t, TILES)
                    act.wait_ge(pt_ready, t + 1)
                    act.activation(prob_t[:, b % 2, r, :, :], PT[1][:, :].rearrange("p (i k) -> p i k", i=4),
                                   ACT.Copy).then_inc(pt_act, 1)
                b = behind(m, SPLIT_HIGH)
                if b is not None:
                    split_output(b)
                for G, j in jobs_at(m - 1):
                    job(G, j)

        @block.tensor
        def _(pe):
            def job(G, j):
                kind, k = divmod(j, KD)
                n = G * KD + k
                bank = JOB[k]
                if kind == 0:
                    if n == 0:
                        pe.wait_ge(w_split, 1)
                    pe.wait_ge(ctx_lo, G + 1)
                    if G > 0:
                        pe.wait_ge(q_copied, n - KD + 1)
                    for i in range(KD):
                        mm = product(pe, bank[:, :], [x[:, i, k * P:(k + 1) * P] for x in wk], [x[:, i, :] for x in cg],
                                     i == 0, i == KD - 1)
                    mm.then_inc(k_ready, 1)
                elif kind == 1:
                    if n == 0:
                        pe.wait_ge(w_split, 2)
                    pe.wait_ge(k_copied, n + 1)
                    for s in (2 * k, 2 * k + 1):
                        for i in range(KD):
                            mm = product(pe, bank[:, (s % 2) * D:(s % 2 + 1) * D], [x[:, i, s * P:(s + 1) * P] for x in cg],
                                         [x[:, i, :] for x in wv], i == 0, i == KD - 1)
                    mm.then_inc(v_ready, 1)
                elif kind == 2:
                    pe.wait_ge(norm["z_ready"], G * GS + GS)
                    pe.wait_ge(v_copied, n + 1)
                    for s in range(GS):
                        tr = pe.transpose(bank[:, s * P:(s + 1) * P], z[:, s, k * P:(k + 1) * P], ident[:, :])
                    tr.then_inc(tr_ready, 1)
                else:
                    if n == 0:
                        pe.wait_ge(w_split, 3)
                    pe.wait_ge(xl_ready, G * KD + KD)
                    for i in range(KD):
                        mm = product(pe, bank[:, :], [x[:, i, k * P:(k + 1) * P] for x in wq], [x[:, i, :] for x in xg],
                                     i == 0, i == KD - 1)
                    mm.then_inc(q_ready, 1)

            for j in range(JOBS):
                job(0, j)
            for m in range(LAST_TICK + 1):
                if m < TICKS:
                    b, r = divmod(m, TILES)
                    G, step = divmod(b, GS)
                    if m % GROUP_TICKS == 0:
                        pe.wait_ge(k_copied, G * KD + KD)
                        pe.wait_ge(q_copied, G * KD + KD)
                    if m >= 2:
                        pe.wait_ge(exp_ready, m - 1)
                    rows = slice(r * ROWT, (r + 1) * ROWT)
                    for i in range(4):
                        mm = pe.matmul(S[m % 2][:, i * P:(i + 1) * P], q_t[rows, G % 2, i // 2, step * P:(step + 1) * P],
                                       k_t[rows, G % 2, i % 2, i // 2, step * P:(step + 1) * P], start=True, stop=True,
                                       tile_position=(r * ROWT, 0))
                    mm.then_inc(s_ready, 1)
                t = m - TURN
                if 0 <= t < TICKS:
                    b, r = divmod(t, TILES)
                    pe.wait_ge(prob_ready, t + 1)
                    if t >= 2:
                        pe.wait_ge((pt_dve, pt_act)[t % 2], t // 2)
                    for i in range(4):
                        tr = pe.transpose(PT[t % 2][:, i * P:(i + 1) * P], prob[:, b % 2, r, i, :], ident[:, :])
                    tr.then_inc(pt_ready, 1)
                t = m - MEAN
                if 0 <= t < TICKS:
                    b, r = divmod(t, TILES)
                    G, s = divmod(b, GS)
                    if r == 0 and s == 0:
                        pe.wait_ge(v_copied, G * KD + KD)
                    if r == 0 and b >= 2:
                        pe.wait_ge(y_added, b - 1)
                    pe.wait_ge((pt_dve, pt_act)[t % 2], t // 2 + 1)
                    rows = slice(r * ROWT, (r + 1) * ROWT)
                    for i in range(4):
                        c, par = divmod(i, 2)
                        mm = pe.matmul(OT(b)[rows, c * P:(c + 1) * P],
                                       v[:, G % 2, par, s, c * P + r * ROWT:c * P + (r + 1) * ROWT], prob_t[:, b % 2, r, i, :],
                                       start=(par == 0), stop=(par == 1), tile_position=(0, r * ROWT))
                    if r == TILES - 1:
                        mm.then_inc(ot_ready, 1)
                b = behind(m, OUT)
                if b is not None:
                    if b == 0:
                        pe.wait_ge(w_split, 4)
                    pe.wait_ge(ot_hi, b + 1)
                    pe.wait_ge(ot_lo, b + 1)
                    for k in range(KD):
                        mm = product(pe, Y(b), [x[:, k, :] for x in o_t], [x[:, k, :] for x in wo], k == 0, k == KD - 1)
                    mm.then_inc(y_ready, 1)
                for G, j in jobs_at(m):
                    job(G, j)


EXPERTS = 8
FFN = 512
KF = FFN // P
W_PARTS = 3
W_COLS = KD * FFN


def stage_experts(nc, ctx, io, mem):
    X, ident, neghalf, psum = mem["x"], mem["ident"], mem["neghalf"], mem["psum"]
    sb = lambda name, shape, dt=F32: ctx.enter_context(nc.sbuf_tensor("e_" + name, shape, dt))
    sem = lambda name: mem["sems"]("e_" + name)
    pair = lambda name, shape: (sb(name + "_hi", shape, F32R), sb(name + "_lo", shape, F32R))
    norm = norm_state(nc, ctx, mem, "en", GS)
    raw = sb("raw", [P, W_PARTS, W_COLS])
    w = pair("w", [P, 2, W_PARTS, W_COLS])
    router_raw = sb("router_raw", [P, KD * EXPERTS])
    router = pair("router", [P, KD * EXPERTS])
    z = sb("z", [P, GS, D])
    xn = pair("xn", [P, KD, SEQS * P])
    gate = sb("gate", [P, 2, GT])
    h_raw = sb("h_raw", [P, 2, GT])
    h = pair("h", [P, 2, KF, GT])
    table = lambda name: sb(name, [P, SEQS, EXPERTS])
    column = lambda name: sb(name, [P, SEQS])
    logit, prob, left, cand, first_hot, second_hot, share, iota = (table(x) for x in (
        "logit", "prob", "left", "cand", "first_hot", "second_hot", "share", "iota"))
    col = {name: column(name) for name in ("max", "sum", "inv", "p1", "p2", "at1", "at2", "e", "w1", "w2", "gap")}

    w_loaded, hi_ready, w_split = sem("w_loaded"), sem("hi_ready"), sem("w_split")
    split_seen = sem("split_seen")
    r_loaded, r_hi, r_split = sem("r_loaded"), sem("r_hi"), sem("r_split")
    iota_ready = sem("iota_ready")
    tr_ready, xh_ready, xl_ready = sem("tr_ready"), sem("xh_ready"), sem("xl_ready")
    logit_ready = sem("logit_ready")
    route_step, route_exp, route_sem = sem("route_step"), sem("route_exp"), sem("route_ready")
    gate_ready, up_ready = sem("gate_ready"), sem("up_ready")
    silu_ready, prod_ready = sem("silu_ready"), sem("prod_ready")
    h_hi, h_lo = sem("h_hi"), sem("h_lo")
    down_ready, added = sem("down_ready"), sem("added")
    GATE, UP = (psum[0], psum[1]), (psum[2], psum[3])
    DOWN = lambda G, half: psum[4 + 2 * (G % 2) + half]
    PAIRS = EXPERTS // 2

    def steps(eng, ahead, rest):
        ahead(0, 0, 0)

        def body(pairs, last):
            for slot in range(2):
                e = pairs * 2 + slot
                for G in range(GROUPS):
                    if G < GROUPS - 1:
                        ahead(e, slot, G + 1)
                    elif not (last and slot == 1):
                        ahead(e + 1, 1 - slot, 0)
                    rest(e, slot, G)
        body(0, False)
        with eng.Fori(1, PAIRS - 1) as pairs:
            body(pairs, False)
        body(PAIRS - 1, True)

    early = lambda n, least: isinstance(n, int) and n < least

    with nc.Block() as block:
        @block.sync
        def _(sp):
            sp.dma_start(router_raw[:, :], io["router_laid"]).then_inc(r_loaded, 16)
            sp.dma_start(raw[:, :, :].rearrange("p a n -> p (a n)"), io["experts_laid"][0]).then_inc(w_loaded, 16)
            with sp.Fori(1, EXPERTS) as e:
                sp.wait_ge(w_split, e * W_PARTS)
                sp.dma_start(raw[:, :, :], io["experts_laid"][bass.ds(e, 1)].rearrange(
                    "e p (a n) -> p (e a) n", a=W_PARTS)).then_inc(w_loaded, 16)

        @block.gpsimd
        def _(pool):
            def split(e, slot, part):
                if part == 0:
                    pool.wait_ge(w_loaded, e * 16 + 16)
                    if not early(e, 2):
                        pool.wait_ge(down_ready, e * GROUPS - GROUPS)
                    pool.sem_inc(split_seen, 1)
                pool.tensor_copy(w[HI][:, slot, part, :], raw[:, part, :]).then_inc(hi_ready, 1)
                pool.wait_ge(hi_ready, e * W_PARTS + part + 1)
                pool.tensor_tensor(w[LO][:, slot, part, :], raw[:, part, :], w[HI][:, slot, part, :].bitcast(F32),
                                   ALU.subtract).then_inc(w_split, 1)

            def h_low(e, slot, G):
                n = e * GROUPS + G
                for f in range(KF):
                    pool.wait_ge(h_hi, n * KF + f + 1)
                    pool.tensor_tensor(h[LO][:, G % 2, f, :], h_raw[:, f % 2, :], h[HI][:, G % 2, f, :].bitcast(F32),
                                       ALU.subtract).then_inc(h_lo, 1)

            pool.iota(iota[:, :, :], pattern=[[0, SEQS], [1, EXPERTS]], base=0, channel_multiplier=0,
                      allow_small_or_imprecise_dtypes=True).then_inc(iota_ready, 1)
            for G in range(GROUPS):
                norm_invert(pool, norm, G)
            pool.wait_ge(r_loaded, 16)
            pool.tensor_copy(router[HI][:, :], router_raw[:, :]).then_inc(r_hi, 1)
            pool.wait_ge(r_hi, 1)
            pool.tensor_tensor(router[LO][:, :], router_raw[:, :], router[HI][:, :].bitcast(F32),
                               ALU.subtract).then_inc(r_split, 1)
            for part in range(W_PARTS):
                split(0, 0, part)

            def body(pairs, last):
                for slot in range(2):
                    e = pairs * 2 + slot
                    for G in range(GROUPS):
                        h_low(e, slot, G)
                        if G < W_PARTS and not (last and slot == 1):
                            split(e + 1, 1 - slot, G)
            body(0, False)
            with pool.Fori(1, PAIRS - 1) as pairs:
                body(pairs, False)
            body(PAIRS - 1, True)

        @block.tensor
        def _(pe):
            for G in range(GROUPS):
                pe.wait_ge(norm["z_ready"], G * GS + GS)
                if G > 0:
                    pe.wait_ge(xl_ready, G * KD)
                for k in range(KD):
                    for s in range(GS):
                        tr = pe.transpose(psum[6 + k][:, s * P:(s + 1) * P], z[:, s, k * P:(k + 1) * P], ident[:, :])
                    tr.then_inc(tr_ready, 1)
            pe.wait_ge(r_split, 1)
            pe.wait_ge(xh_ready, GROUPS * KD)
            pe.wait_ge(xl_ready, GROUPS * KD)
            for b in range(SEQS):
                for k in range(KD):
                    mm = product(pe, psum[5][:, b * EXPERTS:(b + 1) * EXPERTS], [x[:, k, b * P:(b + 1) * P] for x in xn],
                                 [x[:, k * EXPERTS:(k + 1) * EXPERTS] for x in router], k == 0, k == KD - 1)
            mm.then_inc(logit_ready, 1)

            def widen(e, slot, G):
                n = e * GROUPS + G
                tokens = slice(G * GT, (G + 1) * GT)
                if G == 0:
                    pe.wait_ge(w_split, e * W_PARTS + 2)
                for f in range(KF):
                    for part, bank, ready, read in ((0, GATE[f % 2], gate_ready, silu_ready),
                                                    (1, UP[f % 2], up_ready, prod_ready)):
                        if not early(n * KF + f, 2):
                            pe.wait_ge(read, n * KF + f - 1)
                        for k in range(KD):
                            mm = product(pe, bank[:, :], [x[:, slot, part, k * FFN + f * P:k * FFN + (f + 1) * P] for x in w],
                                         [x[:, k, tokens] for x in xn], k == 0, k == KD - 1)
                        mm.then_inc(ready, 1)

            def down(e, slot, G):
                n = e * GROUPS + G
                if G == 0:
                    pe.wait_ge(w_split, e * W_PARTS + 3)
                if not early(n, 2):
                    pe.wait_ge(added, n * GS - GS)
                if early(n, 2):
                    pe.wait_ge(route_step, 1)
                pe.wait_ge(h_hi, n * KF + KF)
                pe.wait_ge(h_lo, n * KF + KF)
                for s in range(GS):
                    out = DOWN(G, s // 2)[:, (s % 2) * D:(s % 2 + 1) * D]
                    for f in range(KF):
                        mm = product(pe, out, [x[:, G % 2, f, s * P:(s + 1) * P] for x in h], [x[:, slot, 2, f * D:(f + 1) * D] for x in w],
                                     f == 0, f == KF - 1)
                mm.then_inc(down_ready, 1)
            steps(pe, widen, down)

        @block.scalar
        def _(act):
            for G in range(GROUPS):
                for k in range(KD):
                    act.wait_ge(tr_ready, G * KD + k + 1)
                    act.activation(xn[HI][:, k, G * GT:(G + 1) * GT], psum[6 + k][:, :], ACT.Copy).then_inc(xh_ready, 1)
            for i, (out, in_) in enumerate(((prob[:, :, :], logit[:, :, :]), (col["e"][:, :], col["gap"][:, :]))):
                act.wait_ge(route_exp, i + 1)
                act.activation(out, in_, ACT.Exp).then_inc(route_sem, 1)

            def silu(n, f):
                act.wait_ge(gate_ready, n * KF + f + 1)
                if not early(n * KF + f, 2):
                    act.wait_ge(prod_ready, n * KF + f - 1)
                act.activation(gate[:, f % 2, :], GATE[f % 2][:, :], ACT.Silu).then_inc(silu_ready, 1)

            def high(n, G, f):
                act.wait_ge(prod_ready, n * KF + f + 1)
                if f == 0 and not early(n, 2):
                    act.wait_ge(down_ready, n - 1)
                act.activation(h[HI][:, G % 2, f, :], h_raw[:, f % 2, :], ACT.Copy).then_inc(h_hi, 1)

            def step(e, slot, G):
                n = e * GROUPS + G
                silu(n, 0)
                for f in range(1, KF):
                    silu(n, f)
                    high(n, G, f - 1)
                high(n, G, KF - 1)
            for G in range(GROUPS):
                step(0, 0, G)
            with act.Fori(1, EXPERTS) as e:
                for G in range(GROUPS):
                    step(e, None, G)

        @block.vector
        def _(dve):
            x_row = lambda G: lambda i: X[:, G * GS + i, :]
            for G in range(GROUPS):
                norm_measure(dve, norm, G, x_row(G))
                if G > 0:
                    dve.wait_ge(tr_ready, G * KD)
                norm_apply(dve, norm, G, x_row(G), lambda i: z[:, i, :])
                for k in range(KD):
                    dve.wait_ge(xh_ready, G * KD + k + 1)
                    tokens = slice(G * GT, (G + 1) * GT)
                    dve.tensor_tensor(xn[LO][:, k, tokens], psum[6 + k][:, :], xn[HI][:, k, tokens].bitcast(F32),
                                      ALU.subtract).then_inc(xl_ready, 1)

            count = [0]

            def then(op):
                count[0] += 1
                op.then_inc(route_step, 1)
                dve.wait_ge(route_step, count[0])
            wide = lambda name: col[name][:, :].unsqueeze(2).broadcast_to([P, SEQS, EXPERTS])
            dve.wait_ge(logit_ready, 1)
            dve.wait_ge(iota_ready, 1)
            then(dve.tensor_copy(logit[:, :, :], psum[5][:, 0:SEQS * EXPERTS].rearrange("p (b e) -> p b e", b=SEQS)))
            then(dve.tensor_reduce(col["max"][:, :], logit[:, :, :], AX.X, ALU.max))
            dve.tensor_tensor(logit[:, :, :], logit[:, :, :], wide("max"), ALU.subtract).then_inc(route_exp, 1)
            dve.wait_ge(route_sem, 1)
            then(dve.tensor_reduce(col["sum"][:, :], prob[:, :, :], AX.X, ALU.add))
            then(dve.reciprocal(col["inv"][:, :], col["sum"][:, :]))
            then(dve.tensor_tensor(prob[:, :, :], prob[:, :, :], wide("inv"), ALU.mult))

            def largest(values, value, at, hot):
                then(dve.tensor_reduce(col[value][:, :], values[:, :, :], AX.X, ALU.max))
                then(dve.tensor_tensor(cand[:, :, :], values[:, :, :], wide(value), ALU.is_equal))
                then(dve.scalar_tensor_tensor(out=cand[:, :, :], in0=cand[:, :, :], scalar=-float(EXPERTS),
                                              in1=iota[:, :, :], op0=ALU.mult, op1=ALU.add))
                then(dve.tensor_reduce(col[at][:, :], cand[:, :, :], AX.X, ALU.min))
                then(dve.tensor_tensor(hot[:, :, :], cand[:, :, :], wide(at), ALU.is_equal))
            largest(prob, "p1", "at1", first_hot)
            then(dve.scalar_tensor_tensor(out=left[:, :, :], in0=first_hot[:, :, :], scalar=-4.0, in1=prob[:, :, :],
                                          op0=ALU.mult, op1=ALU.add))
            largest(left, "p2", "at2", second_hot)
            dve.tensor_tensor(col["gap"][:, :], col["p2"][:, :], col["p1"][:, :], ALU.subtract).then_inc(route_exp, 1)
            dve.wait_ge(route_sem, 2)
            then(dve.tensor_scalar(col["sum"][:, :], col["e"][:, :], 1.0, None, ALU.add))
            then(dve.reciprocal(col["w1"][:, :], col["sum"][:, :]))
            then(dve.tensor_tensor(col["w2"][:, :], col["e"][:, :], col["w1"][:, :], ALU.mult))
            then(dve.tensor_tensor(first_hot[:, :, :], first_hot[:, :, :], wide("w1"), ALU.mult))
            then(dve.tensor_tensor(second_hot[:, :, :], second_hot[:, :, :], wide("w2"), ALU.mult))
            then(dve.tensor_tensor(share[:, :, :], first_hot[:, :, :], second_hot[:, :, :], ALU.add))

            def fuse(e, slot, G):
                n = e * GROUPS + G
                for f in range(KF):
                    dve.wait_ge(silu_ready, n * KF + f + 1)
                    dve.wait_ge(up_ready, n * KF + f + 1)
                    if not early(n * KF + f, 2):
                        dve.wait_ge(h_hi, n * KF + f - 1)
                        dve.wait_ge(h_lo, n * KF + f - 1)
                    dve.tensor_tensor(h_raw[:, f % 2, :], gate[:, f % 2, :], UP[f % 2][:, :], ALU.mult).then_inc(prod_ready, 1)

            def add(e, slot, G):
                n = e * GROUPS + G
                dve.wait_ge(down_ready, n + 1)
                if not early(n, GROUPS):
                    dve.wait_ge(added, n * GS - (GROUPS - 1) * GS)
                for s in range(GS):
                    b = G * GS + s
                    dve.scalar_tensor_tensor(out=X[:, b, :], in0=DOWN(G, s // 2)[:, (s % 2) * D:(s % 2 + 1) * D],
                                             scalar=share[:, b, bass.ds(e, 1)], in1=X[:, b, :], op0=ALU.mult,
                                             op1=ALU.add).then_inc(added, 1)
            steps(dve, fuse, add)


MAGIC = 1.5 * 2.0 ** 23
INT8_MAX = 127.0


def stage_second_layer(nc, ctx, io, mem, out):
    X, ident, ident_bf, psum = mem["x"], mem["ident"], mem["ident_bf"], mem["psum"]
    sb = lambda name, shape, dt=F32: ctx.enter_context(nc.sbuf_tensor("l_" + name, shape, dt))
    sem = lambda name: mem["sems"]("l_" + name)
    pair = lambda name, shape: (sb(name + "_hi", shape, F32R), sb(name + "_lo", shape, F32R))
    norm_a, norm_c, norm_x, norm_q, norm_o, norm_f = (norm_state(nc, ctx, mem, "l" + n, GS) for n in "acxqof")
    shift = {id(n): (sb(f"shift{i}", [P, GS]), sb(f"neg_mean{i}", [P, GS]), sem(f"neg_mean_ready{i}"), sem(f"shift_ready{i}"))
             for i, n in enumerate((norm_a, norm_c, norm_o))}
    neg_one = sb("neg_one", [P, GS])
    neg_one_ready = sem("neg_one_ready")

    w_raw = sb("w_raw", [P, 3, KD * D])
    w = pair("w", [P, 3, KD * D])
    wq, wk, wv = (chunks_of(w, i, KD) for i in range(3))
    z = sb("z", [P, GS, D])
    xg = pair("xg", [P, KD, GT])
    q_t, k_t = sb("q_t", [P, KD, GT]), sb("k_t", [P, KD, GT])
    v = sb("v", [P, GS, D])
    prob, prob_t = sb("prob", [P, GS, P]), sb("prob_t", [P, GS, P])
    neg_max, total, inv = sb("neg_max", [P, GS]), sb("total", [P, GS]), sb("inv", [P, GS])
    w_loaded = [sem(f"w_loaded{i}") for i in range(3)]
    w_hi, w_split = sem("w_hi"), sem("w_split")
    tr_ready, xh_ready, xl_ready = sem("tr_ready"), sem("xh_ready"), sem("xl_ready")
    q_ready, k_ready, v_ready = sem("q_ready"), sem("k_ready"), sem("v_ready")
    q_copied, k_copied, v_copied = sem("q_copied"), sem("k_copied"), sem("v_copied")
    s_ready, max_ready, exp_ready = sem("s_ready"), sem("max_ready"), sem("exp_ready")
    pt_ready, pt_copied = sem("pt_ready"), sem("pt_copied")
    o_ready, inv_ready, added = sem("o_ready"), sem("inv_ready"), sem("added")

    context = sb("context", [P, 2, GS, D])
    gains = sb("gains", [P, 4, KD])
    scaled = sb("scaled", [P, 2, KD])
    factor, inv_factor = sb("factor", [P, 1]), sb("inv_factor", [P, 1])
    rows = sb("rows", [P, 4, D])
    z1, z2, cn = sb("z1", [P, GS, D]), sb("z2", [P, GS, D]), sb("cn", [P, GS, D])
    cq_t, ck_t = sb("cq_t", [P, KD, GT]), sb("ck_t", [P, 2, KD, GT])
    cv = sb("cv", [P, 2, GS, D])
    vg = sb("vg", [P, GS, D])
    cprob, cprob_t = sb("cprob", [P, GS, P]), sb("cprob_t", [P, GS, P])
    cneg_max, ctotal, cinv = sb("cneg_max", [P, GS]), sb("ctotal", [P, GS]), sb("cinv", [P, GS])
    o, oz, og, ob = (sb(n, [P, GS, D]) for n in ("o", "oz", "og", "ob"))
    c_loaded = [sem(f"c_loaded{i}") for i in range(2)]
    p_loaded = sem("p_loaded")
    inv_factor_ready, scaled_ready = sem("inv_factor_ready"), sem("scaled_ready")
    qtr_ready, ktr_ready = sem("qtr_ready"), sem("ktr_ready")
    cq_ready, ck_ready, vg_ready, cv_ready = sem("cq_ready"), sem("ck_ready"), sem("vg_ready"), sem("cv_ready")
    cs_ready, cmax_ready, cexp_ready = sem("cs_ready"), sem("cmax_ready"), sem("cexp_ready")
    cpt_ready, cpt_copied = sem("cpt_ready"), sem("cpt_copied")
    co_ready, cinv_ready, co_scaled = sem("co_ready"), sem("cinv_ready"), sem("co_scaled")
    og_ready, ob_ready, x_ready = sem("og_ready"), sem("ob_ready"), sem("x_ready")
    wide = lambda i: rows[:, i, :].unsqueeze(1).broadcast_to([P, GS, D])

    zf, t1, t2 = (sb(n, [P, GS, D]) for n in ("zf", "t1", "t2"))
    zq = sb("zq", [P, GS, D], BF16)
    xq_t = sb("xq_t", [P, GS * KD, P], BF16)
    amax, scale, inv_scale = (sb(n, [P, 2, GS]) for n in ("amax", "scale", "inv_scale"))
    product_out = sb("product_out", [P, 2, GS, D])
    wf, wt1, wt2 = (sb(n, [P, KD, D]) for n in ("wf", "wt1", "wt2"))
    wfq = sb("wfq", [P, KD, D], BF16)
    wfq_t = sb("wfq_t", [P, KD, D], BF16)
    w_amax, w_scale, w_inv = (sb(n, [P, KD]) for n in ("w_amax", "w_scale", "w_inv"))
    ones = sb("ones", [P, P])
    diag = sb("diag", [P, KD, P])
    col_scale = sb("col_scale", [P, D])
    wf_loaded, ones_ready, w_step = sem("wf_loaded"), sem("ones_ready"), sem("w_step")
    wtr_ready, wt_ready, scales_ready, col_scale_ready = (sem(n) for n in (
        "wtr_ready", "wt_ready", "scales_ready", "col_scale_ready"))
    q_step, rounded, quantised = sem("q_step"), sem("rounded"), sem("quantised")
    ftr_ready, ftr_copied, fy_ready, fy_scaled, fx_ready = (sem(n) for n in (
        "ftr_ready", "ftr_copied", "fy_ready", "fy_scaled", "fx_ready"))
    stored = sem("stored")

    TR = K = psum[0:2]
    S, PT = psum[0], psum[1]
    Q = V = O = psum[2:4]
    CT = CO = psum[4:6]
    CS, CPT = psum[6], psum[7]
    FT, FY = psum[6], psum[6:8]

    (MEASURE, TURN, PROJECT, VALUES, SCORES, PROBS, ADD,
     MEASURE_X, MEASURE_Q, TURN_Q, CSCORES, CPROBS, COUT, MEASURE_O, CADD,
     MEASURE_F, SCALE_F, QUANTISE, MULTIPLY, STORE, PHASES) = range(21)
    MEASURE_C, NORM_C, TURN_C = VALUES, SCORES, PROBS
    APART = 5
    SETUP, SETUP_TURN = 3, 4

    def schedule():
        for step in range(APART * (GROUPS - 1) + PHASES):
            for G in range(GROUPS):
                if 0 <= step - APART * G < PHASES:
                    yield step, step - APART * G, G

    x_rows = lambda G: lambda i: X[:, G * GS + i, :]
    c_rows = lambda G: lambda i: context[:, G % 2, i, :]

    def invert_and_shift(pool, norm, G):
        to, neg_mean, neg_mean_ready, shift_ready = shift[id(norm)]
        pool.wait_ge(norm["var_ready"], G + 1)
        pool.tensor_tensor(neg_mean[:, :], norm["mv"][:, :, 0], neg_one[:, :], ALU.mult).then_inc(neg_mean_ready, 1)
        norm_invert(pool, norm, G)
        pool.wait_ge(norm["rstd_ready"], G + 1)
        pool.wait_ge(neg_mean_ready, G + 1)
        pool.tensor_tensor(to[:, :], neg_mean[:, :], norm["ve"][:, :], ALU.mult).then_inc(shift_ready, 1)

    def apply_on_act(act, norm, G, rows, outs):
        to, _, _, shift_ready = shift[id(norm)]
        act.wait_ge(shift_ready, G + 1)
        for i in range(GS):
            act.activation(outs(i), rows(i), ACT.Identity, bias=to[:, i:i + 1],
                           scale=norm["ve"][:, i:i + 1]).then_inc(norm["z_ready"], 1)

    with nc.Block() as block:
        @block.sync
        def _(sp):
            for i, name in enumerate(("Wq", "Wk", "Wv")):
                sp.dma_start(w_raw[:, i, :], io["L1_attn_" + name + "_laid"]).then_inc(w_loaded[i], 16)
            load_context = lambda G: sp.dma_start(context[:, G % 2, :, :], io["ctx_1024"][G * GS:(G + 1) * GS].rearrange(
                "b t d -> t b d")).then_inc(c_loaded[G % 2], 16)
            sp.dma_start(wf[:, :, :], io["rhs_laid"]).then_inc(wf_loaded, 16)
            load_context(0)
            sp.dma_start(gains[:, :, :], io["qk_gains_laid"]).then_inc(p_loaded, 16)
            sp.dma_start(factor[:, :], io["L1_xattn_inv_scale_factor"].broadcast_to([P, 1])).then_inc(p_loaded, 16)
            for i, name in enumerate(("ln3_w", "ln3_b", "ln4_w", "ln4_b")):
                sp.dma_start(rows[:, i, :], io["L1_xattn_" + name].unsqueeze(0).broadcast_to([P, D])).then_inc(p_loaded, 16)
            load_context(1)
            for G in range(2, GROUPS):
                sp.wait_ge(norm_c["z_ready"], (G - 1) * GS)
                load_context(G)
            for G in range(GROUPS):
                sp.wait_ge(fx_ready, G + 1)
                sp.dma_start(out[G * GS:(G + 1) * GS].rearrange("b t d -> t b d"),
                             X[:, G * GS:(G + 1) * GS, :]).then_inc(stored, 16)
            sp.wait_ge(stored, 16 * GROUPS)

        @block.gpsimd
        def _(pool):
            pool.memset(neg_one[:, :], -1.0).then_inc(neg_one_ready, 1)
            pool.wait_ge(neg_one_ready, 1)
            pool.memset(ones[:, :], 1.0).then_inc(ones_ready, 1)
            for step, phase, G in schedule():
                if phase == MEASURE:
                    invert_and_shift(pool, norm_a, G)
                    if G == 0:
                        for i in range(3):
                            pool.wait_ge(w_hi, i + 1)
                            pool.tensor_tensor(w[LO][:, i, :], w_raw[:, i, :], w[HI][:, i, :].bitcast(F32),
                                               ALU.subtract).then_inc(w_split, 1)
                elif phase == MEASURE_C:
                    invert_and_shift(pool, norm_c, G)
                elif phase == TURN_C:
                    if G == 0:
                        pool.wait_ge(p_loaded, 96)
                    pool.wait_ge(norm_c["z_ready"], G * GS + GS)
                    pool.tensor_tensor(vg[:, :, :], cn[:, :, :], wide(0), ALU.mult).then_inc(vg_ready, 1)
                    pool.wait_ge(vg_ready, G + 1)
                    if G >= 2:
                        pool.wait_ge(co_ready, G - 1)
                    pool.tensor_tensor(cv[:, G % 2, :, :], vg[:, :, :], wide(1), ALU.add).then_inc(cv_ready, 1)
                elif phase == MEASURE_X:
                    norm_invert(pool, norm_x, G)
                elif phase == MEASURE_Q:
                    norm_invert(pool, norm_q, G)
                elif phase == MEASURE_O:
                    invert_and_shift(pool, norm_o, G)
                elif phase == CADD:
                    pool.wait_ge(norm_o["z_ready"], G * GS + GS)
                    pool.tensor_tensor(og[:, :, :], oz[:, :, :], wide(2), ALU.mult).then_inc(og_ready, 1)
                    pool.wait_ge(og_ready, G + 1)
                    pool.tensor_tensor(ob[:, :, :], og[:, :, :], wide(3), ALU.add).then_inc(ob_ready, 1)
                    pool.wait_ge(ob_ready, G + 1)
                    group = X[:, G * GS:(G + 1) * GS, :]
                    pool.tensor_tensor(group, group, ob[:, :, :], ALU.add).then_inc(x_ready, 1)
                elif phase == MEASURE_F:
                    norm_invert(pool, norm_f, G)
                elif phase == STORE:
                    pool.wait_ge(fy_scaled, (G + 1) * GS)
                    group = X[:, G * GS:(G + 1) * GS, :]
                    pool.tensor_tensor(group, group, product_out[:, G % 2, :, :], ALU.add).then_inc(fx_ready, 1)

        @block.tensor
        def _(pe):
            def turn(banks, rows, ready):
                for k in range(KD):
                    for s in range(GS):
                        tr = pe.transpose(banks[k][:, s * P:(s + 1) * P], rows[:, s, k * P:(k + 1) * P], ident[:, :])
                    tr.then_inc(ready, 1)

            def scores(bank, qs, ks, ready):
                for s in range(GS):
                    t = slice(s * P, (s + 1) * P)
                    for k in range(KD):
                        mm = pe.matmul(bank[:, t], qs[:, k, t], ks[:, k, t], start=(k == 0), stop=(k == KD - 1))
                mm.then_inc(ready, 1)

            def turn_probs(bank, probs, ready):
                for s in range(GS):
                    tr = pe.transpose(bank[:, s * P:(s + 1) * P], probs[:, s, :], ident[:, :])
                tr.then_inc(ready, 1)

            def outputs(banks, probs_t, vs, ready):
                for s in range(GS):
                    mm = pe.matmul(banks[s // 2][:, (s % 2) * D:(s % 2 + 1) * D], probs_t[:, s, :], vs[:, s, :],
                                   start=True, stop=True)
                mm.then_inc(ready, 1)

            def project(banks, weights, ready):
                for k in range(KD):
                    for j in range(KD):
                        mm = product(pe, banks[k][:, :], [x[:, j, k * P:(k + 1) * P] for x in weights],
                                     [x[:, j, :] for x in xg], j == 0, j == KD - 1)
                    mm.then_inc(ready, 1)

            done = set()
            for step, phase, G in schedule():
                if step == SETUP_TURN and step not in done:
                    done.add(step)
                    pe.wait_ge(w_step, 5 + KD)
                    for c in range(KD):
                        for k in range(KD):
                            tr = pe.transpose(CS[:, :].bitcast(BF16)[:, k * D + c * P:k * D + (c + 1) * P],
                                              wfq[:, c, k * P:(k + 1) * P], ident_bf[:, :])
                    tr.then_inc(wtr_ready, 1)
                    pe.wait_ge(ones_ready, 1)
                    pe.wait_ge(w_step, 5 + 2 * KD)
                    for c in range(KD):
                        mm = pe.matmul(CPT[:, c * P:(c + 1) * P], ones[:, :], diag[:, c, :], start=True, stop=True)
                    mm.then_inc(scales_ready, 1)
                if phase == TURN:
                    pe.wait_ge(norm_a["z_ready"], G * GS + GS)
                    if G > 0:
                        pe.wait_ge(pt_copied, G)
                    turn(TR, z, tr_ready)
                elif phase == PROJECT:
                    pe.wait_ge(xl_ready, G * KD + KD)
                    if G == 0:
                        pe.wait_ge(w_split, 1)
                    else:
                        pe.wait_ge(added, G * GS)
                    project(Q, wq, q_ready)
                    if G == 0:
                        pe.wait_ge(w_split, 2)
                    project(K, wk, k_ready)
                elif phase == VALUES:
                    if G == 0:
                        pe.wait_ge(w_split, 3)
                    pe.wait_ge(q_copied, G * KD + KD)
                    for h in range(2):
                        for s in (2 * h, 2 * h + 1):
                            for j in range(KD):
                                mm = product(pe, V[h][:, (s % 2) * D:(s % 2 + 1) * D],
                                             [x[:, j, s * P:(s + 1) * P] for x in xg], [x[:, j, :] for x in wv],
                                             j == 0, j == KD - 1)
                        mm.then_inc(v_ready, 1)
                elif phase == SCORES:
                    pe.wait_ge(k_copied, G * KD + KD)
                    scores(S, q_t, k_t, s_ready)
                elif phase == PROBS:
                    pe.wait_ge(exp_ready, G + 1)
                    turn_probs(PT, prob, pt_ready)
                    pe.wait_ge(norm_c["z_ready"], G * GS + GS)
                    if G > 0:
                        pe.wait_ge(cq_ready, G * KD)
                    turn(CT, cn, ktr_ready)
                elif phase == ADD:
                    pe.wait_ge(pt_copied, G + 1)
                    pe.wait_ge(v_copied, G * 2 + 2)
                    outputs(O, prob_t, v, o_ready)
                elif phase == TURN_Q:
                    pe.wait_ge(norm_q["z_ready"], G * GS + GS)
                    pe.wait_ge(ck_ready, G * KD + KD)
                    if G > 0:
                        pe.wait_ge(co_scaled, 2 * G)
                    turn(CT, z2, qtr_ready)
                elif phase == CSCORES:
                    if G == 0:
                        pe.wait_ge(wt_ready, 1)
                        pe.wait_ge(col_scale_ready, 1)
                    if G >= 2:
                        pe.wait_ge(fy_scaled, (G - 1) * GS)
                    pe.wait_ge(cq_ready, G * KD + KD)
                    scores(CS, cq_t, ck_t[:, G % 2, :, :], cs_ready)
                elif phase == CPROBS:
                    pe.wait_ge(cexp_ready, G + 1)
                    turn_probs(CPT, cprob, cpt_ready)
                elif phase == COUT:
                    pe.wait_ge(cpt_copied, G + 1)
                    pe.wait_ge(cv_ready, G + 1)
                    if G + 1 < GROUPS:
                        pe.wait_ge(ck_ready, (G + 1) * KD + KD)
                    outputs(CO, cprob_t, cv[:, G % 2, :, :], co_ready)
                elif phase == QUANTISE:
                    pe.wait_ge(quantised, G + 1)
                    if G > 0:
                        pe.wait_ge(fy_scaled, G * GS)
                    for s in range(GS):
                        for k in range(KD):
                            i = s * KD + k
                            tr = pe.transpose(FT[:, :].bitcast(BF16)[:, i * P:(i + 1) * P], zq[:, s, k * P:(k + 1) * P],
                                              ident_bf[:, :])
                    tr.then_inc(ftr_ready, 1)
                elif phase == MULTIPLY:
                    pe.wait_ge(ftr_copied, G + 1)
                    for s in range(GS):
                        for k in range(KD):
                            mm = pe.matmul(FY[s // 2][:, (s % 2) * D:(s % 2 + 1) * D], xq_t[:, s * KD + k, :],
                                           wfq_t[:, k, :], start=(k == 0), stop=(k == KD - 1))
                    mm.then_inc(fy_ready, 1)

        @block.scalar
        def _(act):
            def exponentials(bank, probs, maxima, sums, ready):
                for s in range(GS):
                    e = act.activation(probs[:, s, :], bank[:, s * P:(s + 1) * P], ACT.Exp, bias=maxima[:, s:s + 1],
                                       accum_out=sums[:, s:s + 1])
                e.then_inc(ready, 1)

            for i in range(3):
                act.wait_ge(w_loaded[i], 16)
                act.activation(w[HI][:, i, :], w_raw[:, i, :], ACT.Copy).then_inc(w_hi, 1)
            done = set()
            for step, phase, G in schedule():
                if step == SETUP_TURN and step not in done:
                    done.add(step)
                    act.wait_ge(wtr_ready, 1)
                    act.activation(wfq_t[:, :, :], CS[:, :].bitcast(BF16)[:, 0:KD * D].rearrange("p (k n) -> p k n", k=KD),
                                   ACT.Copy).then_inc(wt_ready, 1)
                    act.wait_ge(scales_ready, 1)
                    act.activation(col_scale[:, :], CPT[:, 0:D], ACT.Copy).then_inc(col_scale_ready, 1)
                if phase == TURN:
                    if G > 0:
                        act.wait_ge(tr_ready, G * KD)
                    apply_on_act(act, norm_a, G, x_rows(G), lambda i: z[:, i, :])
                    for k in range(KD):
                        act.wait_ge(tr_ready, G * KD + k + 1)
                        act.activation(xg[HI][:, k, :], TR[k][:, :], ACT.Copy).then_inc(xh_ready, 1)
                elif phase == PROJECT:
                    for k in range(KD):
                        act.wait_ge(q_ready, G * KD + k + 1)
                        act.activation(q_t[:, k, :], Q[k][:, :], ACT.Copy, scale=D ** -0.5).then_inc(q_copied, 1)
                elif phase == VALUES:
                    for h in range(2):
                        act.wait_ge(v_ready, G * 2 + h + 1)
                        act.activation(v[:, 2 * h:2 * h + 2, :], V[h][:, :].rearrange("p (s d) -> p s d", s=2),
                                       ACT.Copy).then_inc(v_copied, 1)
                elif phase == SCORES:
                    act.wait_ge(max_ready, G + 1)
                    exponentials(S, prob, neg_max, total, exp_ready)
                    if G > 0:
                        act.wait_ge(ktr_ready, G * KD)
                        act.wait_ge(vg_ready, G)
                    apply_on_act(act, norm_c, G, c_rows(G), lambda i: cn[:, i, :])
                elif phase == PROBS:
                    act.wait_ge(pt_ready, G + 1)
                    act.activation(prob_t[:, :, :], PT[:, :].rearrange("p (s k) -> p s k", s=GS), ACT.Copy).then_inc(pt_copied, 1)
                    if G == 0:
                        act.wait_ge(scaled_ready, 1)
                    for k in range(KD):
                        act.wait_ge(ktr_ready, G * KD + k + 1)
                        act.activation(ck_t[:, G % 2, k, :], CT[k][:, :], ACT.Identity, bias=gains[:, 3, k:k + 1],
                                       scale=gains[:, 2, k:k + 1]).then_inc(ck_ready, 1)
                elif phase == TURN_Q:
                    for k in range(KD):
                        act.wait_ge(qtr_ready, G * KD + k + 1)
                        act.activation(cq_t[:, k, :], CT[k][:, :], ACT.Identity, bias=scaled[:, 1, k:k + 1],
                                       scale=scaled[:, 0, k:k + 1]).then_inc(cq_ready, 1)
                elif phase == CSCORES:
                    act.wait_ge(cmax_ready, G + 1)
                    exponentials(CS, cprob, cneg_max, ctotal, cexp_ready)
                elif phase == CPROBS:
                    act.wait_ge(cpt_ready, G + 1)
                    act.activation(cprob_t[:, :, :], CPT[:, :].rearrange("p (s k) -> p s k", s=GS), ACT.Copy).then_inc(cpt_copied, 1)
                elif phase == CADD:
                    if G > 0:
                        act.wait_ge(og_ready, G)
                    apply_on_act(act, norm_o, G, lambda i: o[:, i, :], lambda i: oz[:, i, :])
                elif phase == MULTIPLY:
                    act.wait_ge(ftr_ready, G + 1)
                    act.activation(xq_t[:, :, :], FT[:, :].bitcast(BF16).rearrange("p (i t) -> p i t", t=P),
                                   ACT.Copy).then_inc(ftr_copied, 1)

        @block.vector
        def _(dve):
            def maxima(bank, to, ready):
                dve.tensor_reduce(to[:, :], bank[:, :].rearrange("p (s k) -> p s k", s=GS), AX.X, ALU.max,
                                  negate=True).then_inc(ready, 1)

            count = [0]

            def then(op):
                count[0] += 1
                op.then_inc(w_step, 1)
                dve.wait_ge(w_step, count[0])

            def setup():
                dve.wait_ge(wf_loaded, 16)
                then(dve.tensor_reduce(w_amax[:, :], wf[:, :, :], AX.X, ALU.max, apply_absolute_value=True))
                then(dve.tensor_scalar(w_scale[:, :], w_amax[:, :], 1e-12, 1.0 / INT8_MAX, ALU.max, ALU.mult))
                then(dve.reciprocal(w_inv[:, :], w_scale[:, :]))
                for c in range(KD):
                    then(dve.tensor_scalar(wt1[:, c, :], wf[:, c, :], w_inv[:, c:c + 1], MAGIC, ALU.mult, ALU.add))
                then(dve.tensor_scalar(wt2[:, :, :], wt1[:, :, :], -MAGIC, INT8_MAX, ALU.add, ALU.min))
                then(dve.tensor_scalar(wfq[:, :, :], wt2[:, :, :], -INT8_MAX, None, ALU.max))
                for c in range(KD):
                    then(dve.tensor_scalar(diag[:, c, :], ident[:, :], w_scale[:, c:c + 1], None, ALU.mult))
                dve.wait_ge(p_loaded, 96)
                dve.reciprocal(inv_factor[:, :], factor[:, :]).then_inc(inv_factor_ready, 1)
                dve.wait_ge(inv_factor_ready, 1)
                dve.tensor_scalar(scaled[:, :, :], gains[:, 0:2, :], inv_factor[:, 0:1], None, ALU.mult).then_inc(scaled_ready, 1)

            done = set()
            for step, phase, G in schedule():
                par = G % 2
                if step == SETUP and step not in done:
                    done.add(step)
                    setup()
                if phase == MEASURE:
                    norm_measure(dve, norm_a, G, x_rows(G))
                elif phase == PROJECT:
                    for k in range(KD):
                        dve.wait_ge(xh_ready, G * KD + k + 1)
                        dve.tensor_tensor(xg[LO][:, k, :], TR[k][:, :], xg[HI][:, k, :].bitcast(F32),
                                          ALU.subtract).then_inc(xl_ready, 1)
                elif phase == VALUES:
                    for k in range(KD):
                        dve.wait_ge(k_ready, G * KD + k + 1)
                        dve.tensor_copy(k_t[:, k, :], K[k][:, :]).then_inc(k_copied, 1)
                    dve.wait_ge(c_loaded[par], 16 * (G // 2) + 16)
                    norm_measure(dve, norm_c, G, c_rows(G))
                elif phase == SCORES:
                    dve.wait_ge(s_ready, G + 1)
                    maxima(S, neg_max, max_ready)
                elif phase == PROBS:
                    dve.wait_ge(exp_ready, G + 1)
                    dve.reciprocal(inv[:, :], total[:, :]).then_inc(inv_ready, 1)
                elif phase == ADD:
                    dve.wait_ge(inv_ready, G + 1)
                    dve.wait_ge(o_ready, G + 1)
                    for s in range(GS):
                        b = G * GS + s
                        dve.scalar_tensor_tensor(out=X[:, b, :], in0=O[s // 2][:, (s % 2) * D:(s % 2 + 1) * D],
                                                 scalar=inv[:, s:s + 1], in1=X[:, b, :], op0=ALU.mult,
                                                 op1=ALU.add).then_inc(added, 1)
                elif phase == MEASURE_X:
                    dve.wait_ge(added, (G + 1) * GS)
                    norm_measure(dve, norm_x, G, x_rows(G))
                elif phase == MEASURE_Q:
                    norm_apply(dve, norm_x, G, x_rows(G), lambda i: z1[:, i, :])
                    dve.wait_ge(norm_x["z_ready"], G * GS + GS)
                    norm_measure(dve, norm_q, G, lambda i: z1[:, i, :])
                elif phase == TURN_Q:
                    if G > 0:
                        dve.wait_ge(qtr_ready, G * KD)
                    norm_apply(dve, norm_q, G, lambda i: z1[:, i, :], lambda i: z2[:, i, :])
                elif phase == CSCORES:
                    dve.wait_ge(cs_ready, G + 1)
                    maxima(CS, cneg_max, cmax_ready)
                elif phase == CPROBS:
                    dve.wait_ge(cexp_ready, G + 1)
                    dve.reciprocal(cinv[:, :], ctotal[:, :]).then_inc(cinv_ready, 1)
                elif phase == COUT:
                    dve.wait_ge(cinv_ready, G + 1)
                    dve.wait_ge(co_ready, G + 1)
                    if G > 0:
                        dve.wait_ge(norm_o["z_ready"], G * GS)
                    for h in range(2):
                        dve.tensor_tensor(o[:, 2 * h:2 * h + 2, :], CO[h][:, :].rearrange("p (s d) -> p s d", s=2),
                                          cinv[:, 2 * h:2 * h + 2].unsqueeze(2).broadcast_to([P, 2, D]),
                                          ALU.mult).then_inc(co_scaled, 1)
                elif phase == MEASURE_O:
                    dve.wait_ge(co_scaled, 2 * G + 2)
                    norm_measure(dve, norm_o, G, lambda i: o[:, i, :])
                elif phase == MEASURE_F:
                    dve.wait_ge(x_ready, G + 1)
                    norm_measure(dve, norm_f, G, x_rows(G))
                elif phase == SCALE_F:
                    norm_apply(dve, norm_f, G, x_rows(G), lambda i: zf[:, i, :])
                    dve.wait_ge(norm_f["z_ready"], G * GS + GS)
                    base = G * (3 + GS)
                    dve.tensor_reduce(amax[:, par, :], zf[:, :, :], AX.X, ALU.max, apply_absolute_value=True).then_inc(q_step, 1)
                    dve.wait_ge(q_step, base + 1)
                    dve.tensor_scalar(scale[:, par, :], amax[:, par, :], 1e-12, 1.0 / INT8_MAX, ALU.max, ALU.mult).then_inc(q_step, 1)
                    dve.wait_ge(q_step, base + 2)
                    dve.reciprocal(inv_scale[:, par, :], scale[:, par, :]).then_inc(q_step, 1)
                elif phase == QUANTISE:
                    base = G * (3 + GS)
                    dve.wait_ge(q_step, base + 3)
                    for i in range(GS):
                        dve.tensor_scalar(t1[:, i, :], zf[:, i, :], inv_scale[:, par, i:i + 1], MAGIC, ALU.mult, ALU.add).then_inc(q_step, 1)
                    dve.wait_ge(q_step, base + 3 + GS)
                    dve.tensor_scalar(t2[:, :, :], t1[:, :, :], -MAGIC, INT8_MAX, ALU.add, ALU.min).then_inc(rounded, 1)
                    dve.wait_ge(rounded, G + 1)
                    if G > 0:
                        dve.wait_ge(ftr_ready, G)
                    dve.tensor_scalar(zq[:, :, :], t2[:, :, :], -INT8_MAX, None, ALU.max).then_inc(quantised, 1)
                elif phase == STORE:
                    dve.wait_ge(fy_ready, G + 1)
                    if G >= 2:
                        dve.wait_ge(fx_ready, G - 1)
                    for s in range(GS):
                        dve.scalar_tensor_tensor(out=product_out[:, par, s, :], in0=FY[s // 2][:, (s % 2) * D:(s % 2 + 1) * D],
                                                 scalar=scale[:, par, s:s + 1], in1=col_scale[:, :], op0=ALU.mult,
                                                 op1=ALU.mult).then_inc(fy_scaled, 1)


def clear_semaphores(nc, handles):
    with nc.Block() as block:
        @block.gpsimd
        def _(pool):
            for handle in handles:
                pool.sem_clear(handle)


def decoder(nc, io, out):
    ctx = ExitStack()
    with ctx:
        sb = lambda name, shape, dt=F32: ctx.enter_context(nc.sbuf_tensor(name, shape, dt))
        sem = lambda name: ctx.enter_context(nc.semaphore(name))

        mem = {"psum": [ctx.enter_context(nc.psum_tensor(f"bank{i}", [P, BANK], F32)) for i in range(8)]}
        mem["sems"] = sem
        mem["x"] = sb("x_res", [P, SEQS, D])
        mem["ident"] = sb("ident", [P, P])
        mem["ident_bf"] = sb("ident_bf", [P, P], BF16)
        mem["causal"] = sb("causal", [P, P], BF16)
        mem["neghalf"] = sb("neghalf", [P, SEQS])
        mem["stats"] = sb("stats", [P, SEQS, 6])
        mem["mv"] = sb("mv", [P, SEQS, 2])
        mem["ve"] = sb("ve", [P, SEQS])
        attn_ctx = ExitStack()
        asb = lambda name, shape, dt=F32: attn_ctx.enter_context(nc.sbuf_tensor(name, shape, dt))
        mem["act"] = asb("act", [P, SEQS, D])
        mem["act_t"] = asb("act_t", [P, KD, SEQS * P])
        mem["attn_w"] = (asb("attn_w_hi", [P, 4, KD * WIDE], F32R), asb("attn_w_lo", [P, 4, KD * WIDE], F32R))
        mem["attn_g"], mem["attn_b"] = asb("attn_g", [P, D]), asb("attn_b", [P, D])
        for name in ("attn_w_loaded", "attn_w_split", "attn_ln_loaded"):
            mem[name] = sem(name)
        with ExitStack() as ssm_ctx:
            mem["attn_raw"] = ssm_ctx.enter_context(nc.sbuf_tensor("attn_raw", [P, KD * WIDE], F32))
            ssb = lambda name, shape: ssm_ctx.enter_context(nc.sbuf_tensor(name, shape, F32))
            w_in = mem["w_in"] = ssb("w_in", [P, KD, PROJ])
            w_out = mem["w_out"] = ssb("w_out", [P, KI, D])
            conv_w = mem["conv_w"] = ssb("conv_w", [P, KI, TAPS])
            conv_b = mem["conv_b"] = ssb("conv_b", [P, KI])
            ln_g = mem["ln_g"] = ssb("ln_g", [P, D])
            ln_b = mem["ln_b"] = ssb("ln_b", [P, D])
            decay = mem["decay"] = ssb("decay", [P, P])
            names = mem["ssm_sems"] = {k: sem("s_" + k) for k in (
                "w_in_loaded", "w_out_loaded", "conv_loaded", "ln_loaded", "decay_loaded")}

            def one(ap, layer):
                return ap[layer] if isinstance(layer, int) else ap[bass.ds(layer, 1)]

            def load_w_in(sp, layer):
                sp.dma_start(w_in[:, :, :], io["L0_attn_in_proj_w"][bass.ds(layer, 1)].rearrange(
                    "l (k p) n -> p (l k) n", p=P)).then_inc(names["w_in_loaded"], 16)

            def load_w_out(sp, layer):
                sp.dma_start(w_out[:, :, :], io["L0_attn_out_proj_w"][bass.ds(layer, 1)].rearrange(
                    "l (k p) n -> p (l k) n", p=P)).then_inc(names["w_out_loaded"], 16)

            def load_conv(sp, layer):
                sp.dma_start(conv_w[:, :, :], io["conv_w_laid"][bass.ds(layer, 1)].rearrange(
                    "l p c t -> p (l c) t")).then_inc(names["conv_loaded"], 16)
                sp.dma_start(conv_b[:, :], io["conv_b_laid"][bass.ds(layer, 1)].rearrange(
                    "l p c -> p (l c)")).then_inc(names["conv_loaded"], 16)

            def load_ln(sp, layer):
                for tile, name in ((ln_g, "L0_attn_ssm_ln_g"), (ln_b, "L0_attn_ssm_ln_b")):
                    sp.dma_start(tile[:, :], io[name][bass.ds(layer, 1), :].broadcast_to([P, D])).then_inc(
                        names["ln_loaded"], 16)

            def prefetch_ssm(sp):
                load_w_in(sp, 0)
                load_conv(sp, 0)
                sp.dma_start(decay[:, :], io["decay"]).then_inc(names["decay_loaded"], 16)
                load_w_out(sp, 0)
                load_ln(sp, 0)
            mem.update(load_w_in=load_w_in, load_w_out=load_w_out, load_conv=load_conv, load_ln=load_ln,
                       prefetch_ssm=prefetch_ssm, prefetch_attn=lambda sp: None)
            stage_load_and_norm(nc, ctx, io, mem)
            stage_ssm(nc, ssm_ctx, io, mem)

        def run(stage, stage_ctx):
            handles = []

            def stage_sem(name):
                handles.append(stage_ctx.enter_context(nc.semaphore(name)))
                return handles[-1]
            mem["sems"] = stage_sem
            stage(nc, stage_ctx, io, mem)
            clear_semaphores(nc, handles)
        with attn_ctx:
            run(stage_self_attention, attn_ctx)
        for stage in (stage_cross_attention, stage_experts):
            with ExitStack() as stage_ctx:
                run(stage, stage_ctx)
        with ExitStack() as stage_ctx:
            mem["sems"] = lambda name: stage_ctx.enter_context(nc.semaphore(name))
            stage_second_layer(nc, stage_ctx, io, mem, out)


def kernel(**inputs):
    import numpy as np
    import concourse.bacc as bacc
    from concourse.bass_utils import run_bass_kernel_spmd

    nc = bacc.Bacc("TRN2", target_bir_lowering=False, num_devices=1)
    laid = {name: np.ascontiguousarray(a) for name, a in inputs.items()}
    laid["conv_w_laid"] = np.ascontiguousarray(laid.pop("L0_attn_conv_w").reshape(SSM_LAYERS, KI, P, TAPS).transpose(0, 2, 1, 3))
    laid["conv_b_laid"] = np.ascontiguousarray(laid.pop("L0_attn_conv_b").reshape(SSM_LAYERS, KI, P).transpose(0, 2, 1))
    laid["attn_w_laid"] = np.stack([laid.pop(f"L0_attn_{w}").reshape(k, P, -1).transpose(1, 0, 2).reshape(P, -1)
                                    for w, k in (("wq", KD), ("wk", KD), ("wv", KD), ("wo", KW))])
    feature_rows = lambda a: a.reshape(-1, P, a.shape[-1]).transpose(1, 0, 2).reshape(P, -1)
    for name in ("W_q", "W_k", "W_v", "W_o"):
        laid[f"L0_xattn_{name}_laid"] = np.ascontiguousarray(feature_rows(laid.pop("L0_xattn_" + name).T))
    for name in ("b_q", "b_k"):
        laid[f"L0_xattn_{name}_laid"] = np.ascontiguousarray(laid.pop("L0_xattn_" + name).reshape(KD, P).T)
    laid["router_laid"] = np.ascontiguousarray(feature_rows(laid.pop("L0_ffn_router_kernel_DE")))
    laid["experts_laid"] = np.stack([np.concatenate(
        [feature_rows(laid[f"L0_ffn_kernel_{w}"][e]) for w in ("gating_EDF", "up_EDF", "down_EFD")], axis=1)
        for e in range(EXPERTS)])
    for w in ("gating_EDF", "up_EDF", "down_EFD"):
        del laid[f"L0_ffn_kernel_{w}"]
    for name in ("Wq", "Wk", "Wv"):
        laid[f"L1_attn_{name}_laid"] = np.ascontiguousarray(feature_rows(laid.pop("L1_attn_" + name).T))
    laid["qk_gains_laid"] = np.ascontiguousarray(np.stack(
        [laid.pop("L1_xattn_" + name).reshape(KD, P).T for name in ("ln1_w", "ln1_b", "ln2_w", "ln2_b")], axis=1))
    laid["rhs_laid"] = np.ascontiguousarray(laid.pop("L1_ffn_rhs").T.reshape(KD, P, D).transpose(1, 0, 2))
    laid["ctx_t_laid"] = np.ascontiguousarray(laid["ctx_1024"].reshape(SEQS * P, KD, P).transpose(2, 1, 0))
    steps = np.arange(P)[None, :] - np.arange(P)[:, None]
    laid["decay"] = np.where(steps >= 0, np.float64(-0.5) ** np.maximum(steps, 0), 0.0).astype(np.float32)
    io = {name: nc.dram_tensor(f"in_{name}", a.shape, mybir.dt.from_np(a.dtype), kind="ExternalInput").ap()
          for name, a in laid.items()}
    out = nc.dram_tensor("out_x", (SEQS, P, D), F32, kind="ExternalOutput").ap()
    decoder(nc, io, out)
    ran = run_bass_kernel_spmd(nc, [{f"in_{name}": a for name, a in laid.items()}], core_ids=[0])
    return ran.results[0]["out_x"]
```

```python
from contextlib import ExitStack

import concourse.bass as bass
from concourse import mybir

F32 = mybir.dt.float32
F32R = mybir.dt.float32r
BF16 = mybir.dt.bfloat16
I32 = mybir.dt.int32
ALU = mybir.AluOpType
ACT = mybir.ActivationFunctionType
AX = mybir.AxisListType

P = 128
SEQS = 16
D = 256
KD = D // P
GS = 4
GROUPS = SEQS // GS
GT = GS * P
INNER = 512
KI = INNER // P
STATE = 64
PROJ = INNER + 2 * STATE
TAPS = 4
SSM_LAYERS = 5
EPS = 1e-5
BANK = 512
HI, LO = 0, 1


def product(pe, out, lhs, rhs, start, stop):
    pe.matmul(out, lhs[HI], rhs[HI], start=start, stop=False)
    pe.matmul(out, lhs[HI], rhs[LO], start=False, stop=False)
    return pe.matmul(out, lhs[LO], rhs[HI], start=False, stop=stop)


def stage_load_and_norm(nc, ctx, io, mem):
    X, ACTV, ACT_T, ident, neghalf = mem["x"], mem["act"], mem["act_t"], mem["ident"], mem["neghalf"]
    sem = lambda name: mem["sems"](name)
    x_loaded = [sem(f"n0_x_loaded{g}") for g in range(GROUPS)]
    const_step = sem("n0_const_step")
    consts_ready = sem("n0_consts_ready")
    stats_ready = sem("n0_stats_ready")
    aggr_ready = sem("n0_aggr_ready")
    var_ready = sem("n0_var_ready")
    rstd_ready = sem("n0_rstd_ready")
    normed = sem("n0_normed")
    tr_ready = sem("n0_tr_ready")
    tr_copied = sem("n0_tr_copied")
    tr_low = sem("n0_tr_low")
    psum, stats, mv, ve = mem["psum"], mem["stats"], mem["mv"], mem["ve"]

    with nc.Block() as block:
        @block.sync
        def _(sp):
            for g in range(GROUPS):
                sp.dma_start(X[:, GS * g:GS * g + GS, :],
                             io["x"][GS * g:GS * g + GS].rearrange("b t d -> t b d")).then_inc(x_loaded[g], 16)
            mem["prefetch_ssm"](sp)

        @block.gpsimd
        def _(pool):
            pool.memset(ident[:, :], 0.0).then_inc(const_step, 1)
            pool.memset(mem["ident_bf"][:, :], 0.0).then_inc(const_step, 1)
            pool.memset(mem["causal"][:, :], 0.0).then_inc(const_step, 1)
            pool.memset(neghalf[:, :], -0.5).then_inc(consts_ready, 1)
            pool.wait_ge(const_step, 3)
            for t in (ident, mem["ident_bf"]):
                pool.affine_select(out=t[:, :], in_=t[:, :], compare_op=ALU.not_equal, fill=1.0, base=0,
                                   pattern=[[-1, P]], channel_multiplier=1).then_inc(consts_ready, 1)
            pool.affine_select(out=mem["causal"][:, :], in_=mem["causal"][:, :], compare_op=ALU.is_ge,
                               fill=-1e30, base=0, pattern=[[-1, P]], channel_multiplier=1).then_inc(consts_ready, 1)
            pool.wait_ge(consts_ready, 4)
            for g in range(GROUPS):
                pool.wait_ge(var_ready, g + 1)
                pool.tensor_tensor(ve[:, GS * g:GS * g + GS], ve[:, GS * g:GS * g + GS],
                                   neghalf[:, 0:GS], ALU.pow).then_inc(rstd_ready, 1)
            split_w_in(pool, mem, 0)

        @block.vector
        def _(dve):
            def normalise(g):
                dve.wait_ge(rstd_ready, g + 1)
                for b in range(GS * g, GS * g + GS):
                    dve.tensor_scalar(ACTV[:, b, :], X[:, b, :], mv[:, b, 0:1], ve[:, b:b + 1],
                                      ALU.subtract, ALU.mult).then_inc(normed, 1)

            def turned_low(g):
                for h in (2 * g, 2 * g + 1):
                    dve.wait_ge(tr_copied, h + 1)
                    tokens = slice(2 * h * P, (2 * h + 2) * P)
                    dve.tensor_tensor(ACT_T[LO][:, :, tokens], psum[6 + h % 2][:, :].rearrange("p (k t) -> p k t", k=KD),
                                      ACT_T[HI][:, :, tokens].bitcast(F32), ALU.subtract).then_inc(tr_low, 1)

            for g in range(GROUPS):
                dve.wait_ge(x_loaded[g], 16)
                for b in range(GS * g, GS * g + GS):
                    dve.bn_stats(stats[:, b, :], X[:, b, :]).then_inc(stats_ready, 1)
                dve.wait_ge(stats_ready, GS * (g + 1))
                for b in range(GS * g, GS * g + GS):
                    dve.bn_aggr(mv[:, b, :], stats[:, b, :]).then_inc(aggr_ready, 1)
                dve.wait_ge(aggr_ready, GS * (g + 1))
                dve.tensor_scalar(ve[:, GS * g:GS * g + GS], mv[:, GS * g:GS * g + GS, 1], EPS, None,
                                  ALU.add).then_inc(var_ready, 1)
                if g > 0:
                    normalise(g - 1)
                if g > 1:
                    turned_low(g - 2)
            normalise(GROUPS - 1)
            turned_low(GROUPS - 2)
            turned_low(GROUPS - 1)

        @block.tensor
        def _(pe):
            pe.wait_ge(consts_ready, 4)
            for h in range(SEQS // 2):
                pe.wait_ge(normed, 2 * h + 2)
                if h >= 2:
                    pe.wait_ge(tr_low, h - 1)
                for s in range(2):
                    for k in range(KD):
                        col = k * D + s * P
                        tr = pe.transpose(psum[6 + h % 2][:, col:col + P],
                                          ACTV[:, 2 * h + s, k * P:(k + 1) * P], ident[:, :])
                tr.then_inc(tr_ready, 1)

        @block.scalar
        def _(act):
            for h in range(SEQS // 2):
                act.wait_ge(tr_ready, h + 1)
                nc.scalar.activation(ACT_T[HI][:, :, 2 * h * P:(2 * h + 2) * P],
                                     psum[6 + h % 2][:, :].rearrange("p (k t) -> p k t", k=KD),
                                     ACT.Copy).then_inc(tr_copied, 1)


def split_w_in(pool, mem, layer, in_use=None):
    raw, (hi, lo), names = mem["w_in_raw"], mem["w_in"], mem["ssm_sems"]
    pool.wait_ge(names["w_in_loaded"], layer * 16 + 16)
    if in_use is not None:
        pool.wait_ge(in_use, layer * GROUPS * KI)
    pool.sem_inc(names["w_in_seen"], 1)
    pool.tensor_copy(hi[:, :, :], raw[:, :, :]).then_inc(names["w_in_hi"], 1)
    pool.wait_ge(names["w_in_hi"], layer + 1)
    pool.tensor_tensor(lo[:, :, :], raw[:, :, :], hi[:, :, :].bitcast(F32), ALU.subtract).then_inc(names["w_in_split"], 1)


def stage_ssm(nc, ctx, io, mem):
    ACTV, ACT_T, ident, neghalf, psum = mem["act"], mem["act_t"], mem["ident"], mem["neghalf"], mem["psum"]
    names = mem["ssm_sems"]
    w_in, w_out, conv_w, conv_b, ln_g, ln_b, decay = (mem[k] for k in (
        "w_in", "w_out", "conv_w", "conv_b", "ln_g", "ln_b", "decay"))
    sb = lambda name, shape: ctx.enter_context(nc.sbuf_tensor(name, shape, F32))
    sem = lambda name: mem["sems"]("s_" + name)
    conv = sb("ssm_conv", [P, KI, GT])
    u = sb("ssm_u", [P, 2, KI, GT])
    turned = sb("ssm_turned", [P, KD, 2 * P])
    b_t = sb("ssm_b_t", [STATE, 2, GT])
    c_t = sb("ssm_c_t", [STATE, 2, GT])
    mix = sb("ssm_mix", [P, GS, P])
    uw = sb("ssm_uw", [P, 2, 2 * D])
    res = sb("ssm_res", [P, 2, 2, D])
    stats, mv, ve = mem["stats"], mem["mv"], mem["ve"]

    bc_ready = sem("bc_ready")
    xs_ready = sem("xs_ready")
    bt_copied = sem("bt_copied")
    ct_copied = sem("ct_copied")
    tap_last = sem("tap_last")
    tap_step = sem("tap_step")
    conv_done = sem("conv_done")
    u_ready = sem("u_ready")
    g_ready = sem("g_ready")
    mix_ready = sem("mix_ready")
    uw_ready = sem("uw_ready")
    uw_copied = sem("uw_copied")
    y_ready = sem("y_ready")
    res_ready = sem("res_ready")
    stats_ready = sem("stats_ready")
    stats_seen = sem("stats_seen")
    aggr_ready = sem("aggr_ready")
    var_ready = sem("var_ready")
    rstd_ready = sem("rstd_ready")
    z_ready = sem("z_ready")
    zg_ready = sem("zg_ready")
    act_ready = sem("act_ready")
    tr_ready = sem("tr_ready")
    tr_copied = sem("tr_copied")
    tr_low = sem("tr_low")
    attn_hi_ready = sem("attn_hi_ready")

    XS = lambda c: psum[c]
    BC, UWY, TR = psum[4], (psum[5], psum[6]), psum[7]
    LAST = SSM_LAYERS - 1

    def layers(eng, body):
        body(0)
        with eng.Fori(1, LAST) as layer:
            body(layer)
        body(LAST)

    with nc.Block() as block:
        @block.sync
        def _(sp):
            def reload(layer):
                sp.wait_ge(names["w_in_split"], layer + 1)
                mem["load_w_in"](sp, layer + 1)
                sp.wait_ge(tap_last, layer * (GROUPS * KI) + GROUPS * KI)
                sp.wait_ge(conv_done, layer * (GROUPS * KI) + GROUPS * KI)
                mem["load_conv"](sp, layer + 1)
                sp.wait_ge(uw_ready, layer * (2 * GROUPS) + 2 * GROUPS)
                mem["load_w_out"](sp, layer + 1)
                sp.wait_ge(mem["attn_w_split"], layer * GROUPS + GROUPS)
                sp.wait_ge(act_ready, layer * (2 * GROUPS) + 2 * GROUPS)
                mem["load_ln"](sp, layer + 1)
            with sp.Fori(0, LAST) as layer:
                sp.dma_start(mem["attn_raw"][:, :], io["attn_w_laid"][bass.ds(layer, 1)].rearrange(
                    "a p n -> p (a n)")).then_inc(mem["attn_w_loaded"], 16)
                reload(layer)
            for tile, name in ((mem["attn_g"], "L0_attn_attn_ln_g"), (mem["attn_b"], "L0_attn_attn_ln_b")):
                sp.dma_start(tile[:, :], io[name].unsqueeze(0).broadcast_to([P, D])).then_inc(mem["attn_ln_loaded"], 16)

        @block.tensor
        def _(pe):
            def project(layer, g, first=False):
                n = layer * GROUPS + g
                pe.wait_ge(names["w_in_split"], layer + 1)
                if not first:
                    pe.wait_ge(tr_low, n * 2 - 2 * GROUPS + 2)
                tokens = slice(g * GT, (g + 1) * GT)
                if g >= 2 or not first:
                    pe.wait_ge(mix_ready, n - 1)
                elif g == 1:
                    pe.wait_ge(bt_copied, 1)
                    pe.wait_ge(ct_copied, 1)
                for k in range(KD):
                    mm = product(pe, BC[:, :], [x[:, k, INNER:PROJ] for x in w_in], [x[:, k, tokens] for x in ACT_T],
                                 k == 0, k == KD - 1)
                mm.then_inc(bc_ready, 1)
                for c in range(KI):
                    if g >= 1 or not first:
                        pe.wait_ge(tap_last, n * KI - KI + c + 1)
                        pe.wait_ge(conv_done, n * KI - KI + c + 1)
                    for k in range(KD):
                        mm = product(pe, XS(c)[:, :], [x[:, k, c * P:(c + 1) * P] for x in w_in],
                                     [x[:, k, tokens] for x in ACT_T], k == 0, k == KD - 1)
                    mm.then_inc(xs_ready, 1)

            def turn(layer, g, h):
                n = layer * GROUPS + g
                pe.wait_ge(act_ready, n * 2 + h + 1)
                if not (layer_is(layer, 0) and g == 0 and h == 0):
                    pe.wait_ge(tr_copied, n * 2 + h)
                for s in range(2):
                    for k in range(KD):
                        tr = pe.transpose(TR[:, k * D + s * P:k * D + (s + 1) * P],
                                          ACTV[:, g * GS + 2 * h + s, k * P:(k + 1) * P], ident[:, :])
                tr.then_inc(tr_ready, 1)

            def mix_tokens(layer, g, first=False, last=False):
                n = layer * GROUPS + g
                ahead = 1 if last else 2
                pe.wait_ge(bt_copied, n + ahead)
                pe.wait_ge(ct_copied, n + ahead)
                for s in range(GS):
                    mm = pe.matmul(BC[:, s * P:(s + 1) * P], b_t[:, g % 2, s * P:(s + 1) * P],
                                   c_t[:, g % 2, s * P:(s + 1) * P], start=True, stop=True)
                mm.then_inc(g_ready, 1)
                pe.wait_ge(u_ready, n * KI + KI)
                if g == 0:
                    pe.wait_ge(names["w_out_loaded"], layer * 16 + 16)
                for h in range(2):
                    if not (first and g == 0):
                        pe.wait_ge(res_ready, n * 2 - 1 + h)
                    for s in range(2):
                        t = (2 * h + s) * P
                        for c in range(KI):
                            mm = pe.matmul(UWY[h][:, s * D:(s + 1) * D], u[:, g % 2, c, t:t + P],
                                           w_out[:, c, :], start=(c == 0), stop=(c == KI - 1))
                    mm.then_inc(uw_ready, 1)
                before = (layer, g - 1) if g > 0 else None if first else (layer - 1, GROUPS - 1)
                if before:
                    turn(*before, 0)
                pe.wait_ge(mix_ready, n + 1)
                for h in range(2):
                    pe.wait_ge(uw_copied, n * 2 + h + 1)
                    for s in range(2):
                        mm = pe.matmul(UWY[h][:, s * D:(s + 1) * D], mix[:, 2 * h + s, :],
                                       uw[:, h, s * D:(s + 1) * D], start=True, stop=True)
                    mm.then_inc(y_ready, 1)
                if before:
                    turn(*before, 1)

            project(0, 0, first=True)

            def layer_steps(layer):
                first, last = layer_is(layer, 0), layer_is(layer, LAST)
                for g in range(GROUPS):
                    if g < GROUPS - 1:
                        project(layer, g + 1, first)
                    elif not last:
                        project(layer + 1, 0)
                    mix_tokens(layer, g, first, last and g == GROUPS - 1)
            layers(pe, layer_steps)
            for h in range(2):
                turn(LAST, GROUPS - 1, h)

        @block.scalar
        def _(act):
            def front(layer, g, first=False):
                n = layer * GROUPS + g
                act.wait_ge(bc_ready, n + 1)
                if not (first and g < 2):
                    act.wait_ge(g_ready, n - 1)
                nc.scalar.activation(b_t[:, g % 2, :], BC[0:STATE, :], ACT.Copy).then_inc(bt_copied, 1)
                if g == 0:
                    act.wait_ge(names["conv_loaded"], layer * 32 + 32)
                for c in range(KI):
                    act.wait_ge(xs_ready, n * KI + c + 1)
                    if not (first and g == 0):
                        act.wait_ge(u_ready, n * KI - KI + c + 1)
                    nc.scalar.activation(conv[:, c, :], XS(c)[:, :], ACT.Identity, bias=conv_b[:, c:c + 1],
                                         scale=conv_w[:, c, TAPS - 1:TAPS]).then_inc(tap_last, 1)

            def silu(layer, g, chunks, first=False):
                n = layer * GROUPS + g
                for c in chunks:
                    act.wait_ge(conv_done, n * KI + c + 1)
                    if not (first and g < 2):
                        act.wait_ge(uw_ready, n * 2 - 2)
                    nc.scalar.activation(u[:, g % 2, c, :], conv[:, c, :], ACT.Silu).then_inc(u_ready, 1)

            def copy_uw(layer, g, h):
                n = layer * GROUPS + g
                act.wait_ge(uw_ready, n * 2 + h + 1)
                nc.scalar.activation(uw[:, h, :], UWY[h][:, :], ACT.Copy).then_inc(uw_copied, 1)

            def copy_turned(layer, g, h):
                n = layer * GROUPS + g
                act.wait_ge(tr_ready, n * 2 + h + 1)
                t = g * GT + 2 * h * P
                bank = TR[:, :].rearrange("p (k t) -> p k t", k=KD)
                act.activation(ACT_T[HI][:, :, t:t + 2 * P], bank, ACT.Copy)
                if not (layer_is(layer, 0) and g == 0 and h == 0):
                    act.wait_ge(tr_low, n * 2 + h)
                act.activation(turned[:, :, :], bank, ACT.Copy).then_inc(tr_copied, 1)

            front(0, 0, first=True)
            silu(0, 0, range(KI), first=True)

            def layer_steps(layer):
                first, last = layer_is(layer, 0), layer_is(layer, LAST)
                for g in range(GROUPS):
                    ahead = (layer, g + 1, first) if g < GROUPS - 1 else None if last else (layer + 1, 0)
                    if ahead:
                        front(*ahead)
                    if ahead:
                        silu(*ahead[:2], range(0, 2), *ahead[2:])
                    copy_uw(layer, g, 0)
                    copy_uw(layer, g, 1)
                    before = (layer, g - 1) if g > 0 else None if first else (layer - 1, GROUPS - 1)
                    if before:
                        copy_turned(*before, 0)
                    if ahead:
                        silu(*ahead[:2], range(2, KI), *ahead[2:])
                    if before:
                        copy_turned(*before, 1)
            layers(act, layer_steps)
            for h in range(2):
                copy_turned(LAST, GROUPS - 1, h)

        @block.vector
        def _(dve):
            def copy_c(layer, g, first=False):
                n = layer * GROUPS + g
                dve.wait_ge(bc_ready, n + 1)
                if not (first and g < 2):
                    dve.wait_ge(g_ready, n - 1)
                dve.tensor_copy(c_t[:, g % 2, :], BC[STATE:P, :]).then_inc(ct_copied, 1)

            def convolve(layer, g, pair):
                n = layer * GROUPS + g
                for back in range(1, TAPS):
                    for c in (2 * pair, 2 * pair + 1):
                        acc = conv[:, c, :].rearrange("p (s t) -> p s t", s=GS)[:, :, back:]
                        xs = XS(c)[:, :].rearrange("p (s t) -> p s t", s=GS)[:, :, 0:P - back]
                        if back == 1:
                            dve.wait_ge(tap_last, n * KI + c + 1)
                        else:
                            dve.wait_ge(tap_step, (n * 2 + pair) * 4 + (back - 2) * 2 + (c - 2 * pair) + 1)
                        op = dve.scalar_tensor_tensor(out=acc, in0=xs, scalar=conv_w[:, c, TAPS - 1 - back:TAPS - back],
                                                      in1=acc, op0=ALU.mult, op1=ALU.add)
                        op.then_inc(conv_done if back == TAPS - 1 else tap_step, 1)

            def decayed(layer, g):
                n = layer * GROUPS + g
                dve.wait_ge(g_ready, n + 1)
                if g == 0 and layer_is(layer, 0):
                    dve.wait_ge(names["decay_loaded"], 16)
                dve.tensor_tensor(mix[:, :, :], BC[:, :].rearrange("p (s t) -> p s t", s=GS),
                                  decay[:, :].unsqueeze(1).broadcast_to([P, GS, P]), ALU.mult).then_inc(mix_ready, 1)

            def norm(layer, g):
                n = layer * GROUPS + g
                for h in range(2):
                    b = g * GS + 2 * h
                    dve.wait_ge(y_ready, n * 2 + h + 1)
                    if not (layer_is(layer, 0) and g == 0):
                        dve.wait_ge(act_ready, n * 2 - 1 + h)
                    dve.tensor_tensor(res[:, h, :, :],
                                      UWY[h][:, :].rearrange("p (s d) -> p s d", s=2),
                                      ACTV[:, b:b + 2, :], ALU.add).then_inc(res_ready, 1)
                    dve.wait_ge(res_ready, n * 2 + h + 1)
                    for s in range(2):
                        dve.bn_stats(stats[:, 2 * h + s, :], res[:, h, s, :]).then_inc(stats_ready, 1)
                    dve.wait_ge(stats_ready, n * 4 + 2 * h + 2)
                    dve.sem_inc(stats_seen, 1)
                    for s in range(2):
                        dve.bn_aggr(mv[:, 2 * h + s, :], stats[:, 2 * h + s, :]).then_inc(aggr_ready, 1)
                    dve.wait_ge(aggr_ready, n * 4 + 2 * h + 2)
                    dve.tensor_scalar(ve[:, 2 * h:2 * h + 2], mv[:, 2 * h:2 * h + 2, 1], EPS, None,
                                      ALU.add).then_inc(var_ready, 1)
                for h in range(2):
                    dve.wait_ge(rstd_ready, n * 2 + h + 1)
                    for s in range(2):
                        i = 2 * h + s
                        dve.tensor_scalar(res[:, h, s, :], res[:, h, s, :], mv[:, i, 0:1],
                                          ve[:, i:i + 1], ALU.subtract, ALU.mult).then_inc(z_ready, 1)

            copy_c(0, 0, True)
            convolve(0, 0, 0)
            convolve(0, 0, 1)

            def layer_steps(layer):
                first, last = layer_is(layer, 0), layer_is(layer, LAST)
                for g in range(GROUPS):
                    ahead = (layer, g + 1) if g < GROUPS - 1 else None if last else (layer + 1, 0)
                    if ahead:
                        copy_c(*ahead, first and g < GROUPS - 1)
                        convolve(*ahead, 0)
                    decayed(layer, g)
                    if ahead:
                        convolve(*ahead, 1)
                    norm(layer, g)
            layers(dve, layer_steps)

        @block.gpsimd
        def _(pool):
            def finish(layer, g):
                n = layer * GROUPS + g
                for h in range(2):
                    pool.wait_ge(var_ready, n * 2 + h + 1)
                    pool.tensor_tensor(ve[:, 2 * h:2 * h + 2], ve[:, 2 * h:2 * h + 2], neghalf[:, 0:2],
                                       ALU.pow).then_inc(rstd_ready, 1)
                if g == 0:
                    pool.wait_ge(names["ln_loaded"], layer * 32 + 32)
                for h in range(2):
                    b = g * GS + 2 * h
                    pool.wait_ge(z_ready, n * 4 + 2 * h + 2)
                    pool.tensor_tensor(res[:, h, :, :], res[:, h, :, :],
                                       ln_g[:, :].unsqueeze(1).broadcast_to([P, 2, D]), ALU.mult).then_inc(zg_ready, 1)
                    pool.wait_ge(zg_ready, n * 2 + h + 1)
                    pool.tensor_tensor(ACTV[:, b:b + 2, :], res[:, h, :, :],
                                       ln_b[:, :].unsqueeze(1).broadcast_to([P, 2, D]), ALU.add).then_inc(act_ready, 1)

            def split_attention_weight(layer, g):
                n = layer * GROUPS + g
                cols = slice(g * 2 * KI * P // 2, (g + 1) * 2 * KI * P // 2)
                w = mem["attn_w"]
                if g == 0:
                    pool.wait_ge(mem["attn_w_loaded"], layer * 16 + 16)
                part = lambda x: x[:, bass.ds(layer, 1), cols].rearrange("p a n -> p (a n)")
                pool.tensor_copy(part(w[HI]), mem["attn_raw"][:, cols]).then_inc(attn_hi_ready, 1)
                pool.wait_ge(attn_hi_ready, n + 1)
                pool.tensor_tensor(part(w[LO]), mem["attn_raw"][:, cols], part(w[HI]).bitcast(F32),
                                   ALU.subtract).then_inc(mem["attn_w_split"], 1)

            def turned_low(layer, g):
                n = layer * GROUPS + g
                for h in range(2):
                    t = g * GT + 2 * h * P
                    hi, lo = (x[:, :, t:t + 2 * P] for x in ACT_T)
                    pool.wait_ge(tr_copied, n * 2 + h + 1)
                    pool.tensor_tensor(lo, turned[:, :, :], hi.bitcast(F32), ALU.subtract).then_inc(tr_low, 1)

            with pool.Fori(0, LAST) as layer:
                for g in range(GROUPS):
                    finish(layer, g)
                    split_attention_weight(layer, g)
                    if g == GROUPS - 3:
                        split_w_in(pool, mem, layer + 1, xs_ready)
                    turned_low(layer, g)
            for g in range(GROUPS):
                finish(LAST, g)
                turned_low(LAST, g)


def layer_is(layer, value):
    return isinstance(layer, int) and layer == value


def chunks_of(pair, i, chunks):
    return [x[:, i, :].rearrange("p (k n) -> p k n", k=chunks) for x in pair]


HEADS = 16
HEAD = 64
WIDE = HEADS * HEAD
KW = WIDE // P
OCT = KW // 2


def stage_self_attention(nc, ctx, io, mem):
    X, ACTV, ACT_T, ident, neghalf, psum = mem["x"], mem["act"], mem["act_t"], mem["ident"], mem["neghalf"], mem["psum"]
    sb = lambda name, shape, dt=F32: ctx.enter_context(nc.sbuf_tensor("a_" + name, shape, dt))
    sem = lambda name: mem["sems"]("a_" + name)
    pair = lambda name, shape: (sb(name + "_hi", shape, F32R), sb(name + "_lo", shape, F32R))
    w = mem["attn_w"]
    wq, wk, wv = (chunks_of(w, i, KD) for i in range(3))
    wo = chunks_of(w, 3, KW)
    ln_g, ln_b = mem["attn_g"], mem["attn_b"]
    q_t = sb("q_t", [P, KW, GT])
    k_t = sb("k_t", [P, KW, GT])
    v = sb("v", [P, GS, WIDE])
    prob = sb("prob", [P, 4, 4, P])
    prob_t = sb("prob_t", [P, 4, 4, P])
    o_t = pair("o_t", [P, OCT, P])
    neg_max, total, inv = (sb(name, [P, 4, 4]) for name in ("neg_max", "total", "inv"))
    res = sb("res", [P, 2, D])
    z = sb("z", [P, 2, D])
    zg = sb("zg", [P, D])
    zb = sb("zb", [P, D])
    stats, mv, ve = mem["stats"], mem["mv"], mem["ve"]

    job_ready = sem("job_ready")
    job_act, job_dve = sem("job_act"), sem("job_dve")
    s_ready = sem("s_ready")
    max_ready, exp_ready = sem("max_ready"), sem("exp_ready")
    inv_ready, prob_ready = sem("inv_ready"), sem("prob_ready")
    pt_ready = sem("pt_ready")
    pt_act, pt_dve = sem("pt_act"), sem("pt_dve")
    ot_ready = sem("ot_ready")
    ot_hi, ot_lo = sem("ot_hi"), sem("ot_lo")
    y_ready, y_added = sem("y_ready"), sem("y_added")
    stats_ready, aggr_ready, var_ready, rstd_ready = (sem(n) for n in (
        "stats_ready", "aggr_ready", "var_ready", "rstd_ready"))
    z_ready, zg_ready, zb_ready, x_ready = sem("z_ready"), sem("zg_ready"), sem("zb_ready"), sem("x_ready")

    HALF_TICKS = 2 * GS
    HALVES = 2 * GROUPS
    TICKS = HALVES * HALF_TICKS
    JOBS = 2 * OCT + GS
    JOB_TICKS = (0, 0, 1, 1, 2, 2, 3, 3, 4, 5, 6, 7)
    INVERT, NORM, TURN, MEAN, SPLIT, OUT, NORM_OUT = 1, 2, 3, 5, 7, 8, 10
    LAST_TICK = TICKS - 2 + NORM_OUT
    S, JOB, PT = psum[0:2], psum[2:4], psum[4:6]
    OT = lambda U: psum[6 + U % 2][:, :]
    Y = lambda U: psum[6 + U % 2][:, 0:D]

    def place(m):
        half, i = divmod(m, HALF_TICKS)
        return half // 2, half % 2, i // 2, i % 2

    def behind(m, ticks):
        t = m - ticks
        return (t // 2, *place(t)[:3]) if t % 2 == 0 and 0 <= t < TICKS else None

    def jobs_at(m):
        half, i = divmod(m, HALF_TICKS)
        return [(half + 1, j) for j in range(JOBS) if JOB_TICKS[j] == i] if half < HALVES - 1 else []

    with nc.Block() as block:
        @block.tensor
        def _(pe):
            def job(half, j):
                n = half * JOBS + j
                G, octet = divmod(half, 2)
                if n >= 2:
                    pe.wait_ge((job_act, job_dve)[j % 2], n // 2)
                bank = JOB[j % 2]
                if j < 2 * OCT:
                    weights, c = (wq, wk)[j % 2], octet * OCT + j // 2
                    for k in range(KD):
                        mm = product(pe, bank[:, :], [x[:, k, c * P:(c + 1) * P] for x in weights], [x[:, k, G * GT:(G + 1) * GT] for x in ACT_T],
                                     k == 0, k == KD - 1)
                else:
                    t = G * GT + (j - 2 * OCT) * P
                    for k in range(KD):
                        mm = product(pe, bank[:, :], [x[:, k, t:t + P] for x in ACT_T],
                                     [x[:, k, octet * BANK:(octet + 1) * BANK] for x in wv], k == 0, k == KD - 1)
                mm.then_inc(job_ready, 1)

            pe.wait_ge(mem["attn_w_split"], 16)
            for j in range(JOBS):
                job(0, j)
            for m in range(LAST_TICK + 1):
                if m < TICKS:
                    G, octet, s, par = place(m)
                    if m % HALF_TICKS == 0:
                        jobs = (m // HALF_TICKS) * (JOBS // 2) + OCT
                        pe.wait_ge(job_act, jobs)
                        pe.wait_ge(job_dve, jobs)
                    if m >= 2:
                        pe.wait_ge(exp_ready, m - 1)
                    pe.matmul(S[par][:, :], mem["ident_bf"][:, :], mem["causal"][:, :].unsqueeze(1).broadcast_to([P, 4, P]),
                              start=True, stop=False, skip_group_check=True)
                    rows = slice(par * HEAD, (par + 1) * HEAD)
                    for i in range(4):
                        mm = pe.matmul(S[par][:, i * P:(i + 1) * P], q_t[rows, OCT * octet + i, s * P:(s + 1) * P],
                                       k_t[rows, OCT * octet + i, s * P:(s + 1) * P],
                                       start=False, stop=True, skip_group_check=True)
                    mm.then_inc(s_ready, 1)
                t = m - TURN
                if 0 <= t < TICKS:
                    pe.wait_ge(prob_ready, t + 1)
                    if t >= 2:
                        pe.wait_ge((pt_dve, pt_act)[t % 2], t // 2)
                    for i in range(4):
                        tr = pe.transpose(PT[t % 2][:, i * P:(i + 1) * P], prob[:, t % 4, i, :], ident[:, :])
                    tr.then_inc(pt_ready, 1)
                t = m - MEAN
                if 0 <= t < TICKS:
                    G, octet, s, par = place(t)
                    U = t // 2
                    if t % HALF_TICKS == 0:
                        jobs = (t // HALF_TICKS + 1) * (JOBS // 2)
                        pe.wait_ge(job_act, jobs)
                        pe.wait_ge(job_dve, jobs)
                    if par == 0 and U >= 2:
                        pe.wait_ge(y_added, U - 1)
                    pe.wait_ge((pt_dve, pt_act)[t % 2], t // 2 + 1)
                    rows = slice(par * HEAD, (par + 1) * HEAD)
                    for i in range(4):
                        head = octet * 8 + 2 * i + par
                        mm = pe.matmul(OT(U)[rows, i * P:(i + 1) * P], v[:, s, head * HEAD:(head + 1) * HEAD],
                                       prob_t[:, t % 4, i, :], start=True, stop=True, tile_position=(0, par * HEAD))
                    if par == 1:
                        mm.then_inc(ot_ready, 1)
                unit = behind(m, OUT)
                if unit:
                    U, G, octet, s = unit
                    pe.wait_ge(ot_hi, U + 1)
                    pe.wait_ge(ot_lo, U + 1)
                    for c in range(OCT):
                        mm = product(pe, Y(U), [x[:, c, :] for x in o_t], [x[:, octet * OCT + c, :] for x in wo],
                                     c == 0, c == OCT - 1)
                    mm.then_inc(y_ready, 1)
                for half, j in jobs_at(m):
                    job(half, j)

        @block.scalar
        def _(act):
            def job(half, j):
                G, octet = divmod(half, 2)
                act.wait_ge(job_ready, half * JOBS + j + 1)
                if j < 2 * OCT:
                    act.activation(q_t[:, octet * OCT + j // 2, :], JOB[0][:, :], ACT.Copy, scale=HEAD ** -0.5).then_inc(job_act, 1)
                else:
                    act.activation(v[:, j - 2 * OCT, octet * BANK:(octet + 1) * BANK], JOB[0][:, :], ACT.Copy).then_inc(job_act, 1)

            for j in range(0, JOBS, 2):
                job(0, j)
            for m in range(LAST_TICK + 1):
                if m < TICKS:
                    act.wait_ge(max_ready, m + 1)
                    for i in range(4):
                        e = act.activation(prob[:, m % 4, i, :], S[m % 2][:, i * P:(i + 1) * P], ACT.Exp,
                                           bias=neg_max[:, m % 4, i:i + 1], accum_out=total[:, m % 4, i:i + 1])
                    e.then_inc(exp_ready, 1)
                t = m - TURN
                if 0 <= t < TICKS and t % 2 == 1:
                    act.wait_ge(pt_ready, t + 1)
                    act.activation(prob_t[:, t % 4, :, :], PT[1][:, :].rearrange("p (i k) -> p i k", i=4),
                                   ACT.Copy).then_inc(pt_act, 1)
                unit = behind(m, SPLIT)
                if unit:
                    U = unit[0]
                    act.wait_ge(ot_ready, U + 1)
                    if U > 0:
                        act.wait_ge(y_ready, U)
                    act.activation(o_t[HI][:, :, :], OT(U).rearrange("p (i k) -> p i k", i=OCT), ACT.Copy).then_inc(ot_hi, 1)
                for half, j in jobs_at(m):
                    if j % 2 == 0:
                        job(half, j)

        @block.vector
        def _(dve):
            def job(half, j):
                G, octet = divmod(half, 2)
                dve.wait_ge(job_ready, half * JOBS + j + 1)
                out = k_t[:, octet * OCT + j // 2, :] if j < 2 * OCT else v[:, j - 2 * OCT, octet * BANK:(octet + 1) * BANK]
                dve.tensor_copy(out, JOB[1][:, :]).then_inc(job_dve, 1)

            def measure(b):
                i = b % 2
                dve.bn_stats(stats[:, i, :], res[:, i, :]).then_inc(stats_ready, 1)
                dve.wait_ge(stats_ready, b + 1)
                dve.bn_aggr(mv[:, i, :], stats[:, i, :]).then_inc(aggr_ready, 1)
                dve.wait_ge(aggr_ready, b + 1)
                dve.tensor_scalar(ve[:, i:i + 1], mv[:, i, 1:2], EPS, None, ALU.add).then_inc(var_ready, 1)

            for j in range(1, JOBS, 2):
                job(0, j)
            for m in range(LAST_TICK + 1):
                if m < TICKS:
                    dve.wait_ge(s_ready, m + 1)
                    dve.tensor_reduce(neg_max[:, m % 4, :], S[m % 2][:, :].rearrange("p (i k) -> p i k", i=4), AX.X, ALU.max,
                                      negate=True).then_inc(max_ready, 1)
                t = m - INVERT
                if 0 <= t < TICKS:
                    dve.wait_ge(exp_ready, t + 1)
                    dve.reciprocal(inv[:, t % 4, :], total[:, t % 4, :]).then_inc(inv_ready, 1)
                t = m - TURN
                if 0 <= t < TICKS and t % 2 == 0:
                    dve.wait_ge(pt_ready, t + 1)
                    dve.tensor_copy(prob_t[:, t % 4, :, :], PT[0][:, :].rearrange("p (i k) -> p i k", i=4)).then_inc(pt_dve, 1)
                unit = behind(m, SPLIT)
                if unit:
                    U = unit[0]
                    dve.wait_ge(ot_hi, U + 1)
                    dve.tensor_tensor(o_t[LO][:, :, :], OT(U).rearrange("p (i k) -> p i k", i=OCT),
                                      o_t[HI][:, :, :].bitcast(F32), ALU.subtract).then_inc(ot_lo, 1)
                unit = behind(m, OUT)
                if unit:
                    U, G, octet, s = unit
                    b = G * GS + s
                    dve.wait_ge(y_ready, U + 1)
                    out = res[:, b % 2, :] if octet else ACTV[:, b, :]
                    dve.tensor_tensor(out, Y(U), ACTV[:, b, :], ALU.add).then_inc(y_added, 1)
                    if octet:
                        dve.wait_ge(y_added, U + 1)
                        measure(b)
                unit = behind(m, NORM_OUT)
                if unit and unit[2]:
                    U, G, octet, s = unit
                    b = G * GS + s
                    i = b % 2
                    dve.wait_ge(rstd_ready, b + 1)
                    dve.tensor_scalar(z[:, i, :], res[:, i, :], mv[:, i, 0:1], ve[:, i:i + 1],
                                      ALU.subtract, ALU.mult).then_inc(z_ready, 1)
                for half, j in jobs_at(m):
                    if j % 2 == 1:
                        job(half, j)

        @block.gpsimd
        def _(pool):
            def finish(b):
                pool.wait_ge(z_ready, b + 1)
                pool.tensor_tensor(zg[:, :], z[:, b % 2, :], ln_g[:, :], ALU.mult).then_inc(zg_ready, 1)
                pool.wait_ge(zg_ready, b + 1)
                pool.tensor_tensor(zb[:, :], zg[:, :], ln_b[:, :], ALU.add).then_inc(zb_ready, 1)
                pool.wait_ge(zb_ready, b + 1)
                pool.tensor_tensor(X[:, b, :], X[:, b, :], zb[:, :], ALU.add).then_inc(x_ready, 1)

            pool.wait_ge(mem["attn_ln_loaded"], 32)
            for m in range(LAST_TICK + 1):
                t = m - NORM
                if 0 <= t < TICKS:
                    pool.wait_ge(inv_ready, t + 1)
                    pool.tensor_tensor(prob[:, t % 4, :, :], prob[:, t % 4, :, :],
                                       inv[:, t % 4, :].unsqueeze(2).broadcast_to([P, 4, P]), ALU.mult).then_inc(prob_ready, 1)
                unit = behind(m, OUT)
                if unit and unit[2]:
                    b = unit[1] * GS + unit[3]
                    i = b % 2
                    pool.wait_ge(var_ready, b + 1)
                    pool.tensor_tensor(ve[:, i:i + 1], ve[:, i:i + 1], neghalf[:, 0:1], ALU.pow).then_inc(rstd_ready, 1)
                unit = behind(m, NORM_OUT)
                if unit and unit[2]:
                    finish(unit[1] * GS + unit[3])


EXPERTS = 8
FFN = 512
KF = FFN // P
W_PARTS = 3
W_COLS = KD * FFN


def norm_state(nc, ctx, mem, name, width):
    norm = {"width": width, "neghalf": mem["neghalf"]}
    for what, shape in (("stats", [P, width, 6]), ("mv", [P, width, 2]), ("ve", [P, width])):
        norm[what] = ctx.enter_context(nc.sbuf_tensor(f"{name}_{what}", shape, F32))
    for what in ("stats_ready", "aggr_ready", "var_ready", "rstd_ready", "z_ready"):
        norm[what] = mem["sems"](f"{name}_{what}")
    return norm


def norm_measure(dve, norm, n, rows):
    w = norm["width"]
    for i in range(w):
        dve.bn_stats(norm["stats"][:, i, :], rows(i)).then_inc(norm["stats_ready"], 1)
    dve.wait_ge(norm["stats_ready"], n * w + w)
    for i in range(w):
        dve.bn_aggr(norm["mv"][:, i, :], norm["stats"][:, i, :]).then_inc(norm["aggr_ready"], 1)
    dve.wait_ge(norm["aggr_ready"], n * w + w)
    dve.tensor_scalar(norm["ve"][:, :], norm["mv"][:, :, 1], EPS, None, ALU.add).then_inc(norm["var_ready"], 1)


def norm_invert(pool, norm, n):
    ve = norm["ve"][:, :]
    pool.wait_ge(norm["var_ready"], n + 1)
    pool.tensor_tensor(ve, ve, norm["neghalf"][:, 0:norm["width"]], ALU.pow).then_inc(norm["rstd_ready"], 1)


def norm_apply(dve, norm, n, rows, outs):
    dve.wait_ge(norm["rstd_ready"], n + 1)
    for i in range(norm["width"]):
        dve.tensor_scalar(outs(i), rows(i), norm["mv"][:, i, 0:1], norm["ve"][:, i:i + 1],
                          ALU.subtract, ALU.mult).then_inc(norm["z_ready"], 1)


XHEAD = D // HEADS
ROWT = 32
TILES = P // ROWT


def stage_cross_attention(nc, ctx, io, mem):
    X, ident, neghalf, psum = mem["x"], mem["ident"], mem["neghalf"], mem["psum"]
    sb = lambda name, shape, dt=F32: ctx.enter_context(nc.sbuf_tensor("x_" + name, shape, dt))
    sem = lambda name: mem["sems"]("x_" + name)
    pair = lambda name, shape: (sb(name + "_hi", shape, F32R), sb(name + "_lo", shape, F32R))
    norm = norm_state(nc, ctx, mem, "xn", GS)
    w_raw = sb("w_raw", [P, 4, KD * D])
    w = pair("w", [P, 4, KD * D])
    wk, wv, wq, wo = (chunks_of(w, i, KD) for i in range(4))
    bq, bk = sb("bq", [P, KD]), sb("bk", [P, KD])
    bq_scaled = sb("bq_scaled", [P, KD])
    bv, bo = sb("bv", [P, D]), sb("bo", [P, D])
    sel = sb("sel", [P, 2])
    ctx_raw = sb("ctx_raw", [P, 2, KD, GT])
    cg = pair("cg", [P, KD, GT])
    z = sb("z", [P, GS, D])
    xg = pair("xg", [P, KD, GT])
    q_t = sb("q_t", [P, 2, KD, GT])
    k_t = sb("k_t", [P, 2, 2, KD, GT])
    v = sb("v", [P, 2, 2, GS, D])
    prob = sb("prob", [P, 2, TILES, 4, P])
    prob_t = sb("prob_t", [P, 2, TILES, 4, P])
    neg_max, total, inv = (sb(name, [P, 2, TILES, 4]) for name in ("neg_max", "total", "inv"))
    o_t = pair("o_t", [P, KD, P])

    w_loaded = [sem(f"w{i}_loaded") for i in range(4)]
    ctx_loaded = [sem(f"ctx_loaded{i}") for i in range(2)]
    bias_loaded = sem("bias_loaded")
    w_hi, w_split = sem("w_hi"), sem("w_split")
    ctx_hi, ctx_lo = sem("ctx_hi"), sem("ctx_lo")
    setup, bq_ready = sem("setup"), sem("bq_ready")
    sel_step = sem("sel_step")
    tr_ready, xh_ready, xl_ready = sem("tr_ready"), sem("xh_ready"), sem("xl_ready")
    q_ready, k_ready, v_ready = sem("q_ready"), sem("k_ready"), sem("v_ready")
    q_copied, k_copied, v_copied = sem("q_copied"), sem("k_copied"), sem("v_copied")
    s_ready, max_ready, exp_ready = sem("s_ready"), sem("max_ready"), sem("exp_ready")
    pt_ready, pt_act, pt_dve = sem("pt_ready"), sem("pt_act"), sem("pt_dve")
    v_cleared, inv_ready, prob_ready = sem("v_cleared"), sem("inv_ready"), sem("prob_ready")
    ot_ready, ot_hi, ot_lo = sem("ot_ready"), sem("ot_hi"), sem("ot_lo")
    y_ready, y_added, x_ready = sem("y_ready"), sem("y_added"), sem("x_ready")

    half_hi, half_split = sem("half_hi"), sem("half_split")

    S, JOB, PT = psum[0:2], psum[2:4], psum[4:6]
    OT = lambda b: psum[6 + b % 2][:, 0:D]
    Y = lambda b: psum[6 + b % 2][:, D:2 * D]
    TICKS = SEQS * TILES
    GROUP_TICKS = GS * TILES
    JOB_TICKS = (0, 2, 4, 6, 8, 9, 11, 13)
    JOBS = len(JOB_TICKS)
    INVERT, TURN, MEAN, SPLIT_HIGH, SPLIT_LOW, OUT, ADD = 1, 3, 5, 9, 9, 11, 12
    LAST_TICK = TICKS - TILES + ADD
    MEASURE_NEXT = GROUP_TICKS - TILES + ADD + 3
    EXPERT_TICK = 7

    def behind(m, ticks):
        b, r = divmod(m - ticks, TILES)
        return b if r == 0 and 0 <= b < SEQS else None

    def jobs_at(m):
        G, i = divmod(m, GROUP_TICKS)
        return [(G + 1, JOB_TICKS.index(i))] if G < GROUPS - 1 and i in JOB_TICKS else []

    with nc.Block() as block:
        @block.sync
        def _(sp):
            load = lambda i, name: sp.dma_start(w_raw[:, i, :], io["L0_xattn_" + name + "_laid"]).then_inc(w_loaded[i], 16)

            def load_context(G):
                sp.dma_start(ctx_raw[:, G % 2, :, :], io["ctx_t_laid"][:, :, G * GT:(G + 1) * GT]).then_inc(ctx_loaded[G % 2], 16)
            load(0, "W_k")
            load_context(0)
            load(1, "W_v")
            for tile, name in ((bq, "b_q"), (bk, "b_k")):
                sp.dma_start(tile[:, :], io["L0_xattn_" + name + "_laid"]).then_inc(bias_loaded, 16)
            for tile, name in ((bv, "b_v"), (bo, "b_o")):
                sp.dma_start(tile[:, :], io["L0_xattn_" + name].unsqueeze(0).broadcast_to([P, D])).then_inc(bias_loaded, 16)
            load(2, "W_q")
            load(3, "W_o")
            load_context(1)
            sp.dma_start(mem["expert_raw"][:, :, :].rearrange("p a n -> p (a n)"), io["experts_laid"][0]).then_inc(
                mem["expert_loaded"], 16)
            for G in range(2, GROUPS):
                sp.wait_ge(ctx_lo, G - 1)
                load_context(G)

        @block.gpsimd
        def _(pool):
            pool.memset(v[:, 0, :, :, :], 0.0).then_inc(v_cleared, 1)
            pool.memset(sel[:, :], 0.0).then_inc(sel_step, 1)
            pool.wait_ge(sel_step, 1)
            for r in range(TILES):
                if r > 0:
                    pool.wait_ge(setup, 2 * r)
                rows = slice(r * ROWT, (r + 1) * ROWT)
                pool.affine_select(out=sel[rows, 0:1], in_=sel[rows, 0:1], compare_op=ALU.is_ge, fill=1.0,
                                   base=-XHEAD, pattern=[[1, 1]], channel_multiplier=1).then_inc(setup, 1)
                pool.wait_ge(setup, 2 * r + 1)
                pool.affine_select(out=sel[rows, 1:2], in_=sel[rows, 1:2], compare_op=ALU.is_ge, fill=1.0,
                                   base=XHEAD - 1, pattern=[[1, 1]], channel_multiplier=-1).then_inc(setup, 1)
            pool.wait_ge(setup, 2 * TILES)
            norm_invert(pool, norm, 0)

            def add_bias(b):
                if b == 0:
                    pool.wait_ge(bias_loaded, 64)
                pool.wait_ge(y_added, b + 1)
                pool.tensor_tensor(X[:, b, :], X[:, b, :], bo[:, :], ALU.add).then_inc(x_ready, 1)

            def weight_low(i):
                pool.wait_ge(w_hi, i + 1)
                pool.tensor_tensor(w[LO][:, i, :], w_raw[:, i, :], w[HI][:, i, :].bitcast(F32), ALU.subtract).then_inc(w_split, 1)

            def context_low(G):
                pool.wait_ge(ctx_hi, G + 1)
                pool.tensor_tensor(cg[LO][:, :, :], ctx_raw[:, G % 2, :, :], cg[HI][:, :, :].bitcast(F32),
                                   ALU.subtract).then_inc(ctx_lo, 1)
            weight_low(0)
            context_low(0)
            for i in range(1, 4):
                weight_low(i)
            pool.memset(v[:, 1, :, :, :], 0.0).then_inc(v_cleared, 1)

            def context_high(G):
                pool.wait_ge(ctx_loaded[G % 2], 16 * (G // 2) + 16)
                pool.wait_ge(v_ready, G * KD)
                pool.tensor_copy(cg[HI][:, :, :], ctx_raw[:, G % 2, :, :]).then_inc(ctx_hi, 1)
            def split_expert(i):
                part, half, low = i // 4, i // 2 % 2, i % 2
                cols = slice(half * W_COLS // 2, (half + 1) * W_COLS // 2)
                raw, (hi, lo) = mem["expert_raw"][:, part, cols], (x[:, 0, part, cols] for x in mem["expert_w"])
                if i == 0:
                    pool.wait_ge(mem["expert_loaded"], 16)
                if not low:
                    pool.tensor_copy(hi, raw).then_inc(mem["expert_hi"] if half else half_hi, 1)
                else:
                    pool.wait_ge(mem["expert_hi"] if half else half_hi, part + 1)
                    pool.tensor_tensor(lo, raw, hi.bitcast(F32), ALU.subtract).then_inc(mem["expert_split"] if half else half_split, 1)

            def invert_next(G):
                ve = mem["ve"][:, G * GS:(G + 1) * GS]
                pool.wait_ge(mem["e_var_ready"], G + 1)
                pool.tensor_tensor(ve, ve, neghalf[:, 0:GS], ALU.pow).then_inc(mem["e_rstd_ready"], 1)
            context_high(1)
            context_low(1)
            for m in range(LAST_TICK + 2):
                t = m - 2
                if 0 <= t < TICKS:
                    b, r = divmod(t, TILES)
                    pool.wait_ge(inv_ready, t + 1)
                    pool.tensor_tensor(prob[:, b % 2, r, :, :], prob[:, b % 2, r, :, :],
                                       inv[:, b % 2, r, :].unsqueeze(2).broadcast_to([P, 4, P]), ALU.mult).then_inc(prob_ready, 1)
                G, i = divmod(m, GROUP_TICKS)
                if i == 4 and G + 1 < GROUPS:
                    norm_invert(pool, norm, G + 1)
                if i == 10 and G + 2 < GROUPS:
                    context_high(G + 2)
                if i == 12 and G + 2 < GROUPS:
                    context_low(G + 2)
                b = behind(m, ADD + 1)
                if b is not None:
                    add_bias(b)
                i, tick = divmod(m - EXPERT_TICK, 4)
                if tick == 0 and 0 <= i < 4 * W_PARTS:
                    split_expert(i)
                G, i = divmod(m - MEASURE_NEXT - 1, GROUP_TICKS)
                if i == 0 and 0 <= G < GROUPS - 1:
                    invert_next(G)
            invert_next(GROUPS - 1)

        @block.vector
        def _(dve):
            rows_of = lambda G: lambda i: X[:, G * GS + i, :]

            def normalise(G):
                if G > 0:
                    dve.wait_ge(tr_ready, G * KD)
                norm_apply(dve, norm, G, rows_of(G), lambda i: z[:, i, :])

            def job(G, j):
                kind, k = divmod(j, KD)
                n = G * KD + k
                bank = JOB[k]
                if kind == 0:
                    dve.wait_ge(k_ready, n + 1)
                    for par in range(2):
                        kc = dve.tensor_scalar(k_t[:, G % 2, par, k, :], bank[:, :], bk[:, k:k + 1], sel[:, par:par + 1],
                                               ALU.add, ALU.mult)
                    kc.then_inc(k_copied, 1)
                elif kind == 1:
                    dve.wait_ge(v_ready, n + 1)
                    if k == 0 and G < 2:
                        dve.wait_ge(v_cleared, G + 1)
                    for par in range(2):
                        heads_of = lambda x: x.rearrange("p s (h a d) -> p s h a d", a=2, d=XHEAD)[:, :, :, par, :]
                        vc = dve.tensor_tensor(heads_of(v[:, G % 2, par, 2 * k:2 * k + 2, :]),
                                               heads_of(bank[:, :].rearrange("p (s d) -> p s d", s=2)),
                                               heads_of(bv[:, :].unsqueeze(1).broadcast_to([P, 2, D])), ALU.add)
                    vc.then_inc(v_copied, 1)
                elif kind == 2:
                    dve.wait_ge(xh_ready, n + 1)
                    dve.tensor_tensor(xg[LO][:, k, :], bank[:, :], xg[HI][:, k, :].bitcast(F32),
                                      ALU.subtract).then_inc(xl_ready, 1)

            def measure_next(G):
                group = range(G * GS, (G + 1) * GS)
                dve.wait_ge(x_ready, G * GS + GS)
                for b in group:
                    dve.bn_stats(mem["stats"][:, b, :], X[:, b, :]).then_inc(mem["e_stats_ready"], 1)
                dve.wait_ge(mem["e_stats_ready"], G * GS + GS)
                for b in group:
                    dve.bn_aggr(mem["mv"][:, b, :], mem["stats"][:, b, :]).then_inc(mem["e_aggr_ready"], 1)
                dve.wait_ge(mem["e_aggr_ready"], G * GS + GS)
                dve.tensor_scalar(mem["ve"][:, G * GS:(G + 1) * GS], mem["mv"][:, G * GS:(G + 1) * GS, 1], EPS, None,
                                  ALU.add).then_inc(mem["e_var_ready"], 1)

            norm_measure(dve, norm, 0, rows_of(0))
            normalise(0)
            dve.wait_ge(bias_loaded, 64)
            dve.tensor_scalar(bq_scaled[:, :], bq[:, :], XHEAD ** -0.5, None, ALU.mult).then_inc(bq_ready, 1)
            dve.wait_ge(setup, 2 * TILES)
            for j in range(JOBS):
                job(0, j)
            for m in range(LAST_TICK + 1):
                if m < TICKS:
                    b, r = divmod(m, TILES)
                    dve.wait_ge(s_ready, m + 1)
                    dve.tensor_reduce(neg_max[:, b % 2, r, :], S[m % 2][:, :].rearrange("p (i k) -> p i k", i=4), AX.X,
                                      ALU.max, negate=True).then_inc(max_ready, 1)
                t = m - INVERT
                if 0 <= t < TICKS:
                    b, r = divmod(t, TILES)
                    dve.wait_ge(exp_ready, t + 1)
                    dve.reciprocal(inv[:, b % 2, r, :], total[:, b % 2, r, :]).then_inc(inv_ready, 1)
                t = m - TURN
                if 0 <= t < TICKS and t % 2 == 0:
                    b, r = divmod(t, TILES)
                    dve.wait_ge(pt_ready, t + 1)
                    dve.tensor_copy(prob_t[:, b % 2, r, :, :], PT[0][:, :].rearrange("p (i k) -> p i k", i=4)).then_inc(pt_dve, 1)
                b = behind(m, SPLIT_LOW)
                if b is not None:
                    dve.wait_ge(ot_hi, b + 1)
                    dve.tensor_tensor(o_t[LO][:, :, :], OT(b).rearrange("p (k t) -> p k t", k=KD),
                                      o_t[HI][:, :, :].bitcast(F32), ALU.subtract).then_inc(ot_lo, 1)
                b = behind(m, ADD)
                if b is not None:
                    dve.wait_ge(y_ready, b + 1)
                    dve.tensor_tensor(X[:, b, :], Y(b), X[:, b, :], ALU.add).then_inc(y_added, 1)
                for G, j in jobs_at(m - 1):
                    job(G, j)
                for G, j in jobs_at(m):
                    if j == 1:
                        norm_measure(dve, norm, G, rows_of(G))
                    elif j == 3:
                        normalise(G)
                G, i = divmod(m - MEASURE_NEXT, GROUP_TICKS)
                if i == 0 and 0 <= G < GROUPS - 1:
                    measure_next(G)
            measure_next(GROUPS - 1)

        @block.scalar
        def _(act):
            def job(G, j):
                kind, k = divmod(j, KD)
                n = G * KD + k
                if kind == 2:
                    act.wait_ge(tr_ready, n + 1)
                    act.activation(xg[HI][:, k, :], JOB[k][:, :], ACT.Copy).then_inc(xh_ready, 1)
                elif kind == 3:
                    act.wait_ge(q_ready, n + 1)
                    act.activation(q_t[:, G % 2, k, :], JOB[k][:, :], ACT.Identity, bias=bq_scaled[:, k:k + 1],
                                   scale=XHEAD ** -0.5).then_inc(q_copied, 1)

            def split_output(b):
                act.wait_ge(ot_ready, b + 1)
                act.activation(o_t[HI][:, :, :], OT(b).rearrange("p (k t) -> p k t", k=KD), ACT.Copy).then_inc(ot_hi, 1)

            for i in range(4):
                act.wait_ge(w_loaded[i], 16)
                act.activation(w[HI][:, i, :], w_raw[:, i, :], ACT.Copy).then_inc(w_hi, 1)
                if i == 0:
                    act.wait_ge(ctx_loaded[0], 16)
                    act.activation(cg[HI][:, :, :], ctx_raw[:, 0, :, :], ACT.Copy).then_inc(ctx_hi, 1)
            act.wait_ge(bq_ready, 1)
            for j in range(JOBS):
                job(0, j)
            for m in range(LAST_TICK + 1):
                if m < TICKS:
                    b, r = divmod(m, TILES)
                    act.wait_ge(max_ready, m + 1)
                    for i in range(4):
                        e = act.activation(prob[:, b % 2, r, i, :], S[m % 2][:, i * P:(i + 1) * P], ACT.Exp,
                                           bias=neg_max[:, b % 2, r, i:i + 1], accum_out=total[:, b % 2, r, i:i + 1])
                    e.then_inc(exp_ready, 1)
                t = m - TURN
                if 0 <= t < TICKS and t % 2 == 1:
                    b, r = divmod(t, TILES)
                    act.wait_ge(pt_ready, t + 1)
                    act.activation(prob_t[:, b % 2, r, :, :], PT[1][:, :].rearrange("p (i k) -> p i k", i=4),
                                   ACT.Copy).then_inc(pt_act, 1)
                b = behind(m, SPLIT_HIGH)
                if b is not None:
                    split_output(b)
                for G, j in jobs_at(m - 1):
                    job(G, j)

        @block.tensor
        def _(pe):
            def job(G, j):
                kind, k = divmod(j, KD)
                n = G * KD + k
                bank = JOB[k]
                if kind == 0:
                    if n == 0:
                        pe.wait_ge(w_split, 1)
                    pe.wait_ge(ctx_lo, G + 1)
                    if G > 0:
                        pe.wait_ge(q_copied, n - KD + 1)
                    for i in range(KD):
                        mm = product(pe, bank[:, :], [x[:, i, k * P:(k + 1) * P] for x in wk], [x[:, i, :] for x in cg],
                                     i == 0, i == KD - 1)
                    mm.then_inc(k_ready, 1)
                elif kind == 1:
                    if n == 0:
                        pe.wait_ge(w_split, 2)
                    pe.wait_ge(k_copied, n + 1)
                    for s in (2 * k, 2 * k + 1):
                        for i in range(KD):
                            mm = product(pe, bank[:, (s % 2) * D:(s % 2 + 1) * D], [x[:, i, s * P:(s + 1) * P] for x in cg],
                                         [x[:, i, :] for x in wv], i == 0, i == KD - 1)
                    mm.then_inc(v_ready, 1)
                elif kind == 2:
                    pe.wait_ge(norm["z_ready"], G * GS + GS)
                    pe.wait_ge(v_copied, n + 1)
                    for s in range(GS):
                        tr = pe.transpose(bank[:, s * P:(s + 1) * P], z[:, s, k * P:(k + 1) * P], ident[:, :])
                    tr.then_inc(tr_ready, 1)
                else:
                    if n == 0:
                        pe.wait_ge(w_split, 3)
                    pe.wait_ge(xl_ready, G * KD + KD)
                    for i in range(KD):
                        mm = product(pe, bank[:, :], [x[:, i, k * P:(k + 1) * P] for x in wq], [x[:, i, :] for x in xg],
                                     i == 0, i == KD - 1)
                    mm.then_inc(q_ready, 1)

            for j in range(JOBS):
                job(0, j)
            for m in range(LAST_TICK + 1):
                if m < TICKS:
                    b, r = divmod(m, TILES)
                    G, step = divmod(b, GS)
                    if m % GROUP_TICKS == 0:
                        pe.wait_ge(k_copied, G * KD + KD)
                        pe.wait_ge(q_copied, G * KD + KD)
                    if m >= 2:
                        pe.wait_ge(exp_ready, m - 1)
                    rows = slice(r * ROWT, (r + 1) * ROWT)
                    for i in range(4):
                        mm = pe.matmul(S[m % 2][:, i * P:(i + 1) * P], q_t[rows, G % 2, i // 2, step * P:(step + 1) * P],
                                       k_t[rows, G % 2, i % 2, i // 2, step * P:(step + 1) * P], start=True, stop=True,
                                       tile_position=(r * ROWT, 0))
                    mm.then_inc(s_ready, 1)
                t = m - TURN
                if 0 <= t < TICKS:
                    b, r = divmod(t, TILES)
                    pe.wait_ge(prob_ready, t + 1)
                    if t >= 2:
                        pe.wait_ge((pt_dve, pt_act)[t % 2], t // 2)
                    for i in range(4):
                        tr = pe.transpose(PT[t % 2][:, i * P:(i + 1) * P], prob[:, b % 2, r, i, :], ident[:, :])
                    tr.then_inc(pt_ready, 1)
                t = m - MEAN
                if 0 <= t < TICKS:
                    b, r = divmod(t, TILES)
                    G, s = divmod(b, GS)
                    if r == 0 and s == 0:
                        pe.wait_ge(v_copied, G * KD + KD)
                    if r == 0 and b >= 2:
                        pe.wait_ge(y_added, b - 1)
                    pe.wait_ge((pt_dve, pt_act)[t % 2], t // 2 + 1)
                    rows = slice(r * ROWT, (r + 1) * ROWT)
                    for i in range(4):
                        c, par = divmod(i, 2)
                        mm = pe.matmul(OT(b)[rows, c * P:(c + 1) * P],
                                       v[:, G % 2, par, s, c * P + r * ROWT:c * P + (r + 1) * ROWT], prob_t[:, b % 2, r, i, :],
                                       start=(par == 0), stop=(par == 1), tile_position=(0, r * ROWT))
                    if r == TILES - 1:
                        mm.then_inc(ot_ready, 1)
                b = behind(m, OUT)
                if b is not None:
                    if b == 0:
                        pe.wait_ge(w_split, 4)
                    pe.wait_ge(ot_hi, b + 1)
                    pe.wait_ge(ot_lo, b + 1)
                    for k in range(KD):
                        mm = product(pe, Y(b), [x[:, k, :] for x in o_t], [x[:, k, :] for x in wo], k == 0, k == KD - 1)
                    mm.then_inc(y_ready, 1)
                for G, j in jobs_at(m):
                    job(G, j)


def stage_experts(nc, ctx, io, mem):
    X, ident, neghalf, psum = mem["x"], mem["ident"], mem["neghalf"], mem["psum"]
    sb = lambda name, shape, dt=F32: ctx.enter_context(nc.sbuf_tensor("e_" + name, shape, dt))
    sem = lambda name: mem["sems"]("e_" + name)
    pair = lambda name, shape: (sb(name + "_hi", shape, F32R), sb(name + "_lo", shape, F32R))
    raw, w = mem["expert_raw"], mem["expert_w"]
    router_raw = sb("router_raw", [P, KD * EXPERTS])
    router = pair("router", [P, KD * EXPERTS])
    z = sb("z", [P, 2, GS, D])
    xn = pair("xn", [P, KD, SEQS * P])
    gate = sb("gate", [P, 2, GT])
    h_raw = sb("h_raw", [P, 2, GT])
    h = pair("h", [P, 2, KF, GT])
    logit_t = sb("logit_t", [EXPERTS, SEQS * P])
    table = lambda name: sb(name, [P, SEQS, EXPERTS])
    column = lambda name: sb(name, [P, SEQS])
    logit, prob, left, cand, first_hot, second_hot, share, iota = (table(x) for x in (
        "logit", "prob", "left", "cand", "first_hot", "second_hot", "share", "iota"))
    col = {name: column(name) for name in ("max", "sum", "inv", "p1", "p2", "at1", "at2", "e", "w1", "w2", "gap")}

    w_loaded, hi_ready, w_split = mem["expert_loaded"], mem["expert_hi"], mem["expert_split"]
    z_ready = sem("z_ready")
    split_seen = sem("split_seen")
    r_loaded, r_hi, r_split = sem("r_loaded"), sem("r_hi"), sem("r_split")
    iota_ready = sem("iota_ready")
    tr_ready, xh_ready, xl_ready = sem("tr_ready"), sem("xh_ready"), sem("xl_ready")
    logit_t_ready, logit_t_copied, logit_ready = sem("logit_t_ready"), sem("logit_t_copied"), sem("logit_ready")
    route_step, route_exp, route_sem = sem("route_step"), sem("route_exp"), sem("route_ready")
    gate_ready, up_ready = sem("gate_ready"), sem("up_ready")
    silu_ready, prod_ready = sem("silu_ready"), sem("prod_ready")
    h_hi, h_lo = sem("h_hi"), sem("h_lo")
    down_ready, added = sem("down_ready"), sem("added")
    GATE, UP = (psum[0], psum[1]), (psum[2], psum[3])
    DOWN = lambda G, half: psum[4 + 2 * (G % 2) + half]
    TR = lambda G, k: psum[4 + 2 * (G % 2) + k]
    PAIRS = EXPERTS // 2

    def steps(eng, ahead, rest):
        ahead(0, 0, 0)

        def body(pairs, last):
            for slot in range(2):
                e = pairs * 2 + slot
                for G in range(GROUPS):
                    if G < GROUPS - 1:
                        ahead(e, slot, G + 1)
                    elif not (last and slot == 1):
                        ahead(e + 1, 1 - slot, 0)
                    rest(e, slot, G)
        body(0, False)
        with eng.Fori(1, PAIRS - 1) as pairs:
            body(pairs, False)
        body(PAIRS - 1, True)

    early = lambda n, least: isinstance(n, int) and n < least

    with nc.Block() as block:
        @block.sync
        def _(sp):
            sp.dma_start(router_raw[:, :], io["router_laid"]).then_inc(r_loaded, 16)
            with sp.Fori(1, EXPERTS) as e:
                sp.wait_ge(w_split, e * W_PARTS)
                sp.dma_start(raw[:, :, :], io["experts_laid"][bass.ds(e, 1)].rearrange(
                    "e p (a n) -> p (e a) n", a=W_PARTS)).then_inc(w_loaded, 16)

        @block.gpsimd
        def _(pool):
            def split(e, slot, part):
                if part == 0:
                    pool.wait_ge(w_loaded, e * 16 + 16)
                    if not early(e, 2):
                        pool.wait_ge(down_ready, e * GROUPS - GROUPS)
                    pool.sem_inc(split_seen, 1)
                pool.tensor_copy(w[HI][:, slot, part, :], raw[:, part, :]).then_inc(hi_ready, 1)
                pool.wait_ge(hi_ready, e * W_PARTS + part + 1)
                pool.tensor_tensor(w[LO][:, slot, part, :], raw[:, part, :], w[HI][:, slot, part, :].bitcast(F32),
                                   ALU.subtract).then_inc(w_split, 1)

            def h_low(e, slot, G):
                n = e * GROUPS + G
                for f in range(KF):
                    pool.wait_ge(h_hi, n * KF + f + 1)
                    pool.tensor_tensor(h[LO][:, G % 2, f, :], h_raw[:, f % 2, :], h[HI][:, G % 2, f, :].bitcast(F32),
                                       ALU.subtract).then_inc(h_lo, 1)

            pool.iota(iota[:, :, :], pattern=[[0, SEQS], [1, EXPERTS]], base=0, channel_multiplier=0,
                      allow_small_or_imprecise_dtypes=True).then_inc(iota_ready, 1)
            pool.wait_ge(r_loaded, 16)
            pool.tensor_copy(router[HI][:, :], router_raw[:, :]).then_inc(r_hi, 1)
            pool.wait_ge(r_hi, 1)
            pool.tensor_tensor(router[LO][:, :], router_raw[:, :], router[HI][:, :].bitcast(F32),
                               ALU.subtract).then_inc(r_split, 1)

            def body(pairs, last):
                for slot in range(2):
                    e = pairs * 2 + slot
                    for G in range(GROUPS):
                        h_low(e, slot, G)
                        if G < W_PARTS and not (last and slot == 1):
                            split(e + 1, 1 - slot, G)
            body(0, False)
            with pool.Fori(1, PAIRS - 1) as pairs:
                body(pairs, False)
            body(PAIRS - 1, True)

        @block.tensor
        def _(pe):
            def turn(G):
                pe.wait_ge(z_ready, G * GS + GS)
                if G > 1:
                    pe.wait_ge(xl_ready, (G - 1) * KD)
                for k in range(KD):
                    for s in range(GS):
                        tr = pe.transpose(TR(G, k)[:, s * P:(s + 1) * P], z[:, G % 2, s, k * P:(k + 1) * P], ident[:, :])
                    tr.then_inc(tr_ready, 1)

            def route():
                pe.wait_ge(r_split, 1)
                pe.wait_ge(xl_ready, GROUPS * KD)
                for G in range(GROUPS):
                    for k in range(KD):
                        mm = product(pe, psum[4 + G][0:EXPERTS, :], [x[:, k * EXPERTS:(k + 1) * EXPERTS] for x in router],
                                     [x[:, k, G * GT:(G + 1) * GT] for x in xn], k == 0, k == KD - 1)
                    mm.then_inc(logit_t_ready, 1)
                pe.wait_ge(logit_t_copied, GROUPS)
                for b in range(SEQS):
                    tr = pe.transpose(psum[5][:, b * EXPERTS:(b + 1) * EXPERTS], logit_t[0:EXPERTS, b * P:(b + 1) * P],
                                      ident[0:EXPERTS, 0:EXPERTS])
                tr.then_inc(logit_ready, 1)
            turn(0)
            turn(1)

            def widen(e, slot, G):
                n = e * GROUPS + G
                tokens = slice(G * GT, (G + 1) * GT)
                if G == 0:
                    pe.wait_ge(w_split, e * W_PARTS + 2)
                if early(n, GROUPS):
                    pe.wait_ge(xl_ready, G * KD + KD)
                for f in range(KF):
                    for part, bank, ready, read in ((0, GATE[f % 2], gate_ready, silu_ready),
                                                    (1, UP[f % 2], up_ready, prod_ready)):
                        if not early(n * KF + f, 2):
                            pe.wait_ge(read, n * KF + f - 1)
                        for k in range(KD):
                            mm = product(pe, bank[:, :], [x[:, slot, part, k * FFN + f * P:k * FFN + (f + 1) * P] for x in w],
                                         [x[:, k, tokens] for x in xn], k == 0, k == KD - 1)
                        mm.then_inc(ready, 1)
                if early(n, 1):
                    turn(2)
                    turn(3)
                elif early(n, 2):
                    route()

            def down(e, slot, G):
                n = e * GROUPS + G
                if G == 0:
                    pe.wait_ge(w_split, e * W_PARTS + 3)
                if not early(n, 2):
                    pe.wait_ge(added, n * GS - GS)
                if early(n, 2):
                    pe.wait_ge(route_step, 1)
                pe.wait_ge(h_hi, n * KF + KF)
                pe.wait_ge(h_lo, n * KF + KF)
                for s in range(GS):
                    out = DOWN(G, s // 2)[:, (s % 2) * D:(s % 2 + 1) * D]
                    for f in range(KF):
                        mm = product(pe, out, [x[:, G % 2, f, s * P:(s + 1) * P] for x in h], [x[:, slot, 2, f * D:(f + 1) * D] for x in w],
                                     f == 0, f == KF - 1)
                mm.then_inc(down_ready, 1)
            steps(pe, widen, down)

        @block.scalar
        def _(act):
            def tokens_high(G):
                for k in range(KD):
                    act.wait_ge(tr_ready, G * KD + k + 1)
                    act.activation(xn[HI][:, k, G * GT:(G + 1) * GT], TR(G, k)[:, :], ACT.Copy).then_inc(xh_ready, 1)

            def route(i, out, in_):
                act.wait_ge(route_exp, i + 1)
                act.activation(out, in_, ACT.Exp).then_inc(route_sem, 1)
            tokens_high(0)
            tokens_high(1)

            def silu(n, f):
                act.wait_ge(gate_ready, n * KF + f + 1)
                if not early(n * KF + f, 2):
                    act.wait_ge(prod_ready, n * KF + f - 1)
                act.activation(gate[:, f % 2, :], GATE[f % 2][:, :], ACT.Silu).then_inc(silu_ready, 1)

            def high(n, G, f):
                act.wait_ge(prod_ready, n * KF + f + 1)
                if f == 0 and not early(n, 2):
                    act.wait_ge(down_ready, n - 1)
                act.activation(h[HI][:, G % 2, f, :], h_raw[:, f % 2, :], ACT.Copy).then_inc(h_hi, 1)

            def step(e, slot, G):
                n = e * GROUPS + G
                silu(n, 0)
                for f in range(1, KF):
                    silu(n, f)
                    high(n, G, f - 1)
                    if early(n, 3) and n == 2 and f == 1:
                        route(0, prob[:, :, :], logit[:, :, :])
                    elif early(n, 3) and n == 2 and f == 3:
                        route(1, col["e"][:, :], col["gap"][:, :])
                high(n, G, KF - 1)
                if early(n, 1):
                    tokens_high(2)
                    tokens_high(3)
                elif early(n, 2):
                    for group in range(GROUPS):
                        act.wait_ge(logit_t_ready, group + 1)
                        act.activation(logit_t[0:EXPERTS, group * GT:(group + 1) * GT], psum[4 + group][0:EXPERTS, :],
                                       ACT.Copy).then_inc(logit_t_copied, 1)
            for G in range(GROUPS):
                step(0, 0, G)
            with act.Fori(1, EXPERTS) as e:
                for G in range(GROUPS):
                    step(e, None, G)

        @block.vector
        def _(dve):
            x_row = lambda G: lambda i: X[:, G * GS + i, :]
            def normalise(G):
                dve.wait_ge(mem["e_rstd_ready"], G + 1)
                if G > 1:
                    dve.wait_ge(tr_ready, (G - 1) * KD)
                for i in range(GS):
                    b = G * GS + i
                    dve.tensor_scalar(z[:, G % 2, i, :], X[:, b, :], mem["mv"][:, b, 0:1], mem["ve"][:, b:b + 1],
                                      ALU.subtract, ALU.mult).then_inc(z_ready, 1)

            def tokens_low(G):
                for k in range(KD):
                    dve.wait_ge(xh_ready, G * KD + k + 1)
                    tokens = slice(G * GT, (G + 1) * GT)
                    dve.tensor_tensor(xn[LO][:, k, tokens], TR(G, k)[:, :], xn[HI][:, k, tokens].bitcast(F32),
                                      ALU.subtract).then_inc(xl_ready, 1)
            normalise(0)
            normalise(1)
            tokens_low(0)
            normalise(2)
            tokens_low(1)
            normalise(3)

            count = [0]

            def then(op):
                count[0] += 1
                op.then_inc(route_step, 1)
                dve.wait_ge(route_step, count[0])
            wide = lambda name: col[name][:, :].unsqueeze(2).broadcast_to([P, SEQS, EXPERTS])

            def largest(values, value, at, hot):
                then(dve.tensor_reduce(col[value][:, :], values[:, :, :], AX.X, ALU.max))
                then(dve.tensor_tensor(cand[:, :, :], values[:, :, :], wide(value), ALU.is_equal))
                then(dve.scalar_tensor_tensor(out=cand[:, :, :], in0=cand[:, :, :], scalar=-float(EXPERTS),
                                              in1=iota[:, :, :], op0=ALU.mult, op1=ALU.add))
                then(dve.tensor_reduce(col[at][:, :], cand[:, :, :], AX.X, ALU.min))
                then(dve.tensor_tensor(hot[:, :, :], cand[:, :, :], wide(at), ALU.is_equal))

            def route(part):
                if part == 0:
                    dve.wait_ge(iota_ready, 1)
                    then(dve.tensor_reduce(col["max"][:, :], logit[:, :, :], AX.X, ALU.max))
                    dve.tensor_tensor(logit[:, :, :], logit[:, :, :], wide("max"), ALU.subtract).then_inc(route_exp, 1)
                elif part == 1:
                    dve.wait_ge(route_sem, 1)
                    then(dve.tensor_reduce(col["sum"][:, :], prob[:, :, :], AX.X, ALU.add))
                    then(dve.reciprocal(col["inv"][:, :], col["sum"][:, :]))
                    then(dve.tensor_tensor(prob[:, :, :], prob[:, :, :], wide("inv"), ALU.mult))
                    largest(prob, "p1", "at1", first_hot)
                elif part == 2:
                    then(dve.scalar_tensor_tensor(out=left[:, :, :], in0=first_hot[:, :, :], scalar=-4.0, in1=prob[:, :, :],
                                                  op0=ALU.mult, op1=ALU.add))
                    largest(left, "p2", "at2", second_hot)
                    dve.tensor_tensor(col["gap"][:, :], col["p2"][:, :], col["p1"][:, :], ALU.subtract).then_inc(route_exp, 1)
                else:
                    dve.wait_ge(route_sem, 2)
                    then(dve.tensor_scalar(col["sum"][:, :], col["e"][:, :], 1.0, None, ALU.add))
                    then(dve.reciprocal(col["w1"][:, :], col["sum"][:, :]))
                    then(dve.tensor_tensor(col["w2"][:, :], col["e"][:, :], col["w1"][:, :], ALU.mult))
                    then(dve.tensor_tensor(first_hot[:, :, :], first_hot[:, :, :], wide("w1"), ALU.mult))
                    then(dve.tensor_tensor(second_hot[:, :, :], second_hot[:, :, :], wide("w2"), ALU.mult))
                    then(dve.tensor_tensor(share[:, :, :], first_hot[:, :, :], second_hot[:, :, :], ALU.add))

            def fuse(e, slot, G):
                n = e * GROUPS + G
                for f in range(KF):
                    dve.wait_ge(silu_ready, n * KF + f + 1)
                    dve.wait_ge(up_ready, n * KF + f + 1)
                    if not early(n * KF + f, 2):
                        dve.wait_ge(h_hi, n * KF + f - 1)
                        dve.wait_ge(h_lo, n * KF + f - 1)
                    dve.tensor_tensor(h_raw[:, f % 2, :], gate[:, f % 2, :], UP[f % 2][:, :], ALU.mult).then_inc(prod_ready, 1)
                    if early(n, 3) and n == 2:
                        route(f)
                if early(n, 1):
                    tokens_low(2)
                    tokens_low(3)
                elif early(n, 2):
                    dve.wait_ge(logit_ready, 1)
                    then(dve.tensor_copy(logit[:, :, :], psum[5][:, 0:SEQS * EXPERTS].rearrange("p (b e) -> p b e", b=SEQS)))

            def add(e, slot, G):
                n = e * GROUPS + G
                if early(n, 1):
                    return
                if early(n, 2):
                    add_group(0, 0)
                add_group(e, G)

            def add_group(e, G):
                n = e * GROUPS + G
                dve.wait_ge(down_ready, n + 1)
                if not early(n, GROUPS):
                    dve.wait_ge(added, n * GS - (GROUPS - 1) * GS)
                for s in range(GS):
                    b = G * GS + s
                    dve.scalar_tensor_tensor(out=X[:, b, :], in0=DOWN(G, s // 2)[:, (s % 2) * D:(s % 2 + 1) * D],
                                             scalar=share[:, b, bass.ds(e, 1)], in1=X[:, b, :], op0=ALU.mult,
                                             op1=ALU.add).then_inc(added, 1)
            steps(dve, fuse, add)


MAGIC = 1.5 * 2.0 ** 23
INT8_MAX = 127.0


def stage_second_layer(nc, ctx, io, mem, out):
    X, ident, ident_bf, psum = mem["x"], mem["ident"], mem["ident_bf"], mem["psum"]
    sb = lambda name, shape, dt=F32: ctx.enter_context(nc.sbuf_tensor("l_" + name, shape, dt))
    sem = lambda name: mem["sems"]("l_" + name)
    pair = lambda name, shape: (sb(name + "_hi", shape, F32R), sb(name + "_lo", shape, F32R))
    norm_a, norm_c, norm_x, norm_q, norm_o, norm_f = (norm_state(nc, ctx, mem, "l" + n, GS) for n in "acxqof")
    for name, norm in (("a", norm_a), ("c", norm_c), ("q", norm_q)):
        norm["shift"], norm["neg_mean"] = sb("shift_" + name, [P, GS]), sb("neg_mean_" + name, [P, GS])
        norm["shift_ready"], norm["neg_mean_ready"] = sem("shift_ready_" + name), sem("neg_mean_ready_" + name)
    neg_one = sb("neg_one", [P, GS])
    neg_one_ready = sem("neg_one_ready")

    w_raw = sb("w_raw", [P, 3, KD * D])
    w = pair("w", [P, 3, KD * D])
    wq, wk, wv = (chunks_of(w, i, KD) for i in range(3))
    z = sb("z", [P, GS, D])
    xg = pair("xg", [P, KD, GT])
    q_t, k_t = sb("q_t", [P, KD, GT]), sb("k_t", [P, KD, GT])
    v = sb("v", [P, GS, D])
    prob, prob_t = sb("prob", [P, GS, P]), sb("prob_t", [P, GS, P])
    neg_max, total, inv = sb("neg_max", [P, GS]), sb("total", [P, GS]), sb("inv", [P, GS])
    w_loaded = [sem(f"w_loaded{i}") for i in range(3)]
    w_hi, w_split = sem("w_hi"), sem("w_split")
    tr_ready, xh_ready, xl_ready = sem("tr_ready"), sem("xh_ready"), sem("xl_ready")
    q_ready, k_ready, v_ready = sem("q_ready"), sem("k_ready"), sem("v_ready")
    q_copied, k_copied, v_copied = sem("q_copied"), sem("k_copied"), sem("v_copied")
    s_ready, max_ready, exp_ready = sem("s_ready"), sem("max_ready"), sem("exp_ready")
    pt_ready, pt_copied = sem("pt_ready"), sem("pt_copied")
    o_ready, inv_ready, added = sem("o_ready"), sem("inv_ready"), sem("added")

    context = sb("context", [P, 2, GS, D])
    gains = sb("gains", [P, 4, KD])
    scaled = sb("scaled", [P, 2, KD])
    factor, inv_factor = sb("factor", [P, 1]), sb("inv_factor", [P, 1])
    rows = sb("rows", [P, 4, D])
    z1, z2, cn = sb("z1", [P, GS, D]), sb("z2", [P, GS, D]), sb("cn", [P, GS, D])
    cq_t, ck_t = sb("cq_t", [P, KD, GT]), sb("ck_t", [P, 2, KD, GT])
    cv = sb("cv", [P, 2, GS, D])
    vg = sb("vg", [P, GS, D])
    cprob, cprob_t = sb("cprob", [P, GS, P]), sb("cprob_t", [P, GS, P])
    cneg_max, ctotal, cinv = sb("cneg_max", [P, GS]), sb("ctotal", [P, GS]), sb("cinv", [P, GS])
    o, og = sb("o", [P, GS, D]), sb("og", [P, GS, D])
    c_loaded = [sem(f"c_loaded{i}") for i in range(2)]
    p_loaded = sem("p_loaded")
    inv_factor_ready, scaled_ready = sem("inv_factor_ready"), sem("scaled_ready")
    qtr_ready, ktr_ready = sem("qtr_ready"), sem("ktr_ready")
    cq_ready, ck_ready, vg_ready, cv_ready = sem("cq_ready"), sem("ck_ready"), sem("vg_ready"), sem("cv_ready")
    cs_ready, cmax_ready, cexp_ready = sem("cs_ready"), sem("cmax_ready"), sem("cexp_ready")
    cpt_ready, cpt_copied = sem("cpt_ready"), sem("cpt_copied")
    co_ready, cinv_ready, co_scaled = sem("co_ready"), sem("cinv_ready"), sem("co_scaled")
    og_ready, xb_ready, x_ready = sem("og_ready"), sem("xb_ready"), sem("x_ready")
    wide = lambda i: rows[:, i, :].unsqueeze(1).broadcast_to([P, GS, D])

    zf, t1, t2 = (sb(n, [P, GS, D]) for n in ("zf", "t1", "t2"))
    zq = sb("zq", [P, GS, D], BF16)
    xq_t = sb("xq_t", [P, GS * KD, P], BF16)
    amax, scale, inv_scale = (sb(n, [P, 2, GS]) for n in ("amax", "scale", "inv_scale"))
    product_out = sb("product_out", [P, 2, GS, D])
    wf, wt1, wt2 = (sb(n, [P, KD, D]) for n in ("wf", "wt1", "wt2"))
    wfq = sb("wfq", [P, KD, D], BF16)
    wfq_t = sb("wfq_t", [P, KD, D], BF16)
    w_amax, w_scale, w_inv = (sb(n, [P, KD]) for n in ("w_amax", "w_scale", "w_inv"))
    ones = sb("ones", [P, P])
    diag = sb("diag", [P, KD, P])
    col_scale = sb("col_scale", [P, D])
    wf_loaded, ones_ready, w_step = sem("wf_loaded"), sem("ones_ready"), sem("w_step")
    wtr_ready, wt_ready, scales_ready, col_scale_ready = (sem(n) for n in (
        "wtr_ready", "wt_ready", "scales_ready", "col_scale_ready"))
    q_step, rounded, quantised = sem("q_step"), sem("rounded"), sem("quantised")
    ftr_ready, ftr_copied, fy_ready, fy_scaled, fx_ready = (sem(n) for n in (
        "ftr_ready", "ftr_copied", "fy_ready", "fy_scaled", "fx_ready"))
    stored = sem("stored")

    TR = K = psum[0:2]
    S, PT = psum[0], psum[1]
    Q = V = O = psum[2:4]
    CT = CO = psum[4:6]
    CS, CPT = psum[6], psum[7]
    FT, FY = psum[6], psum[6:8]

    (MEASURE, TURN, PROJECT, VALUES, SCORES, PROBS, ADD,
     MEASURE_X, MEASURE_Q, TURN_Q, CSCORES, CPROBS, COUT, MEASURE_O, CADD,
     MEASURE_F, SCALE_F, QUANTISE, MULTIPLY, STORE, PHASES) = range(21)
    MEASURE_C, NORM_C, TURN_C, VALUE_C = VALUES, SCORES, PROBS, ADD
    APART = 5
    SETUP, SETUP_TURN = 3, 4

    def schedule():
        for step in range(APART * (GROUPS - 1) + PHASES):
            for G in range(GROUPS):
                if 0 <= step - APART * G < PHASES:
                    yield step, step - APART * G, G

    x_rows = lambda G: lambda i: X[:, G * GS + i, :]
    c_rows = lambda G: lambda i: context[:, G % 2, i, :]

    def invert_and_shift(pool, norm, G):
        pool.wait_ge(norm["var_ready"], G + 1)
        pool.tensor_tensor(norm["neg_mean"][:, :], norm["mv"][:, :, 0], neg_one[:, :], ALU.mult).then_inc(norm["neg_mean_ready"], 1)
        norm_invert(pool, norm, G)
        pool.wait_ge(norm["rstd_ready"], G + 1)
        pool.wait_ge(norm["neg_mean_ready"], G + 1)
        pool.tensor_tensor(norm["shift"][:, :], norm["neg_mean"][:, :], norm["ve"][:, :], ALU.mult).then_inc(norm["shift_ready"], 1)

    def apply_on_act(act, norm, G, rows, outs):
        act.wait_ge(norm["shift_ready"], G + 1)
        for i in range(GS):
            act.activation(outs(i), rows(i), ACT.Identity, bias=norm["shift"][:, i:i + 1],
                           scale=norm["ve"][:, i:i + 1]).then_inc(norm["z_ready"], 1)

    with nc.Block() as block:
        @block.sync
        def _(sp):
            for i, name in enumerate(("Wq", "Wk", "Wv")):
                sp.dma_start(w_raw[:, i, :], io["L1_attn_" + name + "_laid"]).then_inc(w_loaded[i], 16)
            load_context = lambda G: sp.dma_start(context[:, G % 2, :, :], io["ctx_1024"][G * GS:(G + 1) * GS].rearrange(
                "b t d -> t b d")).then_inc(c_loaded[G % 2], 16)
            sp.dma_start(wf[:, :, :], io["rhs_laid"]).then_inc(wf_loaded, 16)
            load_context(0)
            sp.dma_start(gains[:, :, :], io["qk_gains_laid"]).then_inc(p_loaded, 16)
            sp.dma_start(factor[:, :], io["L1_xattn_inv_scale_factor"].broadcast_to([P, 1])).then_inc(p_loaded, 16)
            for i, name in enumerate(("ln3_w", "ln3_b", "ln4_w", "ln4_b")):
                sp.dma_start(rows[:, i, :], io["L1_xattn_" + name].unsqueeze(0).broadcast_to([P, D])).then_inc(p_loaded, 16)
            load_context(1)
            for G in range(2, GROUPS):
                sp.wait_ge(norm_c["z_ready"], (G - 1) * GS)
                load_context(G)
            for h in range(2 * GROUPS):
                sp.wait_ge(fx_ready, h + 1)
                sp.dma_start(out[2 * h:2 * h + 2].rearrange("b t d -> t b d"), X[:, 2 * h:2 * h + 2, :]).then_inc(stored, 16)
            sp.wait_ge(stored, 16 * 2 * GROUPS)

        @block.gpsimd
        def _(pool):
            pool.memset(neg_one[:, :], -1.0).then_inc(neg_one_ready, 1)
            pool.wait_ge(neg_one_ready, 1)
            pool.memset(ones[:, :], 1.0).then_inc(ones_ready, 1)
            for step, phase, G in schedule():
                if phase == MEASURE:
                    invert_and_shift(pool, norm_a, G)
                    if G == 0:
                        for i in range(3):
                            pool.wait_ge(w_hi, i + 1)
                            pool.tensor_tensor(w[LO][:, i, :], w_raw[:, i, :], w[HI][:, i, :].bitcast(F32),
                                               ALU.subtract).then_inc(w_split, 1)
                elif phase == MEASURE_C:
                    invert_and_shift(pool, norm_c, G)
                elif phase == VALUE_C:
                    if G == 0:
                        pool.wait_ge(p_loaded, 96)
                    pool.wait_ge(norm_c["z_ready"], G * GS + GS)
                    pool.tensor_tensor(vg[:, :, :], cn[:, :, :], wide(0), ALU.mult).then_inc(vg_ready, 1)
                    pool.wait_ge(vg_ready, G + 1)
                    if G >= 2:
                        pool.wait_ge(co_ready, G - 1)
                    pool.tensor_tensor(cv[:, G % 2, :, :], vg[:, :, :], wide(1), ALU.add).then_inc(cv_ready, 1)
                elif phase == MEASURE_X:
                    norm_invert(pool, norm_x, G)
                elif phase == MEASURE_Q:
                    invert_and_shift(pool, norm_q, G)
                elif phase == CPROBS:
                    pool.wait_ge(norm_x["z_ready"], G * GS + GS)
                    group = X[:, G * GS:(G + 1) * GS, :]
                    pool.tensor_tensor(group, group, wide(3), ALU.add).then_inc(xb_ready, 1)
                elif phase == MEASURE_O:
                    norm_invert(pool, norm_o, G)
                elif phase == MEASURE_F:
                    norm_invert(pool, norm_f, G)
                elif phase == STORE:
                    for h in range(2):
                        b = G * GS + 2 * h
                        pool.wait_ge(fy_scaled, b + 2)
                        pool.tensor_tensor(X[:, b:b + 2, :], X[:, b:b + 2, :], product_out[:, G % 2, 2 * h:2 * h + 2, :],
                                           ALU.add).then_inc(fx_ready, 1)

        @block.tensor
        def _(pe):
            def turn(banks, rows, ready):
                for k in range(KD):
                    for s in range(GS):
                        tr = pe.transpose(banks[k][:, s * P:(s + 1) * P], rows[:, s, k * P:(k + 1) * P], ident[:, :])
                    tr.then_inc(ready, 1)

            def scores(bank, qs, ks, ready):
                for s in range(GS):
                    t = slice(s * P, (s + 1) * P)
                    for k in range(KD):
                        mm = pe.matmul(bank[:, t], qs[:, k, t], ks[:, k, t], start=(k == 0), stop=(k == KD - 1))
                mm.then_inc(ready, 1)

            def turn_probs(bank, probs, ready):
                for s in range(GS):
                    tr = pe.transpose(bank[:, s * P:(s + 1) * P], probs[:, s, :], ident[:, :])
                tr.then_inc(ready, 1)

            def outputs(banks, probs_t, vs, ready):
                for s in range(GS):
                    mm = pe.matmul(banks[s // 2][:, (s % 2) * D:(s % 2 + 1) * D], probs_t[:, s, :], vs[:, s, :],
                                   start=True, stop=True)
                mm.then_inc(ready, 1)

            def project(banks, weights, ready):
                for k in range(KD):
                    for j in range(KD):
                        mm = product(pe, banks[k][:, :], [x[:, j, k * P:(k + 1) * P] for x in weights],
                                     [x[:, j, :] for x in xg], j == 0, j == KD - 1)
                    mm.then_inc(ready, 1)

            for step, phase, G in schedule():
                if step == SETUP_TURN and G == 0:
                    pe.wait_ge(w_step, 5 + KD)
                    for c in range(KD):
                        for k in range(KD):
                            tr = pe.transpose(CS[:, :].bitcast(BF16)[:, k * D + c * P:k * D + (c + 1) * P],
                                              wfq[:, c, k * P:(k + 1) * P], ident_bf[:, :])
                    tr.then_inc(wtr_ready, 1)
                    pe.wait_ge(ones_ready, 1)
                    pe.wait_ge(w_step, 5 + 2 * KD)
                    for c in range(KD):
                        mm = pe.matmul(CPT[:, c * P:(c + 1) * P], ones[:, :], diag[:, c, :], start=True, stop=True)
                    mm.then_inc(scales_ready, 1)
                if phase == TURN:
                    pe.wait_ge(norm_a["z_ready"], G * GS + GS)
                    if G > 0:
                        pe.wait_ge(pt_copied, G)
                    turn(TR, z, tr_ready)
                elif phase == PROJECT:
                    pe.wait_ge(xl_ready, G * KD + KD)
                    if G == 0:
                        pe.wait_ge(w_split, 1)
                    else:
                        pe.wait_ge(added, G * GS)
                    project(Q, wq, q_ready)
                    if G == 0:
                        pe.wait_ge(w_split, 2)
                    project(K, wk, k_ready)
                elif phase == VALUES:
                    if G == 0:
                        pe.wait_ge(w_split, 3)
                    pe.wait_ge(q_copied, G * KD + KD)
                    for h in range(2):
                        for s in (2 * h, 2 * h + 1):
                            for j in range(KD):
                                mm = product(pe, V[h][:, (s % 2) * D:(s % 2 + 1) * D],
                                             [x[:, j, s * P:(s + 1) * P] for x in xg], [x[:, j, :] for x in wv],
                                             j == 0, j == KD - 1)
                        mm.then_inc(v_ready, 1)
                elif phase == SCORES:
                    pe.wait_ge(k_copied, G * KD + KD)
                    scores(S, q_t, k_t, s_ready)
                elif phase == PROBS:
                    pe.wait_ge(exp_ready, G + 1)
                    turn_probs(PT, prob, pt_ready)
                    pe.wait_ge(norm_c["z_ready"], G * GS + GS)
                    if G > 0:
                        pe.wait_ge(cq_ready, G * KD)
                    turn(CT, cn, ktr_ready)
                elif phase == ADD:
                    pe.wait_ge(pt_copied, G + 1)
                    pe.wait_ge(v_copied, G * 2 + 2)
                    outputs(O, prob_t, v, o_ready)
                elif phase == TURN_Q:
                    pe.wait_ge(norm_q["z_ready"], G * GS + GS)
                    pe.wait_ge(ck_ready, G * KD + KD)
                    if G > 0:
                        pe.wait_ge(co_scaled, G * GS)
                    turn(CT, z2, qtr_ready)
                elif phase == CSCORES:
                    if G == 0:
                        pe.wait_ge(wt_ready, 1)
                        pe.wait_ge(col_scale_ready, 1)
                    if G >= 2:
                        pe.wait_ge(fy_scaled, (G - 1) * GS)
                    pe.wait_ge(cq_ready, G * KD + KD)
                    scores(CS, cq_t, ck_t[:, G % 2, :, :], cs_ready)
                elif phase == CPROBS:
                    pe.wait_ge(cexp_ready, G + 1)
                    turn_probs(CPT, cprob, cpt_ready)
                elif phase == COUT:
                    pe.wait_ge(cpt_copied, G + 1)
                    pe.wait_ge(cv_ready, G + 1)
                    if G + 1 < GROUPS:
                        pe.wait_ge(ck_ready, (G + 1) * KD + KD)
                    outputs(CO, cprob_t, cv[:, G % 2, :, :], co_ready)
                elif phase == QUANTISE:
                    pe.wait_ge(quantised, G + 1)
                    if G > 0:
                        pe.wait_ge(fy_scaled, G * GS)
                    for s in range(GS):
                        for k in range(KD):
                            i = s * KD + k
                            tr = pe.transpose(FT[:, :].bitcast(BF16)[:, i * P:(i + 1) * P], zq[:, s, k * P:(k + 1) * P],
                                              ident_bf[:, :])
                    tr.then_inc(ftr_ready, 1)
                elif phase == MULTIPLY:
                    pe.wait_ge(ftr_copied, G + 1)
                    for s in range(GS):
                        for k in range(KD):
                            mm = pe.matmul(FY[s // 2][:, (s % 2) * D:(s % 2 + 1) * D], xq_t[:, s * KD + k, :],
                                           wfq_t[:, k, :], start=(k == 0), stop=(k == KD - 1))
                    mm.then_inc(fy_ready, 1)

        @block.scalar
        def _(act):
            def exponentials(bank, probs, maxima, sums, ready):
                for s in range(GS):
                    e = act.activation(probs[:, s, :], bank[:, s * P:(s + 1) * P], ACT.Exp, bias=maxima[:, s:s + 1],
                                       accum_out=sums[:, s:s + 1])
                e.then_inc(ready, 1)

            for i in range(3):
                act.wait_ge(w_loaded[i], 16)
                act.activation(w[HI][:, i, :], w_raw[:, i, :], ACT.Copy).then_inc(w_hi, 1)
            for step, phase, G in schedule():
                if step == SETUP_TURN and G == 0:
                    act.wait_ge(wtr_ready, 1)
                    act.activation(wfq_t[:, :, :], CS[:, :].bitcast(BF16)[:, 0:KD * D].rearrange("p (k n) -> p k n", k=KD),
                                   ACT.Copy).then_inc(wt_ready, 1)
                    act.wait_ge(scales_ready, 1)
                    act.activation(col_scale[:, :], CPT[:, 0:D], ACT.Copy).then_inc(col_scale_ready, 1)
                if phase == TURN:
                    if G > 0:
                        act.wait_ge(tr_ready, G * KD)
                    apply_on_act(act, norm_a, G, x_rows(G), lambda i: z[:, i, :])
                    for k in range(KD):
                        act.wait_ge(tr_ready, G * KD + k + 1)
                        act.activation(xg[HI][:, k, :], TR[k][:, :], ACT.Copy).then_inc(xh_ready, 1)
                elif phase == PROJECT:
                    for k in range(KD):
                        act.wait_ge(q_ready, G * KD + k + 1)
                        act.activation(q_t[:, k, :], Q[k][:, :], ACT.Copy, scale=D ** -0.5).then_inc(q_copied, 1)
                elif phase == VALUES:
                    for k in range(KD):
                        act.wait_ge(k_ready, G * KD + k + 1)
                        act.activation(k_t[:, k, :], K[k][:, :], ACT.Copy).then_inc(k_copied, 1)
                    for h in range(2):
                        act.wait_ge(v_ready, G * 2 + h + 1)
                        act.activation(v[:, 2 * h:2 * h + 2, :], V[h][:, :].rearrange("p (s d) -> p s d", s=2),
                                       ACT.Copy).then_inc(v_copied, 1)
                elif phase == SCORES:
                    act.wait_ge(max_ready, G + 1)
                    exponentials(S, prob, neg_max, total, exp_ready)
                    if G > 0:
                        act.wait_ge(ktr_ready, G * KD)
                        act.wait_ge(vg_ready, G)
                    apply_on_act(act, norm_c, G, c_rows(G), lambda i: cn[:, i, :])
                elif phase == PROBS:
                    act.wait_ge(pt_ready, G + 1)
                    act.activation(prob_t[:, :, :], PT[:, :].rearrange("p (s k) -> p s k", s=GS), ACT.Copy).then_inc(pt_copied, 1)
                    if G == 0:
                        act.wait_ge(scaled_ready, 1)
                    for k in range(KD):
                        act.wait_ge(ktr_ready, G * KD + k + 1)
                        act.activation(ck_t[:, G % 2, k, :], CT[k][:, :], ACT.Identity, bias=gains[:, 3, k:k + 1],
                                       scale=gains[:, 2, k:k + 1]).then_inc(ck_ready, 1)
                elif phase == TURN_Q:
                    if G > 0:
                        act.wait_ge(qtr_ready, G * KD)
                    apply_on_act(act, norm_q, G, lambda i: z1[:, i, :], lambda i: z2[:, i, :])
                    for k in range(KD):
                        act.wait_ge(qtr_ready, G * KD + k + 1)
                        act.activation(cq_t[:, k, :], CT[k][:, :], ACT.Identity, bias=scaled[:, 1, k:k + 1],
                                       scale=scaled[:, 0, k:k + 1]).then_inc(cq_ready, 1)
                elif phase == CSCORES:
                    act.wait_ge(cmax_ready, G + 1)
                    exponentials(CS, cprob, cneg_max, ctotal, cexp_ready)
                elif phase == CPROBS:
                    act.wait_ge(cpt_ready, G + 1)
                    act.activation(cprob_t[:, :, :], CPT[:, :].rearrange("p (s k) -> p s k", s=GS), ACT.Copy).then_inc(cpt_copied, 1)
                elif phase == COUT:
                    act.wait_ge(cinv_ready, G + 1)
                    act.wait_ge(co_ready, G + 1)
                    if G > 0:
                        act.wait_ge(og_ready, G * GS)
                    for s in range(GS):
                        act.activation(o[:, s, :], CO[s // 2][:, (s % 2) * D:(s % 2 + 1) * D], ACT.Copy,
                                       scale=cinv[:, s:s + 1]).then_inc(co_scaled, 1)
                elif phase == MULTIPLY:
                    act.wait_ge(ftr_ready, G + 1)
                    act.activation(xq_t[:, :, :], FT[:, :].bitcast(BF16).rearrange("p (i t) -> p i t", t=P),
                                   ACT.Copy).then_inc(ftr_copied, 1)

        @block.vector
        def _(dve):
            def maxima(bank, to, ready):
                dve.tensor_reduce(to[:, :], bank[:, :].rearrange("p (s k) -> p s k", s=GS), AX.X, ALU.max,
                                  negate=True).then_inc(ready, 1)

            count = [0]

            def then(op):
                count[0] += 1
                op.then_inc(w_step, 1)
                dve.wait_ge(w_step, count[0])

            def setup():
                dve.wait_ge(wf_loaded, 16)
                then(dve.tensor_reduce(w_amax[:, :], wf[:, :, :], AX.X, ALU.max, apply_absolute_value=True))
                then(dve.tensor_scalar(w_scale[:, :], w_amax[:, :], 1e-12, 1.0 / INT8_MAX, ALU.max, ALU.mult))
                then(dve.reciprocal(w_inv[:, :], w_scale[:, :]))
                for c in range(KD):
                    then(dve.tensor_scalar(wt1[:, c, :], wf[:, c, :], w_inv[:, c:c + 1], MAGIC, ALU.mult, ALU.add))
                then(dve.tensor_scalar(wt2[:, :, :], wt1[:, :, :], -MAGIC, INT8_MAX, ALU.add, ALU.min))
                then(dve.tensor_scalar(wfq[:, :, :], wt2[:, :, :], -INT8_MAX, None, ALU.max))
                for c in range(KD):
                    then(dve.tensor_scalar(diag[:, c, :], ident[:, :], w_scale[:, c:c + 1], None, ALU.mult))
                dve.wait_ge(p_loaded, 96)
                dve.reciprocal(inv_factor[:, :], factor[:, :]).then_inc(inv_factor_ready, 1)
                dve.wait_ge(inv_factor_ready, 1)
                dve.tensor_scalar(scaled[:, :, :], gains[:, 0:2, :], inv_factor[:, 0:1], None, ALU.mult).then_inc(scaled_ready, 1)

            for step, phase, G in schedule():
                par = G % 2
                if step == SETUP and G == 0:
                    setup()
                if phase == MEASURE:
                    norm_measure(dve, norm_a, G, x_rows(G))
                elif phase == PROJECT:
                    for k in range(KD):
                        dve.wait_ge(xh_ready, G * KD + k + 1)
                        dve.tensor_tensor(xg[LO][:, k, :], TR[k][:, :], xg[HI][:, k, :].bitcast(F32),
                                          ALU.subtract).then_inc(xl_ready, 1)
                elif phase == VALUES:
                    dve.wait_ge(c_loaded[par], 16 * (G // 2) + 16)
                    norm_measure(dve, norm_c, G, c_rows(G))
                elif phase == SCORES:
                    dve.wait_ge(s_ready, G + 1)
                    maxima(S, neg_max, max_ready)
                elif phase == PROBS:
                    dve.wait_ge(exp_ready, G + 1)
                    dve.reciprocal(inv[:, :], total[:, :]).then_inc(inv_ready, 1)
                elif phase == ADD:
                    dve.wait_ge(inv_ready, G + 1)
                    dve.wait_ge(o_ready, G + 1)
                    for s in range(GS):
                        b = G * GS + s
                        dve.scalar_tensor_tensor(out=X[:, b, :], in0=O[s // 2][:, (s % 2) * D:(s % 2 + 1) * D],
                                                 scalar=inv[:, s:s + 1], in1=X[:, b, :], op0=ALU.mult,
                                                 op1=ALU.add).then_inc(added, 1)
                elif phase == MEASURE_X:
                    dve.wait_ge(added, (G + 1) * GS)
                    norm_measure(dve, norm_x, G, x_rows(G))
                elif phase == MEASURE_Q:
                    norm_apply(dve, norm_x, G, x_rows(G), lambda i: z1[:, i, :])
                    dve.wait_ge(norm_x["z_ready"], G * GS + GS)
                    norm_measure(dve, norm_q, G, lambda i: z1[:, i, :])
                elif phase == CSCORES:
                    dve.wait_ge(cs_ready, G + 1)
                    maxima(CS, cneg_max, cmax_ready)
                elif phase == CPROBS:
                    dve.wait_ge(cexp_ready, G + 1)
                    dve.reciprocal(cinv[:, :], ctotal[:, :]).then_inc(cinv_ready, 1)
                elif phase == MEASURE_O:
                    dve.wait_ge(co_scaled, G * GS + GS)
                    norm_measure(dve, norm_o, G, lambda i: o[:, i, :])
                elif phase == CADD:
                    for i in range(GS):
                        dve.scalar_tensor_tensor(out=og[:, i, :], in0=o[:, i, :], scalar=norm_o["mv"][:, i, 0:1], in1=rows[:, 2, :],
                                                 op0=ALU.subtract, op1=ALU.mult).then_inc(og_ready, 1)
                    dve.wait_ge(og_ready, G * GS + GS)
                    dve.wait_ge(norm_o["rstd_ready"], G + 1)
                    dve.wait_ge(xb_ready, G + 1)
                    for i in range(GS):
                        x_row = X[:, G * GS + i, :]
                        dve.scalar_tensor_tensor(out=x_row, in0=og[:, i, :], scalar=norm_o["ve"][:, i:i + 1], in1=x_row,
                                                 op0=ALU.mult, op1=ALU.add).then_inc(x_ready, 1)
                elif phase == MEASURE_F:
                    dve.wait_ge(x_ready, G * GS + GS)
                    norm_measure(dve, norm_f, G, x_rows(G))
                elif phase == SCALE_F:
                    norm_apply(dve, norm_f, G, x_rows(G), lambda i: zf[:, i, :])
                    dve.wait_ge(norm_f["z_ready"], G * GS + GS)
                    base = G * (3 + GS)
                    dve.tensor_reduce(amax[:, par, :], zf[:, :, :], AX.X, ALU.max, apply_absolute_value=True).then_inc(q_step, 1)
                    dve.wait_ge(q_step, base + 1)
                    dve.tensor_scalar(scale[:, par, :], amax[:, par, :], 1e-12, 1.0 / INT8_MAX, ALU.max, ALU.mult).then_inc(q_step, 1)
                    dve.wait_ge(q_step, base + 2)
                    dve.reciprocal(inv_scale[:, par, :], scale[:, par, :]).then_inc(q_step, 1)
                elif phase == QUANTISE:
                    base = G * (3 + GS)
                    dve.wait_ge(q_step, base + 3)
                    for i in range(GS):
                        dve.tensor_scalar(t1[:, i, :], zf[:, i, :], inv_scale[:, par, i:i + 1], MAGIC, ALU.mult, ALU.add).then_inc(q_step, 1)
                    dve.wait_ge(q_step, base + 3 + GS)
                    dve.tensor_scalar(t2[:, :, :], t1[:, :, :], -MAGIC, INT8_MAX, ALU.add, ALU.min).then_inc(rounded, 1)
                    dve.wait_ge(rounded, G + 1)
                    if G > 0:
                        dve.wait_ge(ftr_ready, G)
                    dve.tensor_scalar(zq[:, :, :], t2[:, :, :], -INT8_MAX, None, ALU.max).then_inc(quantised, 1)
                elif phase == STORE:
                    dve.wait_ge(fy_ready, G + 1)
                    if G >= 2:
                        dve.wait_ge(fx_ready, 2 * G - 2)
                    for s in range(GS):
                        dve.scalar_tensor_tensor(out=product_out[:, par, s, :], in0=FY[s // 2][:, (s % 2) * D:(s % 2 + 1) * D],
                                                 scalar=scale[:, par, s:s + 1], in1=col_scale[:, :], op0=ALU.mult,
                                                 op1=ALU.mult).then_inc(fy_scaled, 1)


def clear_semaphores(nc, handles):
    with nc.Block() as block:
        @block.gpsimd
        def _(pool):
            for handle in handles:
                pool.sem_clear(handle)


def decoder(nc, io, out):
    ctx = ExitStack()
    with ctx:
        sb = lambda name, shape, dt=F32: ctx.enter_context(nc.sbuf_tensor(name, shape, dt))
        sem = lambda name: ctx.enter_context(nc.semaphore(name))

        mem = {"psum": [ctx.enter_context(nc.psum_tensor(f"bank{i}", [P, BANK], F32)) for i in range(8)]}
        mem["sems"] = sem
        mem["x"] = sb("x_res", [P, SEQS, D])
        mem["ident"] = sb("ident", [P, P])
        mem["ident_bf"] = sb("ident_bf", [P, P], BF16)
        mem["causal"] = sb("causal", [P, P], BF16)
        mem["neghalf"] = sb("neghalf", [P, SEQS])
        mem["stats"] = sb("stats", [P, SEQS, 6])
        mem["mv"] = sb("mv", [P, SEQS, 2])
        mem["ve"] = sb("ve", [P, SEQS])
        attn_ctx = ExitStack()
        asb = lambda name, shape, dt=F32: attn_ctx.enter_context(nc.sbuf_tensor(name, shape, dt))
        mem["act"] = asb("act", [P, SEQS, D])
        mem["act_t"] = (asb("act_t_hi", [P, KD, SEQS * P], F32R), asb("act_t_lo", [P, KD, SEQS * P], F32R))
        mem["attn_w"] = (asb("attn_w_hi", [P, 4, KD * WIDE], F32R), asb("attn_w_lo", [P, 4, KD * WIDE], F32R))
        mem["attn_g"], mem["attn_b"] = asb("attn_g", [P, D]), asb("attn_b", [P, D])
        for name in ("attn_w_loaded", "attn_w_split", "attn_ln_loaded"):
            mem[name] = sem(name)
        with ExitStack() as ssm_ctx:
            mem["attn_raw"] = ssm_ctx.enter_context(nc.sbuf_tensor("attn_raw", [P, KD * WIDE], F32))
            ssb = lambda name, shape, dt=F32: ssm_ctx.enter_context(nc.sbuf_tensor(name, shape, dt))
            w_in_raw = mem["w_in_raw"] = ssb("w_in_raw", [P, KD, PROJ])
            mem["w_in"] = (ssb("w_in_hi", [P, KD, PROJ], F32R), ssb("w_in_lo", [P, KD, PROJ], F32R))
            w_out = mem["w_out"] = ssb("w_out", [P, KI, D])
            conv_w = mem["conv_w"] = ssb("conv_w", [P, KI, TAPS])
            conv_b = mem["conv_b"] = ssb("conv_b", [P, KI])
            ln_g = mem["ln_g"] = ssb("ln_g", [P, D])
            ln_b = mem["ln_b"] = ssb("ln_b", [P, D])
            decay = mem["decay"] = ssb("decay", [P, P])
            names = mem["ssm_sems"] = {k: sem("s_" + k) for k in (
                "w_in_loaded", "w_in_seen", "w_in_hi", "w_in_split", "w_out_loaded", "conv_loaded", "ln_loaded", "decay_loaded")}

            def load_w_in(sp, layer):
                sp.dma_start(w_in_raw[:, :, :], io["L0_attn_in_proj_w"][bass.ds(layer, 1)].rearrange(
                    "l (k p) n -> p (l k) n", p=P)).then_inc(names["w_in_loaded"], 16)

            def load_w_out(sp, layer):
                sp.dma_start(w_out[:, :, :], io["L0_attn_out_proj_w"][bass.ds(layer, 1)].rearrange(
                    "l (k p) n -> p (l k) n", p=P)).then_inc(names["w_out_loaded"], 16)

            def load_conv(sp, layer):
                sp.dma_start(conv_w[:, :, :], io["conv_w_laid"][bass.ds(layer, 1)].rearrange(
                    "l p c t -> p (l c) t")).then_inc(names["conv_loaded"], 16)
                sp.dma_start(conv_b[:, :], io["conv_b_laid"][bass.ds(layer, 1)].rearrange(
                    "l p c -> p (l c)")).then_inc(names["conv_loaded"], 16)

            def load_ln(sp, layer):
                for tile, name in ((ln_g, "L0_attn_ssm_ln_g"), (ln_b, "L0_attn_ssm_ln_b")):
                    sp.dma_start(tile[:, :], io[name][bass.ds(layer, 1), :].broadcast_to([P, D])).then_inc(
                        names["ln_loaded"], 16)

            def prefetch_ssm(sp):
                load_w_in(sp, 0)
                load_conv(sp, 0)
                sp.dma_start(decay[:, :], io["decay"]).then_inc(names["decay_loaded"], 16)
                load_w_out(sp, 0)
                load_ln(sp, 0)
            mem.update(load_w_in=load_w_in, load_w_out=load_w_out, load_conv=load_conv, load_ln=load_ln,
                       prefetch_ssm=prefetch_ssm)
            stage_load_and_norm(nc, ctx, io, mem)
            stage_ssm(nc, ssm_ctx, io, mem)

        def run(stage, stage_ctx):
            handles = []

            def stage_sem(name):
                handles.append(stage_ctx.enter_context(nc.semaphore(name)))
                return handles[-1]
            mem["sems"] = stage_sem
            stage(nc, stage_ctx, io, mem)
            clear_semaphores(nc, handles)
        with attn_ctx:
            run(stage_self_attention, attn_ctx)
        experts_ctx = ExitStack()
        esb = lambda name, shape, dt=F32: experts_ctx.enter_context(nc.sbuf_tensor(name, shape, dt))
        mem["expert_raw"] = esb("expert_raw", [P, W_PARTS, W_COLS])
        mem["expert_w"] = (esb("expert_w_hi", [P, 2, W_PARTS, W_COLS], F32R), esb("expert_w_lo", [P, 2, W_PARTS, W_COLS], F32R))
        for name in ("expert_loaded", "expert_hi", "expert_split", "e_stats_ready", "e_aggr_ready", "e_var_ready", "e_rstd_ready"):
            mem[name] = sem(name)
        with experts_ctx:
            for stage in (stage_cross_attention, stage_experts):
                with ExitStack() as stage_ctx:
                    run(stage, stage_ctx)
        with ExitStack() as stage_ctx:
            mem["sems"] = lambda name: stage_ctx.enter_context(nc.semaphore(name))
            stage_second_layer(nc, stage_ctx, io, mem, out)


def kernel(**inputs):
    import numpy as np
    import concourse.bacc as bacc
    from concourse.bass_utils import run_bass_kernel_spmd

    nc = bacc.Bacc("TRN2", target_bir_lowering=False, num_devices=1)
    laid = {name: np.ascontiguousarray(a) for name, a in inputs.items()}
    laid["conv_w_laid"] = np.ascontiguousarray(laid.pop("L0_attn_conv_w").reshape(SSM_LAYERS, KI, P, TAPS).transpose(0, 2, 1, 3))
    laid["conv_b_laid"] = np.ascontiguousarray(laid.pop("L0_attn_conv_b").reshape(SSM_LAYERS, KI, P).transpose(0, 2, 1))
    laid["attn_w_laid"] = np.stack([laid.pop(f"L0_attn_{w}").reshape(k, P, -1).transpose(1, 0, 2).reshape(P, -1)
                                    for w, k in (("wq", KD), ("wk", KD), ("wv", KD), ("wo", KW))])
    feature_rows = lambda a: a.reshape(-1, P, a.shape[-1]).transpose(1, 0, 2).reshape(P, -1)
    for name in ("W_q", "W_k", "W_v", "W_o"):
        laid[f"L0_xattn_{name}_laid"] = np.ascontiguousarray(feature_rows(laid.pop("L0_xattn_" + name).T))
    for name in ("b_q", "b_k"):
        laid[f"L0_xattn_{name}_laid"] = np.ascontiguousarray(laid.pop("L0_xattn_" + name).reshape(KD, P).T)
    laid["router_laid"] = np.ascontiguousarray(feature_rows(laid.pop("L0_ffn_router_kernel_DE")))
    laid["experts_laid"] = np.stack([np.concatenate(
        [feature_rows(laid[f"L0_ffn_kernel_{w}"][e]) for w in ("gating_EDF", "up_EDF", "down_EFD")], axis=1)
        for e in range(EXPERTS)])
    for w in ("gating_EDF", "up_EDF", "down_EFD"):
        del laid[f"L0_ffn_kernel_{w}"]
    for name in ("Wq", "Wk", "Wv"):
        laid[f"L1_attn_{name}_laid"] = np.ascontiguousarray(feature_rows(laid.pop("L1_attn_" + name).T))
    laid["qk_gains_laid"] = np.ascontiguousarray(np.stack(
        [laid.pop("L1_xattn_" + name).reshape(KD, P).T for name in ("ln1_w", "ln1_b", "ln2_w", "ln2_b")], axis=1))
    laid["rhs_laid"] = np.ascontiguousarray(laid.pop("L1_ffn_rhs").T.reshape(KD, P, D).transpose(1, 0, 2))
    laid["ctx_t_laid"] = np.ascontiguousarray(laid["ctx_1024"].reshape(SEQS * P, KD, P).transpose(2, 1, 0))
    steps = np.arange(P)[None, :] - np.arange(P)[:, None]
    laid["decay"] = np.where(steps >= 0, np.float64(-0.5) ** np.maximum(steps, 0), 0.0).astype(np.float32)
    io = {name: nc.dram_tensor(f"in_{name}", a.shape, mybir.dt.from_np(a.dtype), kind="ExternalInput").ap()
          for name, a in laid.items()}
    out = nc.dram_tensor("out_x", (SEQS, P, D), F32, kind="ExternalOutput").ap()
    decoder(nc, io, out)
    ran = run_bass_kernel_spmd(nc, [{f"in_{name}": a for name, a in laid.items()}], core_ids=[0])
    return ran.results[0]["out_x"]
```
